# Optimizing a Trainium2 kernel written in Bass

```python
import numpy as np
import jax
import jax.numpy as jnp

def _softmax(x, axis=-1):
    return jax.nn.softmax(x, axis=axis)

def _gelu(x):
    return jax.nn.gelu(x, approximate=True)

def _silu(x):
    return jax.nn.silu(x)

def _sigmoid(x):
    return jax.nn.sigmoid(x)

def _layernorm(x, axis=-1, eps=1e-05):
    m = jnp.mean(x, axis=axis, keepdims=True)
    v = jnp.var(x, axis=axis, keepdims=True)
    return (x - m) / jnp.sqrt(v + eps)

def _scatter_add(tgt, idx, src, axis=0):
    return tgt.at[idx].add(src)

def _segment_sum(src, seg, n):
    return jax.ops.segment_sum(src, seg, n)
kernel_name = 'mk_decoder_postln_d1_seqx_r8_c645d6'

def setup_inputs(seed: int=0):
    np.random.seed(seed)
    _w = jnp.asarray

    def _rec_inputs():
        import jax
        import jax.numpy as jnp
        _rk = jax.random.key(seed)
        x = 7.22e-05 + 1 * jax.random.normal(jax.random.fold_in(_rk, 1), (32, 64, 256), jnp.float32)
        _lenS = 64 - jax.random.randint(jax.random.fold_in(_rk, 7), (32,), 0, max(1, 64 // 4) + 1, jnp.int32)
        _lenS2 = 64 - jax.random.randint(jax.random.fold_in(_rk, 8), (32,), 0, max(1, 64 // 4) + 1, jnp.int32)
        _ctx_512P = jax.random.normal(jax.random.fold_in(_rk, 11), (32, 16, 64), jnp.float32)
        _ctx_512c = jax.random.dirichlet(jax.random.fold_in(_rk, 511), 0.3 * jnp.ones((16,), jnp.float32), (32, 64))
        _ctx_512t = jnp.einsum('bsk,bkd->bsd', _ctx_512c, _ctx_512P)
        _ctx_512t = _ctx_512t * jax.lax.rsqrt(jnp.mean(jnp.square(_ctx_512t)) + 1e-12) * 0.953939
        ctx_512 = -0.000514642 + 1.00011 * (_ctx_512t + 0.3 * jax.random.normal(jax.random.fold_in(_rk, 611), (32, 64, 64), jnp.float32))
        return (x, ctx_512)
    x, ctx_512 = _rec_inputs()

    def _L0_attn_setup():
        import jax, jax.numpy as jnp
        import numpy as np
        HIDDEN = 256
        NUM_HEADS = 16
        HEAD_DIM = HIDDEN // NUM_HEADS
        QB = 127.0
        EPS = 1e-05
        ROPE_BASE = 10000.0

        def _ste(x, xq):
            return x + jax.lax.stop_gradient(xq - x)

        def bitlinear(x, w):
            s = jnp.mean(jnp.abs(w)) + EPS
            wq = jnp.clip(jnp.round(w / s), -1.0, 1.0) * s
            wq = _ste(w, wq)
            g = jnp.max(jnp.abs(x), axis=-1, keepdims=True) + EPS
            xq = jnp.clip(jnp.round(x * (QB / g)), -QB, QB) * (g / QB)
            xq = _ste(x, xq)
            return jnp.einsum('...i,oi->...o', xq, wq)

        def _rotate_half(x):
            x1, x2 = jnp.split(x, 2, axis=-1)
            return jnp.concatenate([-x2, x1], axis=-1)

        def apply_rope(q, k):
            S, D = (q.shape[-2], q.shape[-1])
            inv_freq = 1.0 / ROPE_BASE ** (jnp.arange(0, D, 2, dtype=jnp.float32) / D)
            t = jnp.arange(S, dtype=jnp.float32)
            freqs = jnp.outer(t, inv_freq)
            emb = jnp.concatenate([freqs, freqs], axis=-1)
            cos, sin = (jnp.cos(emb), jnp.sin(emb))
            q = q * cos + _rotate_half(q) * sin
            k = k * cos + _rotate_half(k) * sin
            return (q, k)
        key = jax.random.key(seed)
        k0, k1, k2, k3, k4 = jax.random.split(key, 5)
        B, S = (2, 256)
        hidden_states = jax.random.normal(k0, (B, S, HIDDEN), dtype=jnp.float32)
        init_scale = 0.02
        w_q = jax.random.normal(k1, (HIDDEN, HIDDEN), dtype=jnp.float32) * init_scale
        w_k = jax.random.normal(k2, (HIDDEN, HIDDEN), dtype=jnp.float32) * init_scale
        w_v = jax.random.normal(k3, (HIDDEN, HIDDEN), dtype=jnp.float32) * init_scale
        w_o = jax.random.normal(k4, (HIDDEN, HIDDEN), dtype=jnp.float32) * init_scale
        return {'hidden_states': hidden_states, 'w_q': w_q, 'w_k': w_k, 'w_v': w_v, 'w_o': w_o}
    _L0_attn_all = _L0_attn_setup()
    _L0_attn_in = {k: v for k, v in _L0_attn_all.items() if k in ('w_q', 'w_k', 'w_v', 'w_o')}
    del _L0_attn_all

    def _L0_xattn_setup():
        import jax, jax.numpy as jnp
        import numpy as np
        B, S, E = (2, 256, 256)
        QH, KVH = (32, 8)
        D = E // QH
        G = QH // KVH
        DROPOUT = 1.0
        key = jax.random.key(seed)
        k1, k2, k3 = jax.random.split(key, 3)
        q = jax.random.normal(k1, (B, S, E), dtype=jnp.float32)
        k = jax.random.normal(k2, (B, S, E // G), dtype=jnp.float32)
        v = jax.random.normal(k3, (B, S, E // G), dtype=jnp.float32)
        return {'q': q, 'k': k, 'v': v}
    _L0_xattn_all = _L0_xattn_setup()
    _L0_xattn_in = {k: v for k, v in _L0_xattn_all.items() if k in ()}
    del _L0_xattn_all

    def _L0_ffn_setup():
        import jax, jax.numpy as jnp
        import numpy as np
        TOP_K = 2
        NUM_EXPERTS = 8
        ROUTE_SCALE = 1.0
        key = jax.random.key(seed)
        ks = jax.random.split(key, 8)
        bs, slen, dim, hidden, E = (4, 128, 256, 128, NUM_EXPERTS)
        s = 0.02
        return {'x': jax.random.normal(ks[0], (bs, slen, dim), jnp.float32), 'gate_w': jax.random.normal(ks[1], (E, dim), jnp.float32) * s, 'w1': jax.random.normal(ks[2], (E, hidden, dim), jnp.float32) * s, 'w2': jax.random.normal(ks[3], (E, dim, hidden), jnp.float32) * s, 'w3': jax.random.normal(ks[4], (E, hidden, dim), jnp.float32) * s, 'ws1': jax.random.normal(ks[5], (hidden, dim), jnp.float32) * s, 'ws2': jax.random.normal(ks[6], (dim, hidden), jnp.float32) * s, 'ws3': jax.random.normal(ks[7], (hidden, dim), jnp.float32) * s}
    _L0_ffn_all = _L0_ffn_setup()
    _L0_ffn_in = {k: v for k, v in _L0_ffn_all.items() if k in ('gate_w', 'w1', 'w2', 'w3', 'ws1', 'ws2', 'ws3')}
    del _L0_ffn_all
    return {'x': x, 'ctx_512': ctx_512, 'L0_attn_w_q': _L0_attn_in['w_q'], 'L0_attn_w_k': _L0_attn_in['w_k'], 'L0_attn_w_v': _L0_attn_in['w_v'], 'L0_attn_w_o': _L0_attn_in['w_o'], 'L0_ffn_gate_w': _L0_ffn_in['gate_w'], 'L0_ffn_w1': _L0_ffn_in['w1'], 'L0_ffn_w2': _L0_ffn_in['w2'], 'L0_ffn_w3': _L0_ffn_in['w3'], 'L0_ffn_ws1': _L0_ffn_in['ws1'], 'L0_ffn_ws2': _L0_ffn_in['ws2'], 'L0_ffn_ws3': _L0_ffn_in['ws3']}

def reference(x, ctx_512, L0_attn_w_q, L0_attn_w_k, L0_attn_w_v, L0_attn_w_o, L0_ffn_gate_w, L0_ffn_w1, L0_ffn_w2, L0_ffn_w3, L0_ffn_ws1, L0_ffn_ws2, L0_ffn_ws3):
    import jax
    import jax.numpy as jnp

    def _L0_attn_ref(hidden_states, w_q, w_k, w_v, w_o):
        import jax, jax.numpy as jnp
        import numpy as np
        HIDDEN = 256
        NUM_HEADS = 16
        HEAD_DIM = HIDDEN // NUM_HEADS
        QB = 127.0
        EPS = 1e-05
        ROPE_BASE = 10000.0

        def _ste(x, xq):
            return x + jax.lax.stop_gradient(xq - x)

        def bitlinear(x, w):
            s = jnp.mean(jnp.abs(w)) + EPS
            wq = jnp.clip(jnp.round(w / s), -1.0, 1.0) * s
            wq = _ste(w, wq)
            g = jnp.max(jnp.abs(x), axis=-1, keepdims=True) + EPS
            xq = jnp.clip(jnp.round(x * (QB / g)), -QB, QB) * (g / QB)
            xq = _ste(x, xq)
            return jnp.einsum('...i,oi->...o', xq, wq)

        def _rotate_half(x):
            x1, x2 = jnp.split(x, 2, axis=-1)
            return jnp.concatenate([-x2, x1], axis=-1)

        def apply_rope(q, k):
            S, D = (q.shape[-2], q.shape[-1])
            inv_freq = 1.0 / ROPE_BASE ** (jnp.arange(0, D, 2, dtype=jnp.float32) / D)
            t = jnp.arange(S, dtype=jnp.float32)
            freqs = jnp.outer(t, inv_freq)
            emb = jnp.concatenate([freqs, freqs], axis=-1)
            cos, sin = (jnp.cos(emb), jnp.sin(emb))
            q = q * cos + _rotate_half(q) * sin
            k = k * cos + _rotate_half(k) * sin
            return (q, k)
        B, S, H = hidden_states.shape
        scale = 1.0 / np.sqrt(HEAD_DIM)

        def split_heads(x):
            return x.reshape(B, S, NUM_HEADS, HEAD_DIM).transpose(0, 2, 1, 3)
        q = split_heads(bitlinear(hidden_states, w_q))
        k = split_heads(bitlinear(hidden_states, w_k))
        v = split_heads(bitlinear(hidden_states, w_v))
        q, k = apply_rope(q, k)
        attn_scores = jnp.einsum('bhqd,bhkd->bhqk', q, k) * scale
        attn_weights = jax.nn.softmax(attn_scores, axis=-1)
        ctx = jnp.einsum('bhqk,bhkd->bhqd', attn_weights, v)
        ctx = ctx.transpose(0, 2, 1, 3).reshape(B, S, H)
        return bitlinear(ctx, w_o)

    def _L0_xattn_ref(q, k, v):
        import jax, jax.numpy as jnp
        import numpy as np
        B, S, E = (2, 256, 256)
        QH, KVH = (32, 8)
        D = E // QH
        G = QH // KVH
        DROPOUT = 1.0
        b, s, _ = q.shape
        qh = q.reshape(b, s, KVH, G, D).transpose(0, 2, 3, 1, 4)
        kh = k.reshape(b, s, KVH, D).transpose(0, 2, 1, 3)
        vh = v.reshape(b, s, KVH, D).transpose(0, 2, 1, 3)
        scale = 1.0 / jnp.sqrt(jnp.float32(D))
        scores = jnp.einsum('bkgsd,bktd->bkgst', qh, kh) * scale
        attn = jax.nn.softmax(scores, axis=-1) / DROPOUT
        out = jnp.einsum('bkgst,bktd->bkgsd', attn, vh)
        return out.transpose(0, 3, 1, 2, 4).reshape(b, s, E)

    def _L0_ffn_ref(x, gate_w, w1, w2, w3, ws1, ws2, ws3):
        import jax, jax.numpy as jnp
        import numpy as np
        TOP_K = 2
        NUM_EXPERTS = 8
        ROUTE_SCALE = 1.0
        bs, slen, dim = x.shape
        xf = x.reshape(-1, dim)
        logits = (xf @ gate_w.T).astype(jnp.float32)
        scores = jax.nn.sigmoid(logits)
        top_scores, sel_idx = jax.lax.top_k(scores, TOP_K)
        top_scores = top_scores * ROUTE_SCALE
        routed = jnp.zeros_like(xf)
        for k in range(TOP_K):
            xs = xf * top_scores[:, k][:, None]
            h1 = jnp.einsum('td,ehd->teh', xs, w1)
            h3 = jnp.einsum('td,ehd->teh', xs, w3)
            h = jax.nn.silu(h1) * h3
            onehot = jax.nn.one_hot(sel_idx[:, k], NUM_EXPERTS, dtype=h.dtype)
            routed = routed + jnp.einsum('teh,te,edh->td', h, onehot, w2)
        shared = jax.nn.silu(xf @ ws1.T) * (xf @ ws3.T) @ ws2.T
        out = (shared + routed).reshape(bs, slen, dim)
        return out
    x = _layernorm(x + _L0_attn_ref(x, L0_attn_w_q, L0_attn_w_k, L0_attn_w_v, L0_attn_w_o), axis=-1)
    x = _layernorm(x + _L0_xattn_ref(x, ctx_512, ctx_512), axis=-1)
    x = _layernorm(x + _L0_ffn_ref(x, L0_ffn_gate_w, L0_ffn_w1, L0_ffn_w2, L0_ffn_w3, L0_ffn_ws1, L0_ffn_ws2, L0_ffn_ws3), axis=-1)
    return x

_drawn_inputs = setup_inputs


def setup_inputs(seed=0):
    import zlib

    import numpy as np

    out = dict(_drawn_inputs(seed))
    spreads = {}
    factors = {'L0_attn_w_q': 8.0,
     'L0_attn_w_k': 8.0,
     'L0_attn_w_v': 8.0,
     'L0_attn_w_o': 8.0,
     'L0_ffn_gate_w': 8.0,
     'L0_ffn_w1': 8.0,
     'L0_ffn_w2': 8.0,
     'L0_ffn_w3': 8.0,
     'L0_ffn_ws1': 4.839,
     'L0_ffn_ws2': 4.749,
     'L0_ffn_ws3': 4.768}
    for name, (base, spread) in spreads.items():
        noise = np.random.default_rng([zlib.crc32(name.encode()), seed]).standard_normal(out[name].shape)
        drawn = base * np.exp(spread * noise) if base else spread * noise
        out[name] = jnp.asarray(drawn.astype(out[name].dtype))
    for name, factor in factors.items():
        out[name] = (out[name] * factor).astype(out[name].dtype)
    return out
```

```python
from contextlib import ExitStack

import concourse.bass as bass
import numpy as np
from concourse import mybir

F32 = mybir.dt.float32
F32R = mybir.dt.float32r
F16 = mybir.dt.float16
BF16 = mybir.dt.bfloat16
ALU = mybir.AluOpType
ACT = mybir.ActivationFunctionType
AX = mybir.AxisListType
RMAX = bass.bass_isa.ReduceOp.max
RADD = bass.bass_isa.ReduceOp.add

P = 128
SEQ = 64
HID = 256
KC = HID // P
NE = 8
NB = 5
SH = 16
SD = HID // SH
SP_ = SH // 2
XP = 16
XD = 8
EPS = 1e-5
QB = 127.0
MAGIC = 12582912.0
TINY = 1e-30

C_IDENT = 0
C_SELA = C_IDENT + P
C_SELB = C_SELA + SP_ * P
C_DUP = C_SELB + XP * P
C_COS = C_DUP + 2 * P
C_SIN = C_COS + SD
C_MASKA = C_SIN + SD
C_MASKB = C_MASKA + 2
C_RANK = C_MASKB + 4
C_END = C_RANK + NE


def constants():
    c = np.zeros((P, C_END), np.float32)
    c[:, C_IDENT:C_IDENT + P] = np.eye(P)
    col = np.arange(P)
    for pair in range(SP_):
        for part in range(2):
            c[part * SH + 2 * pair + col // SEQ, C_SELA + pair * P + col] = -1.0
    for pair in range(XP):
        for part in range(2):
            c[part * 2 * XP + 2 * pair + col // SEQ, C_SELB + pair * P + col] = -1.0
    for b in range(2):
        c[b * SEQ + col % SEQ, C_DUP + b * P + col] = 1.0
    inv_freq = (1.0 / np.float32(10000.0) ** (np.arange(0, SD, 2, dtype=np.float32) / np.float32(SD))).astype(np.float32)
    angle = np.outer(np.arange(P) % SEQ, inv_freq).astype(np.float32)
    c[:, C_COS:C_COS + SD] = np.cos(np.concatenate([angle, angle], 1))
    c[:, C_SIN:C_SIN + SD] = np.concatenate([-np.sin(angle), np.sin(angle)], 1)
    for h in range(2):
        c[:, C_MASKA + h] = (col % 32) // SD == h
    for h in range(4):
        c[:, C_MASKB + h] = (col % 32) // XD == h
    c[:, C_RANK:C_END] = NE - np.arange(NE)
    return c


class Tile:

    def __init__(self, base, shift=0):
        self.base, self.shift = base, shift
        self.later = not isinstance(base, int) or base > 0


def decoder_layer(nc, x, x_perm, ctx_in, wq, wk, wv, wo, gate, w1, w2, w3, ws1, ws2, ws3, const, out):
    ntiles = x.shape[0]
    with ExitStack() as stack:
        def sb(name, shape, dt=F32):
            return stack.enter_context(nc.sbuf_tensor(name, shape, dt))

        def bank(name):
            return stack.enter_context(nc.psum_tensor(name, [P, 512], F32))

        def sem(name):
            return stack.enter_context(nc.semaphore(name))

        rises = {}

        def sig(name, per=1):
            handle = sem(name)
            rises[name] = per
            return handle

        def at(t, handle, n):
            per = rises[handle.name]
            return t.base * per + (t.shift * per + n)

        cst = sb("cst", [P, C_END])
        ident = cst[:, C_IDENT:C_IDENT + P]
        ident16 = sb("ident16", [P, P], F16)
        identb = sb("identb", [P, P], BF16)
        selA = sb("selA", [P, SP_ * P], BF16)
        selB = sb("selB", [P, XP * P], BF16)
        dup = cst[:, C_DUP:C_DUP + 2 * P]
        cos = cst[:, C_COS:C_COS + SD]
        sin = cst[:, C_SIN:C_SIN + SD]
        watt = sb("watt", [P, 4, KC, HID])
        wabs = sb("wabs", [P, 4])
        wsum = sb("wsum", [P, 4])
        wscale = sb("wscale", [P, 4])
        winv = sb("winv", [P, 4])
        wround = sb("wround", [P, KC * HID])
        wqk = sb("wqk", [P, KC, 2 * HID], BF16)
        wqk_rot = sb("wqk_rot", [P, KC, 2 * HID], BF16)
        wv_t = sb("wv_t", [P, KC, HID], BF16)
        wo_t = sb("wo_t", [P, KC, HID], BF16)
        score_c = sb("score_c", [P, 1])
        v_c = sb("v_c", [P, 1])
        o_c = sb("o_c", [P, 1])
        COLS = (2 * NE + 2) * P
        w13 = sb("w13", [P, KC, COLS])
        w13h = sb("w13h", [P, KC, COLS], F32R)
        w13l = sb("w13l", [P, KC, COLS], F32R)
        w2f = sb("w2f", [P, NE + 1, HID])
        w2h = sb("w2h", [P, NE + 1, HID], F32R)
        w2l = sb("w2l", [P, NE + 1, HID], F32R)
        gt = sb("gt", [P, KC, NE])
        gth = sb("gth", [P, KC, NE], F32R)
        gtl = sb("gtl", [P, KC, NE], F32R)
        neghalf = sb("neghalf", [P, 1])
        xin = sb("xin", [P, HID])
        xres = sb("xres", [P, HID])
        ga = sb("ga", [P, 12])
        gall = sb("gall", [P, 1])
        rnd = sb("rnd", [P, HID])
        xq = sb("xq", [P, HID], BF16)
        xqT = sb("xqT", [P, KC, P], BF16)
        rope_c = sb("rope_c", [P, 2 * HID])
        rope_s = sb("rope_s", [P, 2 * HID])
        rope = sb("rope", [P, 2 * HID])
        qk_parts = sb("qk_parts", [P, 2 * SP_, 4, 32], F16)
        gvd = sb("gvd", [P, 2])
        vA = sb("vA", [P, 2, SP_, 2, SD + 1])
        qs = sb("qs", [P, SP_, P], F16)
        ks = sb("ks", [P, SP_, 2, 2, SEQ], F16)
        mA = sb("mA", [P, SH])
        mpA = sb("mpA", [P, P], BF16)
        mTA = sb("mTA", [P, P], BF16)
        probsA = sb("probsA", [P, SP_, P])
        rsA = sb("rsA", [P, SH])
        att = sb("att", [P, HID])
        rnd2 = sb("rnd2", [P, HID])
        xq2 = sb("xq2", [P, HID], BF16)
        xq2T = sb("xq2T", [P, KC, P], BF16)
        resA = sb("resA", [P, HID])
        stA = sb("stA", [P, 12])
        x1 = sb("x1", [P, HID])
        ctxt = sb("ctxt", [P, SEQ])
        ctxd = sb("ctxd", [P, 2, SEQ])
        gb = sb("gb", [P, 8])
        call = sb("call", [P, 1])
        cnorm = sb("cnorm", [P, SEQ])
        c_parts = sb("c_parts", [P, 2, 4, 32], F16)
        x_parts = sb("x_parts", [P, 8, 4, 32], F16)
        vB = sb("vB", [P, 2, 4, 2, XD + 1])
        xs = sb("xs", [P, 8, P], F16)
        cs = sb("cs", [P, 2, 2, 4, SEQ], F16)
        mB = sb("mB", [P, 2 * XP])
        mpB = sb("mpB", [P, P], BF16)
        mTB = sb("mTB", [P, P], BF16)
        probsB = sb("probsB", [P, XP, P])
        rsB = sb("rsB", [P, 2 * XP])
        attB = sb("attB", [P, HID])
        resB = sb("resB", [P, HID])
        stB = sb("stB", [P, 12])
        x2 = sb("x2", [P, HID])
        xTh = sb("xTh", [P, KC, P], F32R)
        xTl = sb("xTl", [P, KC, P], F32R)
        tanh_g = sb("tanh_g", [P, NE])
        rt = sb("rt", [P, 8, NE])
        sc9 = sb("sc9", [P, 2 * NB])
        zA = sb("zA", [P, 2, 2 * P])
        zB = sb("zB", [P, 2, 2 * P])
        th = sb("th", [P, 2, 2 * P])
        hg = sb("hg", [P, 2, 2 * P])
        hh = sb("hh", [P, 2, 2 * P])
        hTh = sb("hTh", [P, 2, 2 * P], F32R)
        hTl = sb("hTl", [P, 2, 2 * P], F32R)
        resC = sb("resC", [P, HID])
        stC = sb("stC", [P, 12])
        y = sb("y", [P, HID])
        PA = [bank("PA0"), bank("PA1")]
        PB = [bank("PB0"), bank("PB1")]
        UP = [bank("UP0"), bank("UP1")]
        TR = bank("TR")
        ACC = bank("ACC")

        ld_att, ld_ffn, ld_cst = sem("ld_att"), sem("ld_ffn"), sem("ld_cst")
        set_up = sem("set_up")
        cst16 = sem("cst16")
        wabs_ready, wsum_ready, wchain = sem("wabs_ready"), sem("wsum_ready"), sem("wchain")
        watt_ready, ffn_hi, ffn_lo = sem("watt_ready"), sem("ffn_hi"), sem("ffn_lo")
        xin_ld, xres_ld = sig("xin_ld", 16), sig("xres_ld", 16)
        quant, g_ready, gall_ready, xq_ready = sig("quant", 4), sig("g_ready"), sig("gall_ready"), sig("xq_ready")
        xqT_ps, xqT_ready = sig("xqT_ps"), sig("xqT_ready")
        scales = sig("scales", 2)
        qk_ps, rope_ready, rope_sum = sig("qk_ps", 2), sig("rope_ready", 2), sig("rope_sum")
        qk_hi, qk_lo = sig("qk_hi"), sig("qk_lo")
        v_ps, gvd_ready, v_even, v_odd = sig("v_ps"), sig("gvd_ready"), sig("v_even"), sig("v_odd")
        qs_ps, ks_ps, qs_ready = sig("qs_ps"), sig("ks_ps"), sig("qs_ready")
        ks_even, ks_odd = sig("ks_even"), sig("ks_odd")
        sA_ps, mA_done, mhA_ready, mpA_ready = sig("sA_ps", 2), sig("mA_done", 2), sig("mhA_ready"), sig("mpA_ready")
        mTA_ps, mTA_ready = sig("mTA_ps"), sig("mTA_ready")
        eA_ps, probsA_ready, oA_ps = sig("eA_ps", 2), sig("probsA_ready", 2), sig("oA_ps")
        rsA_ready, att_ready, quant2 = sig("rsA_ready"), sig("att_ready"), sig("quant2", 5)
        xq2_ready, xq2T_ps, xq2T_ready, wo_ps = sig("xq2_ready"), sig("xq2T_ps"), sig("xq2T_ready"), sig("wo_ps")
        resA_ready, bnA, varA_ready = sig("resA_ready"), sig("bnA"), sig("varA_ready")
        epsA, rstdA_ready, x1_ready = sig("epsA"), sig("rstdA_ready"), sig("x1_ready")
        ctxt_ld, ctxd_ld = sig("ctxt_ld", 16), sig("ctxd_ld", 32)
        cmax_ready, call_ready, cscale, c_ready = sig("cmax_ready"), sig("call_ready"), sig("cscale", 4), sig("c_ready")
        vB_ready, x1_hi, x1_lo = sig("vB_ready"), sig("x1_hi"), sig("x1_lo")
        xs_ps, cs_ps, xs_ready, cs_ready = sig("xs_ps"), sig("cs_ps"), sig("xs_ready"), sig("cs_ready")
        sB_ps, mB_done, mhB_ready, mpB_ready = sig("sB_ps", 4), sig("mB_done", 4), sig("mhB_ready"), sig("mpB_ready")
        mTB_ps, mTB_ready = sig("mTB_ps"), sig("mTB_ready")
        eB_ps, probsB_ready, oB_ps = sig("eB_ps", 4), sig("probsB_ready", 4), sig("oB_ps")
        rsB_ready, attB_ready, resB_ready = sig("rsB_ready"), sig("attB_ready"), sig("resB_ready")
        bnB, varB_ready, epsB, rstdB_ready, x2_ready = (sig("bnB"), sig("varB_ready"), sig("epsB"), sig("rstdB_ready"),
                                                        sig("x2_ready"))
        xT_ps, xTh_ready, xTl_ready = sig("xT_ps"), sig("xTh_ready"), sig("xTl_ready")
        gate_ps, gate_th, route, s_ready = sig("gate_ps"), sig("gate_th"), sig("route", 9), sig("s_ready")
        up_ps, zA_ready, th_ready, zB_ready = sig("up_ps", NB), sig("zA_ready", NB), sig("th_ready", NB), sig("zB_ready", NB)
        hg_ready, h_ready, hT_ps = sig("hg_ready", NB), sig("h_ready", NB), sig("hT_ps", NB)
        hTh_ready, hTl_ready, down_ps = sig("hTh_ready", NB), sig("hTl_ready", NB), sig("down_ps", NB)
        resC_ready, bnC, varC_ready = sig("resC_ready"), sig("bnC"), sig("varC_ready")
        epsC, rstdC_ready, y_ready, y_out = sig("epsC"), sig("rstdC_ready"), sig("y_ready"), sig("y_out", 16)

        held = {}

        def settle(eng):
            if eng not in held:
                held[eng] = sem(f"held{len(held)}")
            eng.sem_inc(held[eng], 1)

        def chain(eng, t, handle):
            count = [0]

            def link(ins):
                count[0] += 1
                ins.then_inc(handle, 1)
                eng.wait_ge(handle, at(t, handle, count[0]))
            return link

        def twice(ap, n):
            return ap.rearrange("p (n o d) -> p n o d", n=n, o=1).broadcast_to([P, n, 2, 32])

        def each(ap, n, d):
            return ap.rearrange("p (n o) -> p n o", o=1).broadcast_to([P, n, d])

        def heads(ap, d):
            return ap.rearrange("p (h d) -> p h d", d=d)

        LEFT_HI, LEFT_LO = slice(0, 3, 2), slice(1, 4, 2)
        RIGHT_HI, RIGHT_LO = slice(0, 4, 3), slice(1, 3)

        def width(n):
            return P if n == 0 else 2 * P

        def run(eng, turn):
            turn(Tile(0), None, None)
            turn(Tile(1), Tile(0), None)
            turn(Tile(2), Tile(1), Tile(0))
            with eng.Fori(3, ntiles) as i:
                turn(Tile(i), Tile(i, -1), Tile(i, -2))
            turn(None, Tile(ntiles - 1), Tile(ntiles - 2))
            turn(None, None, Tile(ntiles - 1))

        def rows(dram, t):
            if isinstance(t.base, int):
                n = t.base + t.shift
                return dram[n:n + 1].rearrange("a p c -> (a p) c")
            return dram[bass.ds(t.base + t.shift, 1)].rearrange("a p c -> (a p) c")

        block = stack.enter_context(nc.Block())

        @block.sync
        def _(sp):
            sp.dma_start(cst[:], const).then_inc(ld_cst, 16)
            for n, w in enumerate((wq, wk, wv, wo)):
                sp.dma_start(watt[:, n], w).then_inc(ld_att, 16)

            def load_x(t):
                if t.later:
                    sp.wait_ge(xq_ready, at(t, xq_ready, 0))
                sp.dma_start(xin[:], rows(x, t)).then_inc(xin_ld, 16)

            def load_residual(t):
                if t.later:
                    sp.wait_ge(resA_ready, at(t, resA_ready, 0))
                sp.dma_start(xres[:], rows(x_perm, t)).then_inc(xres_ld, 16)

            def load_context(t):
                if t.later:
                    sp.wait_ge(c_ready, at(t, c_ready, 0))
                sp.dma_start(ctxt[:], rows(ctx_in, t)).then_inc(ctxt_ld, 16)

            def load_context_v(t):
                if t.later:
                    sp.wait_ge(vB_ready, at(t, vB_ready, 0))
                for half in range(2):
                    sp.dma_start(ctxd[half * SEQ:(half + 1) * SEQ],
                                 rows(ctx_in, t).rearrange("(b k) d -> k b d", b=2)).then_inc(ctxd_ld, 16)

            def store(t):
                sp.wait_ge(y_ready, at(t, y_ready, 1))
                sp.dma_start(rows(out, t), y[:]).then_inc(y_out, 16)

            load_x(Tile(0))
            load_residual(Tile(0))
            load_context(Tile(0))
            load_context_v(Tile(0))
            for kc in range(KC):
                view = w13[:, kc, 0:NE * 2 * P].rearrange("p (b m n) -> p b m n", b=NE // 2, m=2)
                for m, w in enumerate((w1, w3)):
                    sp.dma_start(view[:, :, m], w[kc].rearrange("p (b n) -> p b n", b=NE // 2)).then_inc(ld_ffn, 16)
                for m, w in enumerate((ws1, ws3)):
                    first = (2 * NE + m) * P
                    sp.dma_start(w13[:, kc, first:first + P], w[kc]).then_inc(ld_ffn, 16)
            sp.dma_start(gt[:], gate).then_inc(ld_ffn, 16)
            sp.dma_start(w2f[:, 0:NE], w2).then_inc(ld_ffn, 16)
            sp.dma_start(w2f[:, NE], ws2).then_inc(ld_ffn, 16)
            load_x(Tile(1))
            load_context(Tile(1))
            load_residual(Tile(1))
            load_x(Tile(2))
            load_context(Tile(2))
            load_context_v(Tile(1))
            load_residual(Tile(2))
            with sp.Fori(3, ntiles) as i:
                load_x(Tile(i))
                load_context(Tile(i))
                load_context_v(Tile(i, -1))
                store(Tile(i, -3))
                load_residual(Tile(i))
            load_context_v(Tile(ntiles - 1))
            for n in (3, 2, 1):
                store(Tile(ntiles - n))
            sp.wait_ge(y_out, 16 * ntiles)

        FFN_LOADS = 16 * (4 * KC + 3)

        @block.vector
        def _(dve):
            V = nc.vector
            V.memset(neghalf[:], -0.5)
            V.memset(mpA[:], 0.0)
            V.memset(mpB[:], 0.0)
            V.memset(vA[:], 0.0)
            V.memset(sc9[:], 1.0)
            V.memset(vB[:], 0.0).then_inc(set_up, 1)
            dve.wait_ge(set_up, 1)
            V.memset(vA[0:SEQ, :, :, 0, SD:SD + 1], 1.0)
            V.memset(vA[SEQ:P, :, :, 1, SD:SD + 1], 1.0)
            V.memset(vB[0:SEQ, :, :, 0, XD:XD + 1], 1.0)
            V.memset(vB[SEQ:P, :, :, 1, XD:XD + 1], 1.0).then_inc(set_up, 1)
            dve.wait_ge(ld_att, 64)
            V.tensor_reduce(wabs[:], watt[:].rearrange("p w k n -> p w (k n)"), axis=AX.X, op=ALU.add,
                            apply_absolute_value=True).then_inc(wabs_ready, 1)
            dve.wait_ge(wsum_ready, 1)
            links = 0

            def wlink(ins):
                nonlocal links
                links += 1
                ins.then_inc(wchain, 1)
                dve.wait_ge(wchain, links)

            wlink(V.tensor_scalar(wscale[:], wsum[:], 1.0 / (HID * HID), EPS, ALU.mult, ALU.add))
            wlink(V.reciprocal(winv[:], wscale[:]))
            dest = (wqk[:, :, 0:HID], wqk[:, :, HID:2 * HID], wv_t[:], wo_t[:])
            for k in range(4):
                wlink(V.tensor_scalar(wround[:], watt[:, k].rearrange("p k n -> p (k n)"), winv[:, k:k + 1], MAGIC,
                                      ALU.mult, ALU.add))
                wlink(V.tensor_scalar(wround[:], wround[:], MAGIC, 1.0, ALU.subtract, ALU.min))
                wlink(V.tensor_scalar(dest[k], wround[:].rearrange("p (k n) -> p k n", k=KC), -1.0, None, ALU.max))
            src = wqk[:].rearrange("p k (h two d) -> p (k h) two d", two=2, d=SD // 2)
            rot = wqk_rot[:].rearrange("p k (h two d) -> p (k h) two d", two=2, d=SD // 2)
            V.tensor_copy(rot[:, :, 0], src[:, :, 1])
            V.tensor_copy(rot[:, :, 1], src[:, :, 0])
            wlink(V.tensor_tensor(score_c[:], wscale[:, 0:1], wscale[:, 1:2], ALU.mult))
            wlink(V.tensor_scalar(score_c[:], score_c[:], 1.0 / (QB * QB * SD ** 0.5), None, ALU.mult))
            wlink(V.tensor_scalar(v_c[:], wscale[:, 2:3], 1.0 / QB, None, ALU.mult))
            V.tensor_scalar(o_c[:], wscale[:, 3:4], 1.0 / QB, None, ALU.mult).then_inc(watt_ready, 1)

            def statistics(t, st, res, res_ready, bn, var_ready):
                dve.wait_ge(res_ready, at(t, res_ready, 1))
                V.bn_stats(st[:, 0:6], res[:]).then_inc(bn, 1)
                dve.wait_ge(bn, at(t, bn, 1))
                settle(dve)
                V.bn_aggr(st[:, 6:8], st[:, 0:6]).then_inc(var_ready, 1)

            def quantise(t):
                link = chain(dve, t, quant)
                dve.wait_ge(xin_ld, at(t, xin_ld, 16))
                link(V.tensor_reduce(ga[:, 0:1], xin[:], axis=AX.X, op=ALU.max, apply_absolute_value=True))
                if t.later:
                    dve.wait_ge(gall_ready, at(t, gall_ready, 0))
                V.tensor_scalar(ga[:, 1:2], ga[:, 0:1], EPS, None, ALU.add).then_inc(g_ready, 1)
                dve.wait_ge(g_ready, at(t, g_ready, 1))
                link(V.reciprocal(ga[:, 2:3], ga[:, 1:2]))
                link(V.tensor_scalar(ga[:, 2:3], ga[:, 2:3], QB, None, ALU.mult))
                link(V.tensor_scalar(rnd[:], xin[:], ga[:, 2:3], MAGIC, ALU.mult, ALU.add))
                if t.later:
                    dve.wait_ge(xqT_ps, at(t, xqT_ps, 0))
                V.tensor_scalar(xq[:], rnd[:], MAGIC, None, ALU.subtract).then_inc(xq_ready, 1)

            def token_scales(t):
                link = chain(dve, t, scales)
                dve.wait_ge(gall_ready, at(t, gall_ready, 1))
                if t.later:
                    dve.wait_ge(probsA_ready, at(t, probsA_ready, 0))
                    dve.wait_ge(v_ps, at(t, v_ps, 0))
                V.tensor_scalar(ga[:, 5:6], gall[:], gall[:, 0:1], score_c[:, 0:1], ALU.mult, ALU.mult)
                link(V.reciprocal(ga[:, 3:4], gall[:]))
                V.tensor_scalar(ga[:, 6:7], ga[:, 1:2], v_c[:, 0:1], None, ALU.mult)
                link(V.tensor_tensor(ga[:, 4:5], ga[:, 1:2], ga[:, 3:4], ALU.mult))

            def rope_parts(t):
                if t.later:
                    dve.wait_ge(rope_sum, at(t, rope_sum, 0))
                for k, (dst, table) in enumerate(((rope_c, cos), (rope_s, sin))):
                    dve.wait_ge(qk_ps, at(t, qk_ps, k + 1))
                    V.scalar_tensor_tensor(out=heads(dst[:], SD), in0=heads(PA[k][:], SD), scalar=ga[:, 4:5],
                                           in1=table.rearrange("p (o d) -> p o d", o=1).broadcast_to([P, 2 * SH, SD]),
                                           op0=ALU.mult, op1=ALU.mult).then_inc(rope_ready, 1)

            def v_heads(t):
                dve.wait_ge(v_ps, at(t, v_ps, 1))
                if t.later:
                    dve.wait_ge(v_odd, at(t, v_odd, 0))
                V.tensor_copy(gvd[:], PA[1][:, 0:2]).then_inc(gvd_ready, 1)
                dve.wait_ge(gvd_ready, at(t, gvd_ready, 1))
                if t.later:
                    dve.wait_ge(oA_ps, at(t, oA_ps, 0))
                for b in range(2):
                    last = V.tensor_scalar(vA[0:SEQ, b, :, 0, 0:SD], heads(PA[0][0:SEQ, b * P:(b + 1) * P], SD),
                                           gvd[0:SEQ, b:b + 1], None, ALU.mult)
                last.then_inc(v_even, 1)

            def mask_k(t):
                dve.wait_ge(ks_ps, at(t, ks_ps, 1))
                if t.later:
                    dve.wait_ge(eA_ps, at(t, eA_ps, 0))
                V.tensor_scalar(ks[:, :, :, 0].rearrange("p h b t -> p (h b) t"), heads(PA[1][:].bitcast(F16), SEQ),
                                cst[:, C_MASKA:C_MASKA + 1], None, ALU.mult).then_inc(ks_even, 1)

            def maxima_a(t):
                for k in range(2):
                    dve.wait_ge(sA_ps, at(t, sA_ps, k + 1))
                    V.tensor_reduce(mA[:, k * 8:k * 8 + 8], heads(PA[k][:], SEQ), axis=AX.X,
                                    op=ALU.max).then_inc(mA_done, 1)
                dve.wait_ge(mA_done, at(t, mA_done, 2))
                if t.later:
                    dve.wait_ge(mTA_ps, at(t, mTA_ps, 0))
                V.tensor_copy(mpA[:, 0:SH], mA[:]).then_inc(mhA_ready, 1)
                dve.wait_ge(mhA_ready, at(t, mhA_ready, 1))
                V.tensor_tensor(mpA[:, SH:2 * SH], mA[:], mpA[:, 0:SH], ALU.subtract).then_inc(mpA_ready, 1)

            def normalise_a(t):
                dve.wait_ge(oA_ps, at(t, oA_ps, 1))
                o = heads(PA[0][:, 0:SH * (SD + 1)], SD + 1)
                V.reciprocal(rsA[:].rearrange("p (h o) -> p h o", o=1), o[:, :, SD:SD + 1]).then_inc(rsA_ready, 1)
                dve.wait_ge(rsA_ready, at(t, rsA_ready, 1))
                V.tensor_tensor(heads(att[:], SD), o[:, :, 0:SD], each(rsA[:], SH, SD), ALU.mult).then_inc(att_ready, 1)
                dve.wait_ge(att_ready, at(t, att_ready, 1))
                link = chain(dve, t, quant2)
                link(V.tensor_reduce(ga[:, 8:9], att[:], axis=AX.X, op=ALU.max, apply_absolute_value=True))
                link(V.tensor_scalar(ga[:, 8:9], ga[:, 8:9], EPS, None, ALU.add))
                link(V.reciprocal(ga[:, 9:10], ga[:, 8:9]))
                V.tensor_scalar(ga[:, 10:11], ga[:, 8:9], o_c[:, 0:1], None, ALU.mult)
                link(V.tensor_scalar(ga[:, 9:10], ga[:, 9:10], QB, None, ALU.mult))
                link(V.tensor_scalar(rnd2[:], att[:], ga[:, 9:10], MAGIC, ALU.mult, ALU.add))
                V.tensor_scalar(xq2[:], rnd2[:], MAGIC, None, ALU.subtract).then_inc(xq2_ready, 1)

            def residual_a(t):
                dve.wait_ge(wo_ps, at(t, wo_ps, 1))
                dve.wait_ge(xres_ld, at(t, xres_ld, 16))
                V.scalar_tensor_tensor(out=resA[:], in0=PA[1][:, 0:HID], scalar=ga[:, 10:11], in1=xres[:],
                                       op0=ALU.mult, op1=ALU.add).then_inc(resA_ready, 1)
                statistics(t, stA, resA, resA_ready, bnA, varA_ready)

            def norm_a(t):
                dve.wait_ge(rstdA_ready, at(t, rstdA_ready, 1))
                if t.later:
                    dve.wait_ge(x1_hi, at(t, x1_hi, 0))
                    dve.wait_ge(x1_lo, at(t, x1_lo, 0))
                    dve.wait_ge(resB_ready, at(t, resB_ready, 0))
                V.tensor_scalar(x1[:], resA[:], stA[:, 6:7], stA[:, 8:9], ALU.subtract, ALU.mult).then_inc(x1_ready, 1)

            def context_max(t):
                dve.wait_ge(ctxt_ld, at(t, ctxt_ld, 16))
                if t.later:
                    dve.wait_ge(call_ready, at(t, call_ready, 0))
                V.tensor_reduce(gb[:, 0:1], ctxt[:], axis=AX.X, op=ALU.max,
                                apply_absolute_value=True).then_inc(cmax_ready, 1)

            def context_parts(t):
                link = chain(dve, t, cscale)
                dve.wait_ge(call_ready, at(t, call_ready, 1))
                if t.later:
                    dve.wait_ge(probsB_ready, at(t, probsB_ready, 0))
                    dve.wait_ge(cs_ps, at(t, cs_ps, 0))
                link(V.tensor_scalar(gb[:, 1:2], call[:], TINY, None, ALU.max))
                V.tensor_scalar(gb[:, 3:4], gb[:, 1:2], XD ** -0.5, None, ALU.mult)
                link(V.reciprocal(gb[:, 2:3], gb[:, 1:2]))
                link(V.tensor_scalar(cnorm[:], ctxt[:], gb[:, 2:3], None, ALU.mult))
                link(V.tensor_copy(c_parts[:, :, RIGHT_HI], twice(cnorm[:], 2)))
                V.tensor_tensor(c_parts[:, :, RIGHT_LO], twice(cnorm[:], 2), c_parts[:, :, RIGHT_HI],
                                ALU.subtract).then_inc(c_ready, 1)

            def mask_context(t):
                dve.wait_ge(cs_ps, at(t, cs_ps, 1))
                if t.later:
                    dve.wait_ge(eB_ps, at(t, eB_ps, 0))
                for k in range(4):
                    last = V.tensor_scalar(cs[:, :, :, k].rearrange("p c b t -> p (c b) t"),
                                           heads(PB[1][:, 0:P].bitcast(F16), SEQ),
                                           cst[:, C_MASKB + k:C_MASKB + k + 1], None, ALU.mult)
                last.then_inc(cs_ready, 1)

            def maxima_b(t, ks_):
                for k in ks_:
                    dve.wait_ge(sB_ps, at(t, sB_ps, k + 1))
                    V.tensor_reduce(mB[:, k * 8:k * 8 + 8], heads(PB[k % 2][:], SEQ), axis=AX.X,
                                    op=ALU.max).then_inc(mB_done, 1)
                if 3 in ks_:
                    dve.wait_ge(mB_done, at(t, mB_done, 4))
                    if t.later:
                        dve.wait_ge(mTB_ps, at(t, mTB_ps, 0))
                    V.tensor_copy(mpB[:, 0:2 * XP], mB[:]).then_inc(mhB_ready, 1)
                    dve.wait_ge(mhB_ready, at(t, mhB_ready, 1))
                    V.tensor_tensor(mpB[:, 2 * XP:4 * XP], mB[:], mpB[:, 0:2 * XP], ALU.subtract).then_inc(mpB_ready, 1)

            def normalise_b(t):
                dve.wait_ge(oB_ps, at(t, oB_ps, 1))
                o = heads(PB[0][:, 0:2 * XP * (XD + 1)], XD + 1)
                V.reciprocal(rsB[:].rearrange("p (h o) -> p h o", o=1), o[:, :, XD:XD + 1]).then_inc(rsB_ready, 1)
                dve.wait_ge(rsB_ready, at(t, rsB_ready, 1))
                V.tensor_tensor(heads(attB[:], XD), o[:, :, 0:XD], each(rsB[:], 2 * XP, XD),
                                ALU.mult).then_inc(attB_ready, 1)
                dve.wait_ge(attB_ready, at(t, attB_ready, 1))
                V.tensor_tensor(resB[:], attB[:], x1[:], ALU.add).then_inc(resB_ready, 1)
                statistics(t, stB, resB, resB_ready, bnB, varB_ready)

            def norm_b(t):
                dve.wait_ge(rstdB_ready, at(t, rstdB_ready, 1))
                if t.later:
                    dve.wait_ge(xT_ps, at(t, xT_ps, 0))
                    dve.wait_ge(resC_ready, at(t, resC_ready, 0))
                V.tensor_scalar(x2[:], resB[:], stB[:, 6:7], stB[:, 8:9], ALU.subtract, ALU.mult).then_inc(x2_ready, 1)

            def x_low(t):
                dve.wait_ge(xTh_ready, at(t, xTh_ready, 1))
                V.tensor_tensor(xTl[:], TR[:, 0:HID].rearrange("p (k t) -> p k t", k=KC), xTh[:].bitcast(F32),
                                ALU.subtract).then_inc(xTl_ready, 1)

            def top2(t):
                link = chain(dve, t, route)
                scores, top, key, ktop, sel = rt[:, 0], rt[:, 1], rt[:, 2], rt[:, 3], rt[:, 4]
                tie, thr = rt[:, 5, 0:1], rt[:, 5, 1:2]
                rank = cst[:, C_RANK:C_RANK + NE]
                dve.wait_ge(gate_th, at(t, gate_th, 1))
                link(V.tensor_scalar(scores, tanh_g[:], 0.5, 0.5, ALU.mult, ALU.add))
                settle(dve)
                link(V.max(top, scores))
                link(V.scalar_tensor_tensor(out=key, in0=scores, scalar=top[:, 1:2], in1=rank,
                                            op0=ALU.is_equal, op1=ALU.mult))
                settle(dve)
                link(V.max(ktop, key))
                link(V.tensor_tensor(tie, top[:, 0:1], top[:, 1:2], ALU.is_equal))
                link(V.tensor_tensor(thr, ktop[:, 1:2], ktop[:, 0:1], ALU.subtract))
                link(V.scalar_tensor_tensor(out=thr, in0=thr, scalar=tie, in1=ktop[:, 0:1], op0=ALU.mult, op1=ALU.add))
                link(V.tensor_scalar(sel, key, thr, None, ALU.is_ge))
                link(V.scalar_tensor_tensor(out=sel, in0=scores, scalar=top[:, 1:2], in1=sel,
                                            op0=ALU.is_gt, op1=ALU.add))
                V.tensor_tensor(sc9[:, 0:NE], sel, scores, ALU.mult).then_inc(s_ready, 1)
                dve.wait_ge(s_ready, at(t, s_ready, 1))

            def scale_up(t, n):
                w, k = width(n), n % 2
                s = sc9[:, 2 * (n - 1):2 * n] if n else sc9[:, NE:NE + 1]
                dve.wait_ge(up_ps, at(t, up_ps, n + 1))
                if t.later or n >= 2:
                    dve.wait_ge(h_ready, at(t, h_ready, max(n - 1, 0)))
                V.tensor_tensor(heads(zA[:, k, 0:w], P), heads(UP[k][:, 0:w], P), each(s, w // P, P),
                                ALU.mult).then_inc(zA_ready, 1)
                V.tensor_tensor(heads(zB[:, k, 0:w], P), heads(UP[k][:, w:2 * w], P), each(s, w // P, P),
                                ALU.mult).then_inc(zB_ready, 1)

            def gated(t, n):
                w, k = width(n), n % 2
                dve.wait_ge(th_ready, at(t, th_ready, n + 1))
                V.scalar_tensor_tensor(out=hg[:, k, 0:w], in0=th[:, k, 0:w], scalar=1.0, in1=zA[:, k, 0:w],
                                       op0=ALU.add, op1=ALU.mult).then_inc(hg_ready, 1)

            def h_low(t, n):
                w, k = width(n), n % 2
                dve.wait_ge(hTh_ready, at(t, hTh_ready, n + 1))
                V.tensor_tensor(hTl[:, k, 0:w], TR[:, 0:w], hTh[:, k, 0:w].bitcast(F32),
                                ALU.subtract).then_inc(hTl_ready, 1)

            def residual_c(t):
                dve.wait_ge(down_ps, at(t, down_ps, NB))
                V.scalar_tensor_tensor(out=resC[:], in0=ACC[:, 0:HID], scalar=0.5, in1=x2[:],
                                       op0=ALU.mult, op1=ALU.add).then_inc(resC_ready, 1)
                statistics(t, stC, resC, resC_ready, bnC, varC_ready)

            def norm_c(t):
                dve.wait_ge(rstdC_ready, at(t, rstdC_ready, 1))
                if t.later:
                    dve.wait_ge(y_out, at(t, y_out, 0))
                V.tensor_scalar(y[:], resC[:], stC[:, 6:7], stC[:, 8:9], ALU.subtract, ALU.mult).then_inc(y_ready, 1)

            def turn(a, b, c):
                if c:
                    x_low(c)
                if a:
                    quantise(a)
                if b:
                    mask_context(b)
                if a:
                    token_scales(a)
                if c:
                    scale_up(c, 0)
                    top2(c)
                    gated(c, 0)
                    scale_up(c, 1)
                if a:
                    rope_parts(a)
                if b:
                    maxima_b(b, (0, 1))
                if c:
                    h_low(c, 0)
                    gated(c, 1)
                if b:
                    maxima_b(b, (2, 3))
                if c:
                    scale_up(c, 2)
                if a:
                    v_heads(a)
                if c:
                    h_low(c, 1)
                    gated(c, 2)
                if a:
                    mask_k(a)
                if c:
                    scale_up(c, 3)
                    h_low(c, 2)
                    gated(c, 3)
                if a:
                    maxima_a(a)
                if c:
                    scale_up(c, 4)
                    h_low(c, 3)
                    gated(c, 4)
                if b:
                    normalise_b(b)
                if a:
                    normalise_a(a)
                if c:
                    h_low(c, 4)
                    residual_c(c)
                if b:
                    norm_b(b)
                if a:
                    context_max(a)
                if c:
                    norm_c(c)
                if a:
                    residual_a(a)
                    context_parts(a)
                    norm_a(a)

            dve.wait_ge(ld_cst, 16)
            dve.wait_ge(cst16, 1)
            run(dve, turn)

        @block.scalar
        def _(act):
            S = nc.scalar
            act.wait_ge(ld_cst, 16)
            S.copy(ident16[:], ident)
            S.copy(identb[:], ident)
            S.copy(selA[:], cst[:, C_SELA:C_SELB])
            S.copy(selB[:], cst[:, C_SELB:C_DUP]).then_inc(cst16, 1)

            def ffn_high_parts():
                act.wait_ge(ld_ffn, FFN_LOADS)
                S.copy(gth[:], gt[:])
                S.copy(w13h[:], w13[:])
                S.copy(w2h[:], w2f[:]).then_inc(ffn_hi, 1)

            def copy_xqT(t):
                act.wait_ge(xqT_ps, at(t, xqT_ps, 1))
                if t.later:
                    act.wait_ge(v_ps, at(t, v_ps, 0))
                S.copy(xqT[:], PA[0][:, 0:P].bitcast(BF16).rearrange("p (k t) -> p k t", k=KC)).then_inc(xqT_ready, 1)

            def qk_high(t):
                act.wait_ge(rope_sum, at(t, rope_sum, 1))
                if t.later:
                    act.wait_ge(ks_ps, at(t, ks_ps, 0))
                S.copy(qk_parts[:, 0:SP_, LEFT_HI], twice(rope[:, 0:HID], SP_))
                S.copy(qk_parts[:, SP_:2 * SP_, RIGHT_HI], twice(rope[:, HID:2 * HID], SP_)).then_inc(qk_hi, 1)

            def v_heads(t):
                act.wait_ge(v_even, at(t, v_even, 1))
                if t.later:
                    act.wait_ge(oA_ps, at(t, oA_ps, 0))
                for b in range(2):
                    last = S.activation(vA[SEQ:P, b, :, 1, 0:SD], heads(PA[0][SEQ:P, b * P:(b + 1) * P], SD),
                                        ACT.Copy, scale=gvd[SEQ:P, b:b + 1])
                last.then_inc(v_odd, 1)

            def copy_stacks_a(t):
                act.wait_ge(qs_ps, at(t, qs_ps, 1))
                if t.later:
                    act.wait_ge(eA_ps, at(t, eA_ps, 0))
                S.copy(qs[:], heads(PA[0][:].bitcast(F16), P)).then_inc(qs_ready, 1)
                act.wait_ge(ks_even, at(t, ks_even, 1))
                S.activation(ks[:, :, :, 1].rearrange("p h b t -> p (h b) t"), heads(PA[1][:].bitcast(F16), SEQ), ACT.Copy,
                             scale=cst[:, C_MASKA + 1:C_MASKA + 2]).then_inc(ks_odd, 1)

            def copy_maxima_a(t):
                act.wait_ge(mTA_ps, at(t, mTA_ps, 1))
                if t.later:
                    act.wait_ge(eA_ps, at(t, eA_ps, 0))
                S.copy(mTA[:], PA[0][:, 0:P // 2].bitcast(BF16)).then_inc(mTA_ready, 1)

            def exp_a(t):
                if t.later:
                    act.wait_ge(oA_ps, at(t, oA_ps, 0))
                for k in range(2):
                    act.wait_ge(eA_ps, at(t, eA_ps, k + 1))
                    S.activation(probsA[:, 4 * k:4 * k + 4].rearrange("p h t -> p (h t)"), PA[k][:], ACT.Exp,
                                 scale=ga[:, 5:6]).then_inc(probsA_ready, 1)

            def copy_xq2T(t):
                act.wait_ge(xq2T_ps, at(t, xq2T_ps, 1))
                if t.later:
                    act.wait_ge(wo_ps, at(t, wo_ps, 0))
                S.copy(xq2T[:], PA[1][:, 0:P].bitcast(BF16).rearrange("p (k t) -> p k t", k=KC)).then_inc(xq2T_ready, 1)

            def x1_high(t):
                act.wait_ge(x1_ready, at(t, x1_ready, 1))
                if t.later:
                    act.wait_ge(xs_ps, at(t, xs_ps, 0))
                S.copy(x_parts[:, :, LEFT_HI], twice(x1[:], 8)).then_inc(x1_hi, 1)

            def copy_stacks_b(t):
                act.wait_ge(xs_ps, at(t, xs_ps, 1))
                if t.later:
                    act.wait_ge(eB_ps, at(t, eB_ps, 0))
                S.copy(xs[:], heads(PB[0][:].bitcast(F16), P)).then_inc(xs_ready, 1)

            def copy_maxima_b(t):
                act.wait_ge(mTB_ps, at(t, mTB_ps, 1))
                if t.later:
                    act.wait_ge(eB_ps, at(t, eB_ps, 0))
                S.copy(mTB[:], PB[0][:, 0:P // 2].bitcast(BF16)).then_inc(mTB_ready, 1)

            def exp_b(t, banks):
                if t.later and 0 in banks:
                    act.wait_ge(oB_ps, at(t, oB_ps, 0))
                for k in banks:
                    act.wait_ge(eB_ps, at(t, eB_ps, k + 1))
                    S.activation(probsB[:, 4 * k:4 * k + 4].rearrange("p h t -> p (h t)"), PB[k % 2][:], ACT.Exp,
                                 scale=gb[:, 3:4]).then_inc(probsB_ready, 1)

            def x_high(t):
                act.wait_ge(xT_ps, at(t, xT_ps, 1))
                if t.later:
                    act.wait_ge(up_ps, at(t, up_ps, 0))
                S.copy(xTh[:], TR[:, 0:HID].rearrange("p (k t) -> p k t", k=KC)).then_inc(xTh_ready, 1)

            def gate_tanh(t):
                act.wait_ge(gate_ps, at(t, gate_ps, 1))
                if t.later:
                    act.wait_ge(s_ready, at(t, s_ready, 0))
                S.activation(tanh_g[:], TR[:, HID:HID + NE], ACT.Tanh, scale=0.5).then_inc(gate_th, 1)

            def z_tanh(t, n):
                w, k = width(n), n % 2
                act.wait_ge(zA_ready, at(t, zA_ready, n + 1))
                if t.later or n >= 2:
                    act.wait_ge(hg_ready, at(t, hg_ready, max(n - 1, 0)))
                S.activation(th[:, k, 0:w], zA[:, k, 0:w], ACT.Tanh, scale=0.5).then_inc(th_ready, 1)

            def h_high(t, n):
                w, k = width(n), n % 2
                act.wait_ge(hT_ps, at(t, hT_ps, n + 1))
                if t.later or n >= 2:
                    act.wait_ge(down_ps, at(t, down_ps, max(n - 1, 0)))
                S.copy(hTh[:, k, 0:w], TR[:, 0:w]).then_inc(hTh_ready, 1)

            def turn(a, b, c):
                if c:
                    x_high(c)
                if b:
                    x1_high(b)
                if a:
                    copy_xqT(a)
                if c:
                    gate_tanh(c)
                if b:
                    copy_stacks_b(b)
                if c:
                    z_tanh(c, 0)
                    z_tanh(c, 1)
                    h_high(c, 0)
                if a:
                    qk_high(a)
                if c:
                    z_tanh(c, 2)
                    h_high(c, 1)
                if a:
                    v_heads(a)
                if b:
                    copy_maxima_b(b)
                if a:
                    copy_stacks_a(a)
                if c:
                    z_tanh(c, 3)
                    h_high(c, 2)
                if b:
                    exp_b(b, (0, 1))
                if c:
                    z_tanh(c, 4)
                    h_high(c, 3)
                if a:
                    copy_maxima_a(a)
                if b:
                    exp_b(b, (2, 3))
                if a:
                    exp_a(a)
                if c:
                    h_high(c, 4)
                if a:
                    copy_xq2T(a)

            run_first = [True]

            def turn_and_weights(a, b, c):
                turn(a, b, c)
                if run_first[0]:
                    run_first[0] = False
                    ffn_high_parts()

            run(act, turn_and_weights)

        @block.gpsimd
        def _(pool):
            G = nc.gpsimd
            pool.wait_ge(wabs_ready, 1)
            G.partition_all_reduce(wsum[:], wabs[:], P, RADD).then_inc(wsum_ready, 1)
            pool.wait_ge(wsum_ready, 1)
            pool.wait_ge(set_up, 2)

            def ffn_low_parts():
                pool.wait_ge(ffn_hi, 1)
                G.tensor_tensor(gtl[:], gt[:], gth[:].bitcast(F32), ALU.subtract)
                G.tensor_tensor(w13l[:], w13[:], w13h[:].bitcast(F32), ALU.subtract)
                G.tensor_tensor(w2l[:], w2f[:], w2h[:].bitcast(F32), ALU.subtract).then_inc(ffn_lo, 1)

            def rstd(t, var_ready, st, eps_added, rstd_ready):
                pool.wait_ge(var_ready, at(t, var_ready, 1))
                settle(pool)
                G.tensor_scalar(st[:, 7:8], st[:, 7:8], EPS, None, ALU.add).then_inc(eps_added, 1)
                pool.wait_ge(eps_added, at(t, eps_added, 1))
                G.tensor_tensor(st[:, 8:9], st[:, 7:8], neghalf[:], ALU.pow).then_inc(rstd_ready, 1)

            def largest_g(t):
                pool.wait_ge(g_ready, at(t, g_ready, 1))
                if t.later:
                    pool.wait_ge(scales, at(t, scales, 0))
                settle(pool)
                G.partition_all_reduce(gall[:], ga[:, 1:2], P, RMAX).then_inc(gall_ready, 1)
                pool.wait_ge(gall_ready, at(t, gall_ready, 1))

            def add_rope(t):
                pool.wait_ge(rope_ready, at(t, rope_ready, 2))
                if t.later:
                    pool.wait_ge(qk_hi, at(t, qk_hi, 0))
                G.tensor_tensor(rope[:], rope_c[:], rope_s[:], ALU.add).then_inc(rope_sum, 1)

            def qk_low(t):
                pool.wait_ge(qk_hi, at(t, qk_hi, 1))
                G.tensor_tensor(qk_parts[:, 0:SP_, LEFT_LO], twice(rope[:, 0:HID], SP_), qk_parts[:, 0:SP_, LEFT_HI],
                                ALU.subtract)
                G.tensor_tensor(qk_parts[:, SP_:2 * SP_, RIGHT_LO], twice(rope[:, HID:2 * HID], SP_),
                                qk_parts[:, SP_:2 * SP_, RIGHT_HI], ALU.subtract).then_inc(qk_lo, 1)

            def largest_c(t):
                pool.wait_ge(cmax_ready, at(t, cmax_ready, 1))
                if t.later:
                    pool.wait_ge(c_ready, at(t, c_ready, 0))
                settle(pool)
                G.partition_all_reduce(call[:], gb[:, 0:1], P, RMAX).then_inc(call_ready, 1)
                pool.wait_ge(call_ready, at(t, call_ready, 1))

            def context_v(t):
                pool.wait_ge(ctxd_ld, at(t, ctxd_ld, 32))
                pool.wait_ge(x1_lo, at(t, x1_lo, 1))
                if t.later:
                    pool.wait_ge(oB_ps, at(t, oB_ps, 0))
                settle(pool)
                for h in range(2):
                    for b in range(2):
                        last = G.tensor_copy(vB[h * SEQ:(h + 1) * SEQ, b, :, h, 0:XD],
                                             ctxd[h * SEQ:(h + 1) * SEQ, b].rearrange(
                                                 "p (q two d) -> p q two d", two=2, d=XD)[:, :, h])
                last.then_inc(vB_ready, 1)
                pool.wait_ge(vB_ready, at(t, vB_ready, 1))

            def x1_low(t):
                pool.wait_ge(x1_hi, at(t, x1_hi, 1))
                G.tensor_tensor(x_parts[:, :, LEFT_LO], twice(x1[:], 8), x_parts[:, :, LEFT_HI],
                                ALU.subtract).then_inc(x1_lo, 1)

            def times_up(t, n):
                w, k = width(n), n % 2
                pool.wait_ge(zB_ready, at(t, zB_ready, n + 1))
                if t.later or n >= 2:
                    pool.wait_ge(hT_ps, at(t, hT_ps, max(n - 1, 0)))
                pool.wait_ge(hg_ready, at(t, hg_ready, n + 1))
                G.tensor_tensor(hh[:, k, 0:w], hg[:, k, 0:w], zB[:, k, 0:w], ALU.mult).then_inc(h_ready, 1)

            def turn(a, b, c):
                if b:
                    x1_low(b)
                    context_v(b)
                if a:
                    largest_g(a)
                if c:
                    times_up(c, 0)
                if a:
                    add_rope(a)
                if c:
                    times_up(c, 1)
                if a:
                    qk_low(a)
                if c:
                    times_up(c, 2)
                    times_up(c, 3)
                    times_up(c, 4)
                if b:
                    rstd(b, varB_ready, stB, epsB, rstdB_ready)
                if a:
                    largest_c(a)
                if c:
                    rstd(c, varC_ready, stC, epsC, rstdC_ready)
                if a:
                    rstd(a, varA_ready, stA, epsA, rstdA_ready)

            pool_first = [True]

            def turn_and_weights(a, b, c):
                turn(a, b, c)
                if pool_first[0]:
                    pool_first[0] = False
                    ffn_low_parts()

            run(pool, turn_and_weights)

        @block.tensor
        def _(pe):
            T = nc.tensor
            pe.wait_ge(cst16, 1)
            pe.wait_ge(set_up, 2)
            pe.wait_ge(watt_ready, 1)

            def transpose_xq(t):
                pe.wait_ge(xq_ready, at(t, xq_ready, 1))
                if t.later:
                    pe.wait_ge(att_ready, at(t, att_ready, 0))
                for k in range(KC):
                    last = T.transpose(PA[0][:, 0:P].bitcast(BF16)[:, k * P:(k + 1) * P], xq[:, k * P:(k + 1) * P], identb[:])
                last.then_inc(xqT_ps, 1)

            def project_qk(t):
                pe.wait_ge(xqT_ready, at(t, xqT_ready, 1))
                if t.later:
                    pe.wait_ge(resA_ready, at(t, resA_ready, 0))
                for n, w in enumerate((wqk, wqk_rot)):
                    for k in range(KC):
                        last = T.matmul(PA[n][:], xqT[:, k], w[:, k], start=(k == 0), stop=(k == KC - 1))
                    last.then_inc(qk_ps, 1)

            def project_v(t):
                pe.wait_ge(rope_ready, at(t, rope_ready, 2))
                for b in range(2):
                    for h in range(2):
                        for k in range(KC):
                            T.matmul(PA[0][h * SEQ:(h + 1) * SEQ, b * P:(b + 1) * P], xqT[:, k, b * SEQ:(b + 1) * SEQ],
                                     wv_t[:, k].rearrange("p (h two d) -> p h two d", two=2, d=SD)[:, :, h],
                                     start=(k == 0), stop=(k == KC - 1))
                pe.wait_ge(scales, at(t, scales, 2))
                for b in range(2):
                    last = T.matmul(PA[1][:, b:b + 1], dup[:, b * P:(b + 1) * P], ga[:, 6:7], start=True, stop=True)
                last.then_inc(v_ps, 1)

            def stack_a(t):
                pe.wait_ge(qk_lo, at(t, qk_lo, 1))
                pe.wait_ge(v_odd, at(t, v_odd, 1))
                for pair in range(SP_):
                    last = T.transpose(PA[0][:].bitcast(F16)[:, pair * P:(pair + 1) * P],
                                       qk_parts[:, pair].rearrange("p a d -> p (a d)"), ident16[:])
                last.then_inc(qs_ps, 1)
                for pair in range(SP_):
                    last = T.transpose(PA[1][:].bitcast(F16)[:, pair * P:(pair + 1) * P],
                                       qk_parts[:, SP_ + pair].rearrange("p a d -> p (a d)"), ident16[:])
                last.then_inc(ks_ps, 1)

            def scores_a(t):
                pe.wait_ge(qs_ready, at(t, qs_ready, 1))
                pe.wait_ge(ks_odd, at(t, ks_odd, 1))
                for pair in range(SP_):
                    for b in range(2):
                        first = pair % 4 * P
                        last = T.matmul(PA[pair // 4][b * SEQ:(b + 1) * SEQ, first:first + P],
                                        qs[:, pair, b * SEQ:(b + 1) * SEQ], ks[:, pair, b].rearrange("p h t -> p (h t)"),
                                        start=True, stop=True)
                    if pair % 4 == 3:
                        last.then_inc(sA_ps, 1)

            def transpose_maxima_a(t):
                pe.wait_ge(mpA_ready, at(t, mpA_ready, 1))
                T.transpose(PA[0][:, 0:P // 2].bitcast(BF16), mpA[:], identb[:]).then_inc(mTA_ps, 1)

            def exponents_a(t):
                pe.wait_ge(mTA_ready, at(t, mTA_ready, 1))
                for pair in range(SP_):
                    first = pair % 4 * P
                    T.matmul(PA[pair // 4][:, first:first + P], selA[:, pair * P:(pair + 1) * P], mTA[:],
                             start=True, stop=False)
                    for b in range(2):
                        last = T.matmul(PA[pair // 4][:, first + b * SEQ:first + (b + 1) * SEQ],
                                        ks[:, pair, b].rearrange("p h t -> p (h t)"), qs[:, pair, b * SEQ:(b + 1) * SEQ],
                                        start=False, stop=(b == 1))
                    if pair % 4 == 3:
                        last.then_inc(eA_ps, 1)

            def attend_a(t):
                pe.wait_ge(probsA_ready, at(t, probsA_ready, 2))
                for pair in range(SP_):
                    first = pair * 2 * (SD + 1)
                    for b in range(2):
                        last = T.matmul(PA[0][b * SEQ:(b + 1) * SEQ, first:first + 2 * (SD + 1)],
                                        probsA[:, pair, b * SEQ:(b + 1) * SEQ],
                                        vA[:, b, pair].rearrange("p h d -> p (h d)"), start=True, stop=True)
                last.then_inc(oA_ps, 1)

            def transpose_xq2(t):
                pe.wait_ge(xq2_ready, at(t, xq2_ready, 1))
                for k in range(KC):
                    last = T.transpose(PA[1][:, 0:P].bitcast(BF16)[:, k * P:(k + 1) * P], xq2[:, k * P:(k + 1) * P], identb[:])
                last.then_inc(xq2T_ps, 1)

            def project_out(t):
                pe.wait_ge(xq2T_ready, at(t, xq2T_ready, 1))
                for k in range(KC):
                    last = T.matmul(PA[1][:, 0:HID], xq2T[:, k], wo_t[:, k], start=(k == 0), stop=(k == KC - 1))
                last.then_inc(wo_ps, 1)

            def stack_context(t):
                pe.wait_ge(c_ready, at(t, c_ready, 1))
                if t.later:
                    pe.wait_ge(probsB_ready, at(t, probsB_ready, 0))
                for c in range(2):
                    last = T.transpose(PB[1][:, 0:P].bitcast(F16)[:, c * P:(c + 1) * P],
                                       c_parts[:, c].rearrange("p a d -> p (a d)"), ident16[:])
                last.then_inc(cs_ps, 1)

            def stack_x1(t):
                pe.wait_ge(x1_lo, at(t, x1_lo, 1))
                if t.later:
                    pe.wait_ge(attB_ready, at(t, attB_ready, 0))
                for cg in range(8):
                    last = T.transpose(PB[0][:].bitcast(F16)[:, cg * P:(cg + 1) * P],
                                       x_parts[:, cg].rearrange("p a d -> p (a d)"), ident16[:])
                last.then_inc(xs_ps, 1)

            def scores_b(t, banks):
                if 0 in banks:
                    pe.wait_ge(xs_ready, at(t, xs_ready, 1))
                    pe.wait_ge(cs_ready, at(t, cs_ready, 1))
                for n in banks:
                    if n >= 2:
                        pe.wait_ge(mB_done, at(t, mB_done, n - 1))
                    for cg in (2 * n, 2 * n + 1):
                        first = cg % 2 * 4 * SEQ
                        for b in range(2):
                            last = T.matmul(PB[n % 2][b * SEQ:(b + 1) * SEQ, first:first + 4 * SEQ],
                                            xs[:, cg, b * SEQ:(b + 1) * SEQ], cs[:, cg // 4, b].rearrange("p h t -> p (h t)"),
                                            start=True, stop=True)
                    last.then_inc(sB_ps, 1)

            def transpose_maxima_b(t):
                pe.wait_ge(mpB_ready, at(t, mpB_ready, 1))
                T.transpose(PB[0][:, 0:P // 2].bitcast(BF16), mpB[:], identb[:]).then_inc(mTB_ps, 1)

            def exponents_b(t, banks):
                if 0 in banks:
                    pe.wait_ge(mTB_ready, at(t, mTB_ready, 1))
                for n in banks:
                    if n >= 2:
                        pe.wait_ge(probsB_ready, at(t, probsB_ready, n - 1))
                    for hp in range(4 * n, 4 * n + 4):
                        c, cg, half = hp // 8, hp // 2, hp % 2
                        first = hp % 4 * P
                        T.matmul(PB[n % 2][:, first:first + P], selB[:, hp * P:(hp + 1) * P], mTB[:], start=True, stop=False)
                        for b in range(2):
                            last = T.matmul(PB[n % 2][:, first + b * SEQ:first + (b + 1) * SEQ],
                                            cs[:, c, b, 2 * half:2 * half + 2].rearrange("p h t -> p (h t)"),
                                            xs[:, cg, b * SEQ:(b + 1) * SEQ], start=False, stop=(b == 1))
                    last.then_inc(eB_ps, 1)

            def attend_b(t):
                pe.wait_ge(probsB_ready, at(t, probsB_ready, 4))
                pe.wait_ge(vB_ready, at(t, vB_ready, 1))
                for hp in range(XP):
                    first = hp * 2 * (XD + 1)
                    for b in range(2):
                        last = T.matmul(PB[0][b * SEQ:(b + 1) * SEQ, first:first + 2 * (XD + 1)],
                                        probsB[:, hp, b * SEQ:(b + 1) * SEQ],
                                        vB[:, b, hp // 8 * 2 + hp % 2].rearrange("p h d -> p (h d)"),
                                        start=True, stop=True)
                last.then_inc(oB_ps, 1)

            parts = [(a, w, k) for a, w in ((xTh, 0), (xTl, 0), (xTh, 1)) for k in range(KC)]

            def transpose_x2(t):
                pe.wait_ge(x2_ready, at(t, x2_ready, 1))
                if t.later:
                    pe.wait_ge(hTl_ready, at(t, hTl_ready, 0))
                for k in range(KC):
                    last = T.transpose(TR[:, k * P:(k + 1) * P], x2[:, k * P:(k + 1) * P], ident)
                last.then_inc(xT_ps, 1)

            def gate_logits(t):
                pe.wait_ge(ffn_lo, 1)
                pe.wait_ge(xTl_ready, at(t, xTl_ready, 1))
                for n, (a, w, k) in enumerate(parts):
                    last = T.matmul(TR[:, HID:HID + NE], a[:, k], (gth, gtl)[w][:, k], start=(n == 0), stop=(n == 5))
                last.then_inc(gate_ps, 1)

            def up(t, m):
                first, w_ = (4 * (m - 1) * P, 4 * P) if m else (2 * NE * P, 2 * P)
                if t.later or m >= 2:
                    pe.wait_ge(zB_ready, at(t, zB_ready, max(m - 1, 0)))
                for n, (a, w, k) in enumerate(parts):
                    last = T.matmul(UP[m % 2][:, 0:w_], a[:, k], (w13h, w13l)[w][:, k, first:first + w_],
                                    start=(n == 0), stop=(n == 5))
                last.then_inc(up_ps, 1)

            def transpose_h(t, m):
                pe.wait_ge(h_ready, at(t, h_ready, m + 1))
                if m:
                    pe.wait_ge(hTl_ready, at(t, hTl_ready, m))
                else:
                    pe.wait_ge(gate_th, at(t, gate_th, 1))
                for e in range(width(m) // P):
                    last = T.transpose(TR[:, e * P:(e + 1) * P], hh[:, m % 2, e * P:(e + 1) * P], ident)
                last.then_inc(hT_ps, 1)

            def down(t, m):
                pe.wait_ge(hTl_ready, at(t, hTl_ready, m + 1))
                if m == 0 and t.later:
                    pe.wait_ge(resC_ready, at(t, resC_ready, 0))
                for e in range(width(m) // P):
                    ex = 2 * (m - 1) + e if m else NE
                    for n, (a, w) in enumerate(((hTh, w2h), (hTl, w2h), (hTh, w2l))):
                        last = T.matmul(ACC[:, 0:HID], a[:, m % 2, e * P:(e + 1) * P], w[:, ex],
                                        start=(m == 0 and n == 0), stop=(m == NB - 1 and e == 1 and n == 2))
                last.then_inc(down_ps, 1)

            def turn(a, b, c):
                if c:
                    transpose_x2(c)
                if b:
                    stack_context(b)
                if a:
                    transpose_xq(a)
                if b:
                    stack_x1(b)
                if c:
                    gate_logits(c)
                    up(c, 0)
                if a:
                    project_qk(a)
                if c:
                    up(c, 1)
                if b:
                    scores_b(b, (0, 1))
                if a:
                    project_v(a)
                if c:
                    transpose_h(c, 0)
                if b:
                    scores_b(b, (2, 3))
                if c:
                    down(c, 0)
                    up(c, 2)
                    transpose_h(c, 1)
                if b:
                    transpose_maxima_b(b)
                if a:
                    stack_a(a)
                if c:
                    down(c, 1)
                    up(c, 3)
                    transpose_h(c, 2)
                if b:
                    exponents_b(b, (0, 1))
                if a:
                    scores_a(a)
                if c:
                    down(c, 2)
                    up(c, 4)
                    transpose_h(c, 3)
                if b:
                    exponents_b(b, (2, 3))
                if a:
                    transpose_maxima_a(a)
                if c:
                    down(c, 3)
                if a:
                    exponents_a(a)
                if b:
                    attend_b(b)
                if c:
                    transpose_h(c, 4)
                if a:
                    attend_a(a)
                if c:
                    down(c, 4)
                if a:
                    transpose_xq2(a)
                    project_out(a)

            run(pe, turn)


def kernel(x, ctx_512, L0_attn_w_q, L0_attn_w_k, L0_attn_w_v, L0_attn_w_o, L0_ffn_gate_w, L0_ffn_w1, L0_ffn_w2,
           L0_ffn_w3, L0_ffn_ws1, L0_ffn_ws2, L0_ffn_ws3):
    import concourse.bacc as bacc
    from concourse.bass_utils import run_bass_kernel_spmd

    def chunks(w):
        w = np.asarray(w)
        return w.T.reshape(KC, P, w.shape[0]).transpose(1, 0, 2)

    def experts(w):
        w = np.asarray(w)
        return w.transpose(2, 0, 1).reshape(KC, P, -1)

    order = np.arange(HID).reshape(2, 4, 4, XD).transpose(0, 2, 1, 3).reshape(-1)
    arrays = {
        "x": np.asarray(x).reshape(-1, P, HID),
        "x_perm": np.asarray(x).reshape(-1, P, HID)[:, :, order],
        "ctx": np.asarray(ctx_512).reshape(-1, P, SEQ),
        "wq": chunks(L0_attn_w_q), "wk": chunks(L0_attn_w_k), "wv": chunks(L0_attn_w_v), "wo": chunks(np.asarray(L0_attn_w_o)[order]),
        "gate": chunks(np.asarray(L0_ffn_gate_w)[:, order]),
        "w1": experts(np.asarray(L0_ffn_w1)[:, :, order]),
        "w2": np.asarray(L0_ffn_w2)[:, order].transpose(2, 0, 1),
        "w3": experts(np.asarray(L0_ffn_w3)[:, :, order]),
        "ws1": experts(np.asarray(L0_ffn_ws1)[None][:, :, order]),
        "ws2": np.asarray(L0_ffn_ws2)[order].T,
        "ws3": experts(np.asarray(L0_ffn_ws3)[None][:, :, order]),
        "const": constants(),
    }
    arrays = {k: np.ascontiguousarray(v) for k, v in arrays.items()}
    nc = bacc.Bacc("TRN2", target_bir_lowering=False, num_devices=1)
    args = [nc.dram_tensor(k, v.shape, mybir.dt.from_np(v.dtype), kind="ExternalInput").ap() for k, v in arrays.items()]
    shape = arrays["x"].shape
    out = nc.dram_tensor("out", shape, F32, kind="ExternalOutput").ap()
    decoder_layer(nc, *args, out)
    r = run_bass_kernel_spmd(nc, [arrays], core_ids=[0])
    return r.results[0]["out"][:, :, np.argsort(order)].reshape(x.shape)
```

```python
from contextlib import ExitStack

import concourse.bass as bass
import numpy as np
from concourse import mybir

F32 = mybir.dt.float32
F32R = mybir.dt.float32r
F16 = mybir.dt.float16
BF16 = mybir.dt.bfloat16
ALU = mybir.AluOpType
ACT = mybir.ActivationFunctionType
AX = mybir.AxisListType
RMAX = bass.bass_isa.ReduceOp.max
RADD = bass.bass_isa.ReduceOp.add

P = 128
SEQ = 64
HID = 256
KC = HID // P
NE = 8
NB = 5
SH = 16
SD = HID // SH
SP_ = SH // 2
XP = 16
XD = 8
EPS = 1e-5
QB = 127.0
MAGIC = 12582912.0
TINY = 1e-30
LAG = 5

C_IDENT = 0
C_SELA = C_IDENT + P
C_SELB = C_SELA + SP_ * P
C_DUP = C_SELB + XP * P
C_COS = C_DUP + 2 * P
C_SIN = C_COS + SD
C_MASKA = C_SIN + SD
C_RANK = C_MASKA + 2
C_END = C_RANK + NE


def constants():
    c = np.zeros((P, C_END), np.float32)
    c[:, C_IDENT:C_IDENT + P] = np.eye(P)
    col = np.arange(P)
    for pair in range(SP_):
        for part in range(2):
            c[part * SH + 2 * pair + col // SEQ, C_SELA + pair * P + col] = -1.0
    for pair in range(XP):
        for part in range(2):
            c[part * 2 * XP + 2 * pair + col // SEQ, C_SELB + pair * P + col] = -1.0
    for b in range(2):
        c[b * SEQ + col % SEQ, C_DUP + b * P + col] = 1.0
    inv_freq = (1.0 / np.float32(10000.0) ** (np.arange(0, SD, 2, dtype=np.float32) / np.float32(SD))).astype(np.float32)
    angle = np.outer(np.arange(P) % SEQ, inv_freq).astype(np.float32)
    c[:, C_COS:C_COS + SD] = np.cos(np.concatenate([angle, angle], 1))
    c[:, C_SIN:C_SIN + SD] = np.concatenate([-np.sin(angle), np.sin(angle)], 1)
    for h in range(2):
        c[:, C_MASKA + h] = (col % 32) // SD == h
    c[:, C_RANK:C_END] = (NE - np.arange(NE)) / (2.0 * NE)
    return c


class Tile:

    def __init__(self, base, shift=0):
        self.base, self.shift = base, shift
        self.later = not isinstance(base, int) or base > 0


def decoder_layer(nc, x, x_perm, ctx_in, wq, wk, wv, wo, gate, w1, w2, w3, ws1, ws2, ws3, const, out):
    ntiles = x.shape[0]
    with ExitStack() as stack:
        def sb(name, shape, dt=F32):
            return stack.enter_context(nc.sbuf_tensor(name, shape, dt))

        def bank(name):
            return stack.enter_context(nc.psum_tensor(name, [P, 512], F32))

        def sem(name):
            return stack.enter_context(nc.semaphore(name))

        rises = {}

        def sig(name, per=1):
            handle = sem(name)
            rises[name] = per
            return handle

        def at(t, handle, n):
            per = rises[handle.name]
            return t.base * per + (t.shift * per + n)

        cst = sb("cst", [P, C_END])
        ident = cst[:, C_IDENT:C_IDENT + P]
        ident16 = sb("ident16", [P, P], F16)
        identb = sb("identb", [P, P], BF16)
        selA = sb("selA", [P, SP_ * P], BF16)
        selB = sb("selB", [P, XP * P], BF16)
        dup = cst[:, C_DUP:C_DUP + 2 * P]
        cos = cst[:, C_COS:C_COS + SD]
        sin = cst[:, C_SIN:C_SIN + SD]
        watt = sb("watt", [P, 4, KC, HID])
        wabs = sb("wabs", [P, 4])
        wsum = sb("wsum", [P, 4])
        wscale = sb("wscale", [P, 4])
        winv = sb("winv", [P, 4])
        wround = sb("wround", [P, KC * HID])
        wqk = sb("wqk", [P, KC, 2 * HID], BF16)
        wqk_rot = sb("wqk_rot", [P, KC, 2 * HID], BF16)
        wv_t = sb("wv_t", [P, KC, HID], BF16)
        wo_t = sb("wo_t", [P, KC, HID], BF16)
        score_c = sb("score_c", [P, 1])
        v_c = sb("v_c", [P, 1])
        o_c = sb("o_c", [P, 1])
        COLS = (2 * NE + 2) * P + NE
        w13 = sb("w13", [P, KC, COLS])
        w13h = sb("w13h", [P, KC, COLS], F32R)
        w13l = sb("w13l", [P, KC, COLS], F32R)
        w2f = sb("w2f", [P, NE + 1, HID])
        w2h = sb("w2h", [P, NE + 1, HID], F32R)
        w2l = sb("w2l", [P, NE + 1, HID], F32R)
        neghalf = sb("neghalf", [P, 1])
        xin = sb("xin", [P, HID])
        xres = sb("xres", [P, HID])
        ga = sb("ga", [P, 12])
        gall = sb("gall", [P, 1])
        rnd = sb("rnd", [P, HID])
        xq = sb("xq", [P, HID], BF16)
        xqT = sb("xqT", [P, KC, P], BF16)
        rope_c = sb("rope_c", [P, 2 * HID])
        rope_s = sb("rope_s", [P, 2 * HID])
        rope = sb("rope", [P, 2 * HID])
        qk_parts = sb("qk_parts", [P, 2 * SP_, 4, 32], F16)
        gvd = sb("gvd", [P, 2])
        vA = sb("vA", [P, 2, SP_, 2, SD + 1])
        qs = sb("qs", [P, SP_, P], F16)
        ks = sb("ks", [P, SP_, 2, 2, SEQ], F16)
        mA = sb("mA", [P, SH])
        mpA = sb("mpA", [P, P], BF16)
        mTA = sb("mTA", [P, P], BF16)
        probsA = sb("probsA", [P, SP_, P])
        rsA = sb("rsA", [P, SH])
        att = sb("att", [P, HID])
        rnd2 = sb("rnd2", [P, HID])
        xq2 = sb("xq2", [P, HID], BF16)
        xq2T = sb("xq2T", [P, KC, P], BF16)
        resA = sb("resA", [P, HID])
        stA = sb("stA", [P, 12])
        x1 = sb("x1", [P, HID])
        ctxt = sb("ctxt", [P, SEQ])
        ctxd = sb("ctxd", [P, 2, SEQ])
        gb = sb("gb", [P, 8])
        call = sb("call", [P, 1])
        cnorm = sb("cnorm", [P, SEQ])
        c_parts = sb("c_parts", [P, 8 * (P + XD)], F16)
        x_parts = sb("x_parts", [P, 8, 4, 32], F16)
        vB = sb("vB", [P, 2, 4, 2, XD + 1])
        xs = sb("xs", [P, 8, P], F16)
        cs = sb("cs", [P, 2, 2, 4, SEQ], F16)
        mB = sb("mB", [P, 2 * XP])
        mpB = sb("mpB", [P, P], BF16)
        mTB = sb("mTB", [P, P], BF16)
        probsB = sb("probsB", [P, XP, P])
        rsB = sb("rsB", [P, 2 * XP])
        attB = sb("attB", [P, HID])
        resB = sb("resB", [P, HID])
        stB = sb("stB", [P, 12])
        x2 = sb("x2", [P, HID])
        xTh = sb("xTh", [P, KC, P], F32R)
        xTl = sb("xTl", [P, KC, P], F32R)
        tanh_g = sb("tanh_g", [P, NE])
        rt = sb("rt", [P, 8, NE])
        gate_s = sb("gate_s", [P, 3, NE])
        th = sb("th", [P, 2, 2 * P])
        ug = sb("ug", [P, 2, 2 * P])
        hh = sb("hh", [P, 2, 2 * P])
        hTh = sb("hTh", [P, 2, 2 * P], F32R)
        hTl = sb("hTl", [P, 2, 2 * P], F32R)
        resC = sb("resC", [P, HID])
        stC = sb("stC", [P, 12])
        y = sb("y", [P, HID])
        PA = [bank("PA0"), bank("PA1")]
        PB = [bank("PB0"), bank("PB1")]
        UP = [bank("UP0"), bank("UP1")]
        TR = bank("TR")
        ACC = bank("ACC")

        ld_att, ld_ffn, ld_cst = sem("ld_att"), sem("ld_ffn"), sem("ld_cst")
        set_up = sem("set_up")
        cst16 = sem("cst16")
        wabs_ready, wsum_ready, wchain = sem("wabs_ready"), sem("wsum_ready"), sem("wchain")
        watt_ready, ffn_hi, ffn_lo = sem("watt_ready"), sem("ffn_hi"), sem("ffn_lo")
        xin_ld, xres_ld = sig("xin_ld", 16), sig("xres_ld", 16)
        quant, g_ready, gall_ready, xq_ready = sig("quant", 4), sig("g_ready"), sig("gall_ready"), sig("xq_ready")
        xqT_ps, xqT_ready = sig("xqT_ps"), sig("xqT_ready")
        scales = sig("scales", 2)
        qk_ps, rope_ready, rope_sum = sig("qk_ps", 2), sig("rope_ready", 2), sig("rope_sum")
        qk_hi, q_lo, k_lo = sig("qk_hi", 2), sig("q_lo"), sig("k_lo")
        v_ps, gvd_ready, v_even, v_odd = sig("v_ps"), sig("gvd_ready"), sig("v_even"), sig("v_odd")
        qs_ps, ks_ps, qs_ready = sig("qs_ps"), sig("ks_ps"), sig("qs_ready")
        ks_even, ks_odd = sig("ks_even"), sig("ks_odd")
        sA_ps, mA_done, mhA_ready, mpA_ready = sig("sA_ps", 2), sig("mA_done", 2), sig("mhA_ready"), sig("mpA_ready")
        mTA_ps, mTA_ready = sig("mTA_ps"), sig("mTA_ready")
        eA_ps, probsA_ready, oA_ps = sig("eA_ps", 2), sig("probsA_ready", 2), sig("oA_ps")
        rsA_ready, att_ready, quant2 = sig("rsA_ready"), sig("att_ready"), sig("quant2", 4)
        xq2_ready, xq2T_ps, xq2T_ready, wo_ps = sig("xq2_ready"), sig("xq2T_ps"), sig("xq2T_ready"), sig("wo_ps")
        resA_ready, bnA, varA_ready = sig("resA_ready"), sig("bnA"), sig("varA_ready")
        epsA, powA, rstdA_ready, x1_ready = sig("epsA"), sig("powA"), sig("rstdA_ready"), sig("x1_ready")
        ctxt_ld, ctxd_ld = sig("ctxt_ld", 16), sig("ctxd_ld", 32)
        cmax_ready, call_ready, cscale, c_ready = sig("cmax_ready"), sig("call_ready"), sig("cscale", 3), sig("c_ready")
        c_high = sig("c_high")
        vB_ready, x1_hi, x1_lo = sig("vB_ready"), sig("x1_hi"), sig("x1_lo")
        xs_ps, cs_ps, xs_ready, cs_ready = sig("xs_ps"), sig("cs_ps"), sig("xs_ready"), sig("cs_ready")
        sB_ps, mB_done, mhB_ready, mpB_ready = sig("sB_ps", 4), sig("mB_done", 4), sig("mhB_ready"), sig("mpB_ready")
        mTB_ps, mTB_ready = sig("mTB_ps"), sig("mTB_ready")
        eB_ps, probsB_ready, oB_ps = sig("eB_ps", 4), sig("probsB_ready", 4), sig("oB_ps")
        rsB_ready, attB_ready, resB_ready = sig("rsB_ready"), sig("attB_ready"), sig("resB_ready")
        bnB, varB_ready, epsB, powB, rstdB_ready, x2_ready = (sig("bnB"), sig("varB_ready"), sig("epsB"), sig("powB"), sig("rstdB_ready"),
                                                        sig("x2_ready"))
        xT_ps, xTh_ready, xTl_ready = sig("xT_ps"), sig("xTh_ready"), sig("xTl_ready")
        gate_th, route, s_ready, sh_ready = sig("gate_th"), sig("route", 5), sig("s_ready"), sig("sh_ready")
        up_ps, th_ready, u_ready = sig("up_ps", NB), sig("th_ready", NB), sig("u_ready", NB)
        h_ready, hT_ps = sig("h_ready", NB), sig("hT_ps", NB)
        hTh_ready, hTl_ready, down_ps = sig("hTh_ready", NB), sig("hTl_ready", NB), sig("down_ps", NB)
        resC_ready, bnC, varC_ready = sig("resC_ready"), sig("bnC"), sig("varC_ready")
        epsC, powC, rstdC_ready, y_ready, y_out = sig("epsC"), sig("powC"), sig("rstdC_ready"), sig("y_ready"), sig("y_out", 16)

        held = {}

        def settle(eng):
            if eng not in held:
                held[eng] = sem(f"held{len(held)}")
            eng.sem_inc(held[eng], 1)

        def chain(eng, t, handle):
            count = [0]

            def link(ins):
                count[0] += 1
                ins.then_inc(handle, 1)
                eng.wait_ge(handle, at(t, handle, count[0]))
            return link

        def twice(ap, n):
            return ap.rearrange("p (n o d) -> p n o d", n=n, o=1).broadcast_to([P, n, 2, 32])

        def each(ap, n, d):
            return ap.rearrange("p (n o) -> p n o", o=1).broadcast_to([P, n, d])

        def heads(ap, d):
            return ap.rearrange("p (h d) -> p h d", d=d)

        LEFT_HI, LEFT_LO = slice(0, 3, 2), slice(1, 4, 2)
        RIGHT_HI, RIGHT_LO = slice(0, 4, 3), slice(1, 3)

        def width(n):
            return P if n == 0 else 2 * P

        def run(eng, turn, after_second=None):
            def single(i):
                turn(*[Tile(i - k) if 0 <= i - k < ntiles else None for k in range(LAG + 1)])
            single(0)
            single(1)
            if after_second:
                after_second()
            for i in range(2, LAG + 1):
                single(i)
            with eng.Fori(LAG + 1, ntiles) as i:
                turn(*[Tile(i, -k) for k in range(LAG + 1)])
            for i in range(ntiles, ntiles + LAG):
                single(i)

        def rows(dram, t):
            if isinstance(t.base, int):
                n = t.base + t.shift
                return dram[n:n + 1].rearrange("a p c -> (a p) c")
            return dram[bass.ds(t.base + t.shift, 1)].rearrange("a p c -> (a p) c")

        block = stack.enter_context(nc.Block())

        @block.sync
        def _(sp):
            sp.dma_start(cst[:], const).then_inc(ld_cst, 16)
            for n, w in enumerate((wq, wk, wv, wo)):
                sp.dma_start(watt[:, n], w).then_inc(ld_att, 16)

            def load_x(t):
                if t.later:
                    sp.wait_ge(xq_ready, at(t, xq_ready, 0))
                sp.dma_start(xin[:], rows(x, t)).then_inc(xin_ld, 16)

            def load_residual(t):
                if t.later:
                    sp.wait_ge(resA_ready, at(t, resA_ready, 0))
                sp.dma_start(xres[:], rows(x_perm, t)).then_inc(xres_ld, 16)

            def load_context(t):
                if t.later:
                    sp.wait_ge(c_ready, at(t, c_ready, 0))
                sp.dma_start(ctxt[:], rows(ctx_in, t)).then_inc(ctxt_ld, 16)

            def load_context_v(t):
                if t.later:
                    sp.wait_ge(vB_ready, at(t, vB_ready, 0))
                for half in range(2):
                    sp.dma_start(ctxd[half * SEQ:(half + 1) * SEQ],
                                 rows(ctx_in, t).rearrange("(b k) d -> k b d", b=2)).then_inc(ctxd_ld, 16)

            def store(t):
                sp.wait_ge(y_ready, at(t, y_ready, 1))
                sp.dma_start(rows(out, t), y[:]).then_inc(y_out, 16)

            load_x(Tile(0))
            load_residual(Tile(0))
            load_context(Tile(0))
            load_context_v(Tile(0))
            for kc in range(KC):
                view = w13[:, kc, 0:NE * 2 * P].rearrange("p (b m n) -> p b m n", b=NE // 2, m=2)
                for m, w in enumerate((w1, w3)):
                    sp.dma_start(view[:, :, m], w[kc].rearrange("p (b n) -> p b n", b=NE // 2)).then_inc(ld_ffn, 16)
                for m, w in enumerate((ws1, ws3)):
                    first = (2 * NE + m) * P
                    sp.dma_start(w13[:, kc, first:first + P], w[kc]).then_inc(ld_ffn, 16)
            sp.dma_start(w13[:, :, (2 * NE + 2) * P:], gate).then_inc(ld_ffn, 16)
            sp.dma_start(w2f[:, 0:NE], w2).then_inc(ld_ffn, 16)
            sp.dma_start(w2f[:, NE], ws2).then_inc(ld_ffn, 16)
            def turn(t0, t1, t2, t3, t4, t5):
                if t0 and t0.later:
                    load_x(t0)
                if t5:
                    store(t5)
                if t1 and t1.later:
                    load_context(t1)
                if t1 and t1.later:
                    load_residual(t1)
                if t1 and t1.later:
                    load_context_v(t1)

            run(sp, turn)
            sp.wait_ge(y_out, 16 * ntiles)

        FFN_LOADS = 16 * (4 * KC + 3)

        @block.vector
        def _(dve):
            V = nc.vector
            V.memset(neghalf[:], -0.5)
            V.memset(mpA[:], 0.0)
            V.memset(mpB[:], 0.0)
            V.memset(vA[:], 0.0)
            V.memset(c_parts[:], 0.0)
            V.memset(vB[:], 0.0).then_inc(set_up, 1)
            dve.wait_ge(set_up, 1)
            V.memset(vA[0:SEQ, :, :, 0, SD:SD + 1], 1.0)
            V.memset(vA[SEQ:P, :, :, 1, SD:SD + 1], 1.0)
            V.memset(vB[0:SEQ, :, :, 0, XD:XD + 1], 1.0)
            V.memset(vB[SEQ:P, :, :, 1, XD:XD + 1], 1.0).then_inc(set_up, 1)
            dve.wait_ge(ld_att, 64)
            V.tensor_reduce(wabs[:], watt[:].rearrange("p w k n -> p w (k n)"), axis=AX.X, op=ALU.add,
                            apply_absolute_value=True).then_inc(wabs_ready, 1)
            dve.wait_ge(wsum_ready, 1)
            links = 0

            def wlink(ins):
                nonlocal links
                links += 1
                ins.then_inc(wchain, 1)
                dve.wait_ge(wchain, links)

            wlink(V.tensor_scalar(wscale[:], wsum[:], 1.0 / (HID * HID), EPS, ALU.mult, ALU.add))
            wlink(V.reciprocal(winv[:], wscale[:]))
            dest = (wqk[:, :, 0:HID], wqk[:, :, HID:2 * HID], wv_t[:], wo_t[:])
            for k in range(4):
                wlink(V.tensor_scalar(wround[:], watt[:, k].rearrange("p k n -> p (k n)"), winv[:, k:k + 1], MAGIC,
                                      ALU.mult, ALU.add))
                wlink(V.tensor_scalar(wround[:], wround[:], MAGIC, 1.0, ALU.subtract, ALU.min))
                wlink(V.tensor_scalar(dest[k], wround[:].rearrange("p (k n) -> p k n", k=KC), -1.0, None, ALU.max))
            src = wqk[:].rearrange("p k (h two d) -> p (k h) two d", two=2, d=SD // 2)
            rot = wqk_rot[:].rearrange("p k (h two d) -> p (k h) two d", two=2, d=SD // 2)
            V.tensor_copy(rot[:, :, 0], src[:, :, 1])
            V.tensor_copy(rot[:, :, 1], src[:, :, 0])
            wlink(V.tensor_tensor(score_c[:], wscale[:, 0:1], wscale[:, 1:2], ALU.mult))
            wlink(V.tensor_scalar(score_c[:], score_c[:], 1.0 / (QB * QB * SD ** 0.5), None, ALU.mult))
            wlink(V.tensor_scalar(v_c[:], wscale[:, 2:3], 1.0 / QB, None, ALU.mult))
            V.tensor_scalar(o_c[:], wscale[:, 3:4], 1.0 / QB, None, ALU.mult).then_inc(watt_ready, 1)

            def statistics(t, st, res, res_ready, bn, var_ready):
                dve.wait_ge(res_ready, at(t, res_ready, 1))
                V.bn_stats(st[:, 0:6], res[:]).then_inc(bn, 1)
                dve.wait_ge(bn, at(t, bn, 1))
                settle(dve)
                V.bn_aggr(st[:, 6:8], st[:, 0:6]).then_inc(var_ready, 1)

            def quantise(t):
                link = chain(dve, t, quant)
                dve.wait_ge(xin_ld, at(t, xin_ld, 16))
                link(V.tensor_reduce(ga[:, 0:1], xin[:], axis=AX.X, op=ALU.max, apply_absolute_value=True))
                if t.later:
                    dve.wait_ge(gall_ready, at(t, gall_ready, 0))
                V.tensor_scalar(ga[:, 1:2], ga[:, 0:1], EPS, None, ALU.add).then_inc(g_ready, 1)
                link(V.tensor_scalar(ga[:, 2:3], ga[:, 0:1], EPS, 1.0 / QB, ALU.add, ALU.mult))
                link(V.reciprocal(ga[:, 2:3], ga[:, 2:3]))
                link(V.tensor_scalar(rnd[:], xin[:], ga[:, 2:3], MAGIC, ALU.mult, ALU.add))
                if t.later:
                    dve.wait_ge(xqT_ps, at(t, xqT_ps, 0))
                V.tensor_scalar(xq[:], rnd[:], MAGIC, None, ALU.subtract).then_inc(xq_ready, 1)

            def token_scales(t):
                link = chain(dve, t, scales)
                dve.wait_ge(gall_ready, at(t, gall_ready, 1))
                if t.later:
                    dve.wait_ge(probsA_ready, at(t, probsA_ready, 0))
                    dve.wait_ge(v_ps, at(t, v_ps, 0))
                V.tensor_scalar(ga[:, 5:6], gall[:], gall[:, 0:1], score_c[:, 0:1], ALU.mult, ALU.mult)
                link(V.reciprocal(ga[:, 3:4], gall[:]))
                V.tensor_scalar(ga[:, 6:7], ga[:, 1:2], v_c[:, 0:1], None, ALU.mult)
                link(V.tensor_tensor(ga[:, 4:5], ga[:, 1:2], ga[:, 3:4], ALU.mult))

            def rope_parts(t):
                if t.later:
                    dve.wait_ge(rope_sum, at(t, rope_sum, 0))
                for k, (dst, table) in enumerate(((rope_c, cos), (rope_s, sin))):
                    dve.wait_ge(qk_ps, at(t, qk_ps, k + 1))
                    V.scalar_tensor_tensor(out=heads(dst[:], SD), in0=heads(PA[k][:], SD), scalar=ga[:, 4:5],
                                           in1=table.rearrange("p (o d) -> p o d", o=1).broadcast_to([P, 2 * SH, SD]),
                                           op0=ALU.mult, op1=ALU.mult).then_inc(rope_ready, 1)

            def q_low(t):
                dve.wait_ge(qk_hi, at(t, qk_hi, 1))
                V.tensor_tensor(qk_parts[:, 0:SP_, LEFT_LO], twice(rope[:, 0:HID], SP_), qk_parts[:, 0:SP_, LEFT_HI],
                                ALU.subtract).then_inc(q_lo, 1)

            def v_heads(t):
                dve.wait_ge(v_ps, at(t, v_ps, 1))
                if t.later:
                    dve.wait_ge(v_odd, at(t, v_odd, 0))
                V.tensor_copy(gvd[:], PA[1][:, 0:2]).then_inc(gvd_ready, 1)
                dve.wait_ge(gvd_ready, at(t, gvd_ready, 1))
                if t.later:
                    dve.wait_ge(oA_ps, at(t, oA_ps, 0))
                for b in range(2):
                    last = V.tensor_scalar(vA[0:SEQ, b, :, 0, 0:SD], heads(PA[0][0:SEQ, b * P:(b + 1) * P], SD),
                                           gvd[0:SEQ, b:b + 1], None, ALU.mult)
                last.then_inc(v_even, 1)

            def mask_k(t):
                dve.wait_ge(ks_ps, at(t, ks_ps, 1))
                if t.later:
                    dve.wait_ge(eA_ps, at(t, eA_ps, 0))
                V.tensor_scalar(ks[:, :, :, 0].rearrange("p h b t -> p (h b) t"), heads(PA[1][:].bitcast(F16), SEQ),
                                cst[:, C_MASKA:C_MASKA + 1], None, ALU.mult).then_inc(ks_even, 1)

            def maxima_a(t):
                for k in range(2):
                    dve.wait_ge(sA_ps, at(t, sA_ps, k + 1))
                    V.tensor_reduce(mA[:, k * 8:k * 8 + 8], heads(PA[k][:], SEQ), axis=AX.X,
                                    op=ALU.max).then_inc(mA_done, 1)
                dve.wait_ge(mA_done, at(t, mA_done, 2))
                if t.later:
                    dve.wait_ge(mTA_ps, at(t, mTA_ps, 0))
                V.tensor_copy(mpA[:, 0:SH], mA[:]).then_inc(mhA_ready, 1)
                dve.wait_ge(mhA_ready, at(t, mhA_ready, 1))
                V.tensor_tensor(mpA[:, SH:2 * SH], mA[:], mpA[:, 0:SH], ALU.subtract).then_inc(mpA_ready, 1)

            def normalise_a(t):
                dve.wait_ge(oA_ps, at(t, oA_ps, 1))
                o = heads(PA[0][:, 0:SH * (SD + 1)], SD + 1)
                V.reciprocal(rsA[:].rearrange("p (h o) -> p h o", o=1), o[:, :, SD:SD + 1]).then_inc(rsA_ready, 1)
                dve.wait_ge(rsA_ready, at(t, rsA_ready, 1))
                V.tensor_tensor(heads(att[:], SD), o[:, :, 0:SD], each(rsA[:], SH, SD), ALU.mult).then_inc(att_ready, 1)
                dve.wait_ge(att_ready, at(t, att_ready, 1))
                link = chain(dve, t, quant2)
                link(V.tensor_reduce(ga[:, 8:9], att[:], axis=AX.X, op=ALU.max, apply_absolute_value=True))
                link(V.tensor_scalar(ga[:, 9:10], ga[:, 8:9], EPS, 1.0 / QB, ALU.add, ALU.mult))
                link(V.reciprocal(ga[:, 9:10], ga[:, 9:10]))
                V.tensor_scalar(ga[:, 10:11], ga[:, 8:9], EPS, o_c[:, 0:1], ALU.add, ALU.mult)
                link(V.tensor_scalar(rnd2[:], att[:], ga[:, 9:10], MAGIC, ALU.mult, ALU.add))
                V.tensor_scalar(xq2[:], rnd2[:], MAGIC, None, ALU.subtract).then_inc(xq2_ready, 1)

            def residual_a(t):
                dve.wait_ge(wo_ps, at(t, wo_ps, 1))
                dve.wait_ge(xres_ld, at(t, xres_ld, 16))
                if t.later:
                    dve.wait_ge(x1_ready, at(t, x1_ready, 0))
                    dve.wait_ge(x1_hi, at(t, x1_hi, 0))
                V.scalar_tensor_tensor(out=resA[:], in0=TR[:, 0:HID], scalar=ga[:, 10:11], in1=xres[:],
                                       op0=ALU.mult, op1=ALU.add).then_inc(resA_ready, 1)
                statistics(t, stA, resA, resA_ready, bnA, varA_ready)

            def context_max(t):
                dve.wait_ge(ctxt_ld, at(t, ctxt_ld, 16))
                if t.later:
                    dve.wait_ge(call_ready, at(t, call_ready, 0))
                V.tensor_reduce(gb[:, 0:1], ctxt[:], axis=AX.X, op=ALU.max,
                                apply_absolute_value=True).then_inc(cmax_ready, 1)

            def context_parts(t):
                link = chain(dve, t, cscale)
                dve.wait_ge(call_ready, at(t, call_ready, 1))
                if t.later:
                    dve.wait_ge(probsB_ready, at(t, probsB_ready, 0))
                    dve.wait_ge(cs_ps, at(t, cs_ps, 0))
                link(V.tensor_scalar(gb[:, 1:2], call[:], TINY, None, ALU.max))
                V.tensor_scalar(gb[:, 3:4], gb[:, 1:2], XD ** -0.5, None, ALU.mult)
                link(V.reciprocal(gb[:, 2:3], gb[:, 1:2]))
                link(V.tensor_scalar(cnorm[:], ctxt[:], gb[:, 2:3], None, ALU.mult))
                parts = c_parts[:].rearrange("p (g w) -> p g w", w=P + XD)[:, :, 0:P].rearrange(
                    "p g (a d) -> p g a d", a=4)[:, :, :, 0:XD]
                source = cnorm[:].rearrange("p (g o d) -> p g o d", o=1, d=XD).broadcast_to([P, 8, 2, XD])
                V.tensor_copy(parts[:, :, RIGHT_HI], source).then_inc(c_high, 1)
                dve.wait_ge(c_high, at(t, c_high, 1))
                V.tensor_tensor(parts[:, :, RIGHT_LO], source, parts[:, :, RIGHT_HI], ALU.subtract).then_inc(c_ready, 1)

            def copy_context(t):
                dve.wait_ge(cs_ps, at(t, cs_ps, 1))
                if t.later:
                    dve.wait_ge(eB_ps, at(t, eB_ps, 0))
                V.tensor_copy(cs[:].rearrange("p c b h t -> p (c b h t)"), PB[1][:].bitcast(F16)).then_inc(cs_ready, 1)

            def maxima_b(t, ks_):
                for k in ks_:
                    dve.wait_ge(sB_ps, at(t, sB_ps, k + 1))
                    V.tensor_reduce(mB[:, k * 8:k * 8 + 8], heads(PB[k % 2][:], SEQ), axis=AX.X,
                                    op=ALU.max).then_inc(mB_done, 1)
                if 3 in ks_:
                    dve.wait_ge(mB_done, at(t, mB_done, 4))
                    if t.later:
                        dve.wait_ge(mTB_ps, at(t, mTB_ps, 0))
                    V.tensor_copy(mpB[:, 0:2 * XP], mB[:]).then_inc(mhB_ready, 1)
                    dve.wait_ge(mhB_ready, at(t, mhB_ready, 1))
                    V.tensor_tensor(mpB[:, 2 * XP:4 * XP], mB[:], mpB[:, 0:2 * XP], ALU.subtract).then_inc(mpB_ready, 1)

            def normalise_b(t):
                dve.wait_ge(oB_ps, at(t, oB_ps, 1))
                o = heads(PB[0][:, 0:2 * XP * (XD + 1)], XD + 1)
                V.reciprocal(rsB[:].rearrange("p (h o) -> p h o", o=1), o[:, :, XD:XD + 1]).then_inc(rsB_ready, 1)
                dve.wait_ge(rsB_ready, at(t, rsB_ready, 1))
                if t.later:
                    dve.wait_ge(resB_ready, at(t, resB_ready, 0))
                V.tensor_tensor(heads(attB[:], XD), o[:, :, 0:XD], each(rsB[:], 2 * XP, XD),
                                ALU.mult).then_inc(attB_ready, 1)

            def x_low(t):
                dve.wait_ge(xTh_ready, at(t, xTh_ready, 1))
                V.tensor_tensor(xTl[:], TR[:, 0:HID].rearrange("p (k t) -> p k t", k=KC), xTh[:].bitcast(F32),
                                ALU.subtract).then_inc(xTl_ready, 1)

            def top2(t):
                link = chain(dve, t, route)
                scores, top, key, ktop = rt[:, 0], rt[:, 1], rt[:, 2], rt[:, 3]
                rank = cst[:, C_RANK:C_RANK + NE]
                dve.wait_ge(gate_th, at(t, gate_th, 1))
                link(V.tensor_scalar(scores, tanh_g[:], 0.5, 0.5, ALU.mult, ALU.add))
                settle(dve)
                link(V.max(top, scores))
                link(V.scalar_tensor_tensor(out=key, in0=scores, scalar=top[:, 1:2], in1=rank,
                                            op0=ALU.is_equal, op1=ALU.mult))
                link(V.scalar_tensor_tensor(out=key, in0=scores, scalar=top[:, 1:2], in1=key,
                                            op0=ALU.is_gt, op1=ALU.add))
                settle(dve)
                link(V.max(ktop, key))
                if t.later:
                    dve.wait_ge(th_ready, at(t, th_ready, 0))
                V.scalar_tensor_tensor(out=gate_s[:, 0], in0=key, scalar=ktop[:, 1:2], in1=scores,
                                       op0=ALU.is_ge, op1=ALU.mult).then_inc(s_ready, 1)
                dve.wait_ge(s_ready, at(t, s_ready, 1))
                V.tensor_scalar(gate_s[:, 1], gate_s[:, 0], 0.5, None, ALU.mult)
                V.tensor_tensor(gate_s[:, 2], gate_s[:, 0], gate_s[:, 0], ALU.mult).then_inc(sh_ready, 1)

            def gated(t, n):
                w, k = width(n), n % 2
                dve.wait_ge(th_ready, at(t, th_ready, n + 1))
                V.scalar_tensor_tensor(out=ug[:, k, 0:w], in0=th[:, k, 0:w], scalar=1.0, in1=UP[k][:, 0:w],
                                       op0=ALU.add, op1=ALU.mult).then_inc(u_ready, 1)
                dve.wait_ge(u_ready, at(t, u_ready, n + 1))
                if t.later or n >= 2:
                    dve.wait_ge(hT_ps, at(t, hT_ps, max(n - 1, 0)))
                if n == 0:
                    V.tensor_tensor(hh[:, k, 0:w], UP[k][:, w:2 * w], ug[:, k, 0:w], ALU.mult).then_inc(h_ready, 1)
                else:
                    if n == 1:
                        dve.wait_ge(sh_ready, at(t, sh_ready, 1))
                    for e in range(2):
                        ex = 2 * (n - 1) + e
                        last = V.scalar_tensor_tensor(out=hh[:, k, e * P:(e + 1) * P], in0=UP[k][:, w + e * P:w + (e + 1) * P],
                                                      scalar=gate_s[:, 2, ex:ex + 1], in1=ug[:, k, e * P:(e + 1) * P],
                                                      op0=ALU.mult, op1=ALU.mult)
                    last.then_inc(h_ready, 1)

            def h_low(t, n):
                w, k = width(n), n % 2
                dve.wait_ge(hTh_ready, at(t, hTh_ready, n + 1))
                V.tensor_tensor(hTl[:, k, 0:w], TR[:, 0:w], hTh[:, k, 0:w].bitcast(F32),
                                ALU.subtract).then_inc(hTl_ready, 1)

            def residual_c(t):
                dve.wait_ge(down_ps, at(t, down_ps, NB))
                if t.later:
                    dve.wait_ge(y_ready, at(t, y_ready, 0))
                V.scalar_tensor_tensor(out=resC[:], in0=ACC[:, 0:HID], scalar=0.5, in1=x2[:],
                                       op0=ALU.mult, op1=ALU.add).then_inc(resC_ready, 1)
                statistics(t, stC, resC, resC_ready, bnC, varC_ready)

            def turn(t0, t1, t2, t3, t4, t5):
                if t2:
                    context_parts(t2)
                if t4:
                    gated(t4, 4)
                    h_low(t4, 3)
                if t3:
                    normalise_b(t3)
                if t4:
                    h_low(t4, 4)
                if t3:
                    statistics(t3, stB, resB, resB_ready, bnB, varB_ready)
                if t1:
                    v_heads(t1)
                    q_low(t1)
                if t4:
                    residual_c(t4)
                if t2:
                    residual_a(t2)
                if t1:
                    mask_k(t1)
                if t3:
                    x_low(t3)
                if t2:
                    copy_context(t2)
                if t0:
                    quantise(t0)
                if t1:
                    maxima_a(t1)
                if t3:
                    gated(t3, 0)
                if t1:
                    context_max(t1)
                if t3:
                    top2(t3)
                if t2:
                    maxima_b(t2, (0, 1))
                if t3:
                    h_low(t3, 0)
                    gated(t3, 1)
                if t2:
                    maxima_b(t2, (2, 3))
                if t3:
                    gated(t3, 2)
                    h_low(t3, 1)
                if t0:
                    token_scales(t0)
                if t3:
                    gated(t3, 3)
                if t1:
                    normalise_a(t1)
                if t3:
                    h_low(t3, 2)
                if t0:
                    rope_parts(t0)

            dve.wait_ge(ld_cst, 16)
            dve.wait_ge(cst16, 1)
            run(dve, turn)

        @block.scalar
        def _(act):
            S = nc.scalar
            act.wait_ge(ld_cst, 16)
            S.copy(ident16[:], ident)
            S.copy(identb[:], ident)
            S.copy(selA[:], cst[:, C_SELA:C_SELB])
            S.copy(selB[:], cst[:, C_SELB:C_DUP]).then_inc(cst16, 1)

            def ffn_high_parts():
                act.wait_ge(ld_ffn, FFN_LOADS)
                S.copy(w13h[:], w13[:])
                S.copy(w2h[:], w2f[:]).then_inc(ffn_hi, 1)

            def normalise(dst, res, st):
                return S.activation(dst, res, ACT.Identity, scale=st[:, 8:9], bias=st[:, 10:11])

            def copy_xqT(t):
                act.wait_ge(xqT_ps, at(t, xqT_ps, 1))
                if t.later:
                    act.wait_ge(v_ps, at(t, v_ps, 0))
                S.copy(xqT[:], PA[0][:, 0:P].bitcast(BF16).rearrange("p (k t) -> p k t", k=KC)).then_inc(xqT_ready, 1)

            def qk_high(t):
                act.wait_ge(rope_sum, at(t, rope_sum, 1))
                if t.later:
                    act.wait_ge(ks_ps, at(t, ks_ps, 0))
                S.copy(qk_parts[:, 0:SP_, LEFT_HI], twice(rope[:, 0:HID], SP_)).then_inc(qk_hi, 1)
                S.copy(qk_parts[:, SP_:2 * SP_, RIGHT_HI], twice(rope[:, HID:2 * HID], SP_)).then_inc(qk_hi, 1)

            def v_heads(t):
                act.wait_ge(v_even, at(t, v_even, 1))
                if t.later:
                    act.wait_ge(oA_ps, at(t, oA_ps, 0))
                for b in range(2):
                    last = S.activation(vA[SEQ:P, b, :, 1, 0:SD], heads(PA[0][SEQ:P, b * P:(b + 1) * P], SD),
                                        ACT.Copy, scale=gvd[SEQ:P, b:b + 1])
                last.then_inc(v_odd, 1)

            def copy_stacks_a(t):
                act.wait_ge(qs_ps, at(t, qs_ps, 1))
                if t.later:
                    act.wait_ge(eA_ps, at(t, eA_ps, 0))
                S.copy(qs[:], heads(PA[0][:].bitcast(F16), P)).then_inc(qs_ready, 1)
                act.wait_ge(ks_even, at(t, ks_even, 1))
                S.activation(ks[:, :, :, 1].rearrange("p h b t -> p (h b) t"), heads(PA[1][:].bitcast(F16), SEQ), ACT.Copy,
                             scale=cst[:, C_MASKA + 1:C_MASKA + 2]).then_inc(ks_odd, 1)

            def copy_maxima_a(t):
                act.wait_ge(mTA_ps, at(t, mTA_ps, 1))
                if t.later:
                    act.wait_ge(eA_ps, at(t, eA_ps, 0))
                S.copy(mTA[:], PA[0][:, 0:P // 2].bitcast(BF16)).then_inc(mTA_ready, 1)

            def exp_a(t):
                if t.later:
                    act.wait_ge(oA_ps, at(t, oA_ps, 0))
                for k in range(2):
                    act.wait_ge(eA_ps, at(t, eA_ps, k + 1))
                    S.activation(probsA[:, 4 * k:4 * k + 4].rearrange("p h t -> p (h t)"), PA[k][:], ACT.Exp,
                                 scale=ga[:, 5:6]).then_inc(probsA_ready, 1)

            def copy_xq2T(t):
                act.wait_ge(xq2T_ps, at(t, xq2T_ps, 1))
                if t.later:
                    act.wait_ge(wo_ps, at(t, wo_ps, 0))
                S.copy(xq2T[:], TR[:, 0:P].bitcast(BF16).rearrange("p (k t) -> p k t", k=KC)).then_inc(xq2T_ready, 1)

            def norm_a(t):
                act.wait_ge(rstdA_ready, at(t, rstdA_ready, 1))
                if t.later:
                    act.wait_ge(x1_lo, at(t, x1_lo, 0))
                    act.wait_ge(resB_ready, at(t, resB_ready, 0))
                    act.wait_ge(xs_ps, at(t, xs_ps, 0))
                normalise(x1[:], resA[:], stA).then_inc(x1_ready, 1)
                normalise(x_parts[:, :, LEFT_HI], twice(resA[:], 8), stA).then_inc(x1_hi, 1)

            def copy_stacks_b(t):
                act.wait_ge(xs_ps, at(t, xs_ps, 1))
                if t.later:
                    act.wait_ge(eB_ps, at(t, eB_ps, 0))
                S.copy(xs[:], heads(PB[0][:].bitcast(F16), P)).then_inc(xs_ready, 1)

            def copy_maxima_b(t):
                act.wait_ge(mTB_ps, at(t, mTB_ps, 1))
                if t.later:
                    act.wait_ge(eB_ps, at(t, eB_ps, 0))
                S.copy(mTB[:], PB[0][:, 0:P // 2].bitcast(BF16)).then_inc(mTB_ready, 1)

            def exp_b(t, banks):
                if t.later and 0 in banks:
                    act.wait_ge(oB_ps, at(t, oB_ps, 0))
                for k in banks:
                    act.wait_ge(eB_ps, at(t, eB_ps, k + 1))
                    S.activation(probsB[:, 4 * k:4 * k + 4].rearrange("p h t -> p (h t)"), PB[k % 2][:], ACT.Exp,
                                 scale=gb[:, 3:4]).then_inc(probsB_ready, 1)

            def x_high(t):
                act.wait_ge(xT_ps, at(t, xT_ps, 1))
                if t.later:
                    act.wait_ge(up_ps, at(t, up_ps, 0))
                S.copy(xTh[:], TR[:, 0:HID].rearrange("p (k t) -> p k t", k=KC)).then_inc(xTh_ready, 1)

            def norm_b(t):
                act.wait_ge(rstdB_ready, at(t, rstdB_ready, 1))
                if t.later:
                    act.wait_ge(xT_ps, at(t, xT_ps, 0))
                    act.wait_ge(resC_ready, at(t, resC_ready, 0))
                normalise(x2[:], resB[:], stB).then_inc(x2_ready, 1)

            def norm_c(t):
                act.wait_ge(rstdC_ready, at(t, rstdC_ready, 1))
                if t.later:
                    act.wait_ge(y_out, at(t, y_out, 0))
                normalise(y[:], resC[:], stC).then_inc(y_ready, 1)

            def gate_tanh(t):
                act.wait_ge(up_ps, at(t, up_ps, 1))
                if t.later:
                    act.wait_ge(s_ready, at(t, s_ready, 0))
                S.activation(tanh_g[:], UP[0][:, 2 * P:2 * P + NE], ACT.Tanh, scale=0.5).then_inc(gate_th, 1)

            def tanh_up(t, n):
                w, k = width(n), n % 2
                act.wait_ge(up_ps, at(t, up_ps, n + 1))
                if n == 1:
                    act.wait_ge(sh_ready, at(t, sh_ready, 1))
                if t.later or n >= 2:
                    act.wait_ge(u_ready, at(t, u_ready, max(n - 1, 0)))
                for e in range(w // P):
                    ex = 2 * (n - 1) + e
                    last = S.activation(th[:, k, e * P:(e + 1) * P], UP[k][:, e * P:(e + 1) * P], ACT.Tanh,
                                        scale=gate_s[:, 1, ex:ex + 1] if n else 0.5)
                last.then_inc(th_ready, 1)

            def h_high(t, n):
                w, k = width(n), n % 2
                act.wait_ge(hT_ps, at(t, hT_ps, n + 1))
                if t.later or n >= 2:
                    act.wait_ge(down_ps, at(t, down_ps, max(n - 1, 0)))
                S.copy(hTh[:, k, 0:w], TR[:, 0:w]).then_inc(hTh_ready, 1)

            def turn(t0, t1, t2, t3, t4, t5):
                if t5:
                    norm_c(t5)
                if t4:
                    h_high(t4, 4)
                if t1:
                    qk_high(t1)
                if t2:
                    copy_xq2T(t2)
                if t1:
                    v_heads(t1)
                if t3:
                    norm_b(t3)
                    x_high(t3)
                if t1:
                    copy_stacks_a(t1)
                if t2:
                    norm_a(t2)
                if t3:
                    gate_tanh(t3)
                    tanh_up(t3, 0)
                if t2:
                    copy_stacks_b(t2)
                if t3:
                    h_high(t3, 0)
                if t1:
                    copy_maxima_a(t1)
                if t3:
                    tanh_up(t3, 1)
                if t1:
                    exp_a(t1)
                if t3:
                    tanh_up(t3, 2)
                    h_high(t3, 1)
                if t2:
                    copy_maxima_b(t2)
                if t3:
                    tanh_up(t3, 3)
                if t2:
                    exp_b(t2, (0, 1))
                if t0:
                    copy_xqT(t0)
                if t3:
                    h_high(t3, 2)
                if t2:
                    exp_b(t2, (2, 3))
                if t3:
                    tanh_up(t3, 4)
                    h_high(t3, 3)

            run(act, turn, ffn_high_parts)

        @block.gpsimd
        def _(pool):
            G = nc.gpsimd
            pool.wait_ge(wabs_ready, 1)
            G.partition_all_reduce(wsum[:], wabs[:], P, RADD).then_inc(wsum_ready, 1)
            pool.wait_ge(wsum_ready, 1)
            pool.wait_ge(set_up, 2)

            def ffn_low_parts():
                pool.wait_ge(ffn_hi, 1)
                G.tensor_tensor(w13l[:], w13[:], w13h[:].bitcast(F32), ALU.subtract)
                G.tensor_tensor(w2l[:], w2f[:], w2h[:].bitcast(F32), ALU.subtract).then_inc(ffn_lo, 1)

            def rstd(t, var_ready, st, eps_added, powered, rstd_ready):
                pool.wait_ge(var_ready, at(t, var_ready, 1))
                settle(pool)
                G.tensor_scalar(st[:, 9:10], st[:, 6:7], -1.0, None, ALU.mult)
                G.tensor_scalar(st[:, 7:8], st[:, 7:8], EPS, None, ALU.add).then_inc(eps_added, 1)
                pool.wait_ge(eps_added, at(t, eps_added, 1))
                G.tensor_tensor(st[:, 8:9], st[:, 7:8], neghalf[:], ALU.pow).then_inc(powered, 1)
                pool.wait_ge(powered, at(t, powered, 1))
                G.tensor_tensor(st[:, 10:11], st[:, 9:10], st[:, 8:9], ALU.mult).then_inc(rstd_ready, 1)

            def largest_g(t):
                pool.wait_ge(g_ready, at(t, g_ready, 1))
                if t.later:
                    pool.wait_ge(scales, at(t, scales, 0))
                settle(pool)
                G.partition_all_reduce(gall[:], ga[:, 1:2], P, RMAX).then_inc(gall_ready, 1)
                pool.wait_ge(gall_ready, at(t, gall_ready, 1))

            def add_rope(t):
                pool.wait_ge(rope_ready, at(t, rope_ready, 2))
                if t.later:
                    pool.wait_ge(q_lo, at(t, q_lo, 0))
                G.tensor_tensor(rope[:], rope_c[:], rope_s[:], ALU.add).then_inc(rope_sum, 1)

            def k_low(t):
                pool.wait_ge(qk_hi, at(t, qk_hi, 2))
                G.tensor_tensor(qk_parts[:, SP_:2 * SP_, RIGHT_LO], twice(rope[:, HID:2 * HID], SP_),
                                qk_parts[:, SP_:2 * SP_, RIGHT_HI], ALU.subtract).then_inc(k_lo, 1)

            def largest_c(t):
                pool.wait_ge(cmax_ready, at(t, cmax_ready, 1))
                if t.later:
                    pool.wait_ge(c_ready, at(t, c_ready, 0))
                settle(pool)
                G.partition_all_reduce(call[:], gb[:, 0:1], P, RMAX).then_inc(call_ready, 1)
                pool.wait_ge(call_ready, at(t, call_ready, 1))

            def context_v(t):
                pool.wait_ge(ctxd_ld, at(t, ctxd_ld, 32))
                pool.wait_ge(x1_lo, at(t, x1_lo, 1))
                if t.later:
                    pool.wait_ge(oB_ps, at(t, oB_ps, 0))
                settle(pool)
                for h in range(2):
                    for b in range(2):
                        last = G.tensor_copy(vB[h * SEQ:(h + 1) * SEQ, b, :, h, 0:XD],
                                             ctxd[h * SEQ:(h + 1) * SEQ, b].rearrange(
                                                 "p (q two d) -> p q two d", two=2, d=XD)[:, :, h])
                last.then_inc(vB_ready, 1)
                pool.wait_ge(vB_ready, at(t, vB_ready, 1))

            def x1_low(t):
                pool.wait_ge(x1_hi, at(t, x1_hi, 1))
                G.tensor_tensor(x_parts[:, :, LEFT_LO], twice(x1[:], 8), x_parts[:, :, LEFT_HI],
                                ALU.subtract).then_inc(x1_lo, 1)

            def residual_b(t):
                pool.wait_ge(attB_ready, at(t, attB_ready, 1))
                if t.later:
                    pool.wait_ge(x2_ready, at(t, x2_ready, 0))
                G.tensor_tensor(resB[:], attB[:], x1[:], ALU.add).then_inc(resB_ready, 1)

            def turn(t0, t1, t2, t3, t4, t5):
                if t1:
                    add_rope(t1)
                if t3:
                    residual_b(t3)
                if t1:
                    k_low(t1)
                if t3:
                    rstd(t3, varB_ready, stB, epsB, powB, rstdB_ready)
                if t2:
                    rstd(t2, varA_ready, stA, epsA, powA, rstdA_ready)
                    x1_low(t2)
                    context_v(t2)
                if t1:
                    largest_c(t1)
                if t4:
                    rstd(t4, varC_ready, stC, epsC, powC, rstdC_ready)
                if t0:
                    largest_g(t0)

            run(pool, turn, ffn_low_parts)

        @block.tensor
        def _(pe):
            T = nc.tensor
            pe.wait_ge(cst16, 1)
            pe.wait_ge(set_up, 2)
            pe.wait_ge(watt_ready, 1)

            def transpose_xq(t):
                pe.wait_ge(xq_ready, at(t, xq_ready, 1))
                if t.later:
                    pe.wait_ge(att_ready, at(t, att_ready, 0))
                for k in range(KC):
                    last = T.transpose(PA[0][:, 0:P].bitcast(BF16)[:, k * P:(k + 1) * P], xq[:, k * P:(k + 1) * P], identb[:])
                last.then_inc(xqT_ps, 1)

            def project_qk(t):
                pe.wait_ge(xqT_ready, at(t, xqT_ready, 1))
                for n, w in enumerate((wqk, wqk_rot)):
                    for k in range(KC):
                        last = T.matmul(PA[n][:], xqT[:, k], w[:, k], start=(k == 0), stop=(k == KC - 1))
                    last.then_inc(qk_ps, 1)

            def project_v(t):
                pe.wait_ge(rope_ready, at(t, rope_ready, 2))
                for b in range(2):
                    for h in range(2):
                        for k in range(KC):
                            T.matmul(PA[0][h * SEQ:(h + 1) * SEQ, b * P:(b + 1) * P], xqT[:, k, b * SEQ:(b + 1) * SEQ],
                                     wv_t[:, k].rearrange("p (h two d) -> p h two d", two=2, d=SD)[:, :, h],
                                     start=(k == 0), stop=(k == KC - 1))
                pe.wait_ge(scales, at(t, scales, 2))
                for b in range(2):
                    last = T.matmul(PA[1][:, b:b + 1], dup[:, b * P:(b + 1) * P], ga[:, 6:7], start=True, stop=True)
                last.then_inc(v_ps, 1)

            def stack_a(t):
                pe.wait_ge(q_lo, at(t, q_lo, 1))
                pe.wait_ge(k_lo, at(t, k_lo, 1))
                pe.wait_ge(v_odd, at(t, v_odd, 1))
                for pair in range(SP_):
                    last = T.transpose(PA[1][:].bitcast(F16)[:, pair * P:(pair + 1) * P],
                                       qk_parts[:, SP_ + pair].rearrange("p a d -> p (a d)"), ident16[:])
                last.then_inc(ks_ps, 1)
                for pair in range(SP_):
                    last = T.transpose(PA[0][:].bitcast(F16)[:, pair * P:(pair + 1) * P],
                                       qk_parts[:, pair].rearrange("p a d -> p (a d)"), ident16[:])
                last.then_inc(qs_ps, 1)

            def scores_a(t):
                pe.wait_ge(qs_ready, at(t, qs_ready, 1))
                pe.wait_ge(ks_odd, at(t, ks_odd, 1))
                for pair in range(SP_):
                    for b in range(2):
                        first = pair % 4 * P
                        last = T.matmul(PA[pair // 4][b * SEQ:(b + 1) * SEQ, first:first + P],
                                        qs[:, pair, b * SEQ:(b + 1) * SEQ], ks[:, pair, b].rearrange("p h t -> p (h t)"),
                                        start=True, stop=True)
                    if pair % 4 == 3:
                        last.then_inc(sA_ps, 1)

            def transpose_maxima_a(t):
                pe.wait_ge(mpA_ready, at(t, mpA_ready, 1))
                T.transpose(PA[0][:, 0:P // 2].bitcast(BF16), mpA[:], identb[:]).then_inc(mTA_ps, 1)

            def exponents_a(t):
                pe.wait_ge(mTA_ready, at(t, mTA_ready, 1))
                for pair in range(SP_):
                    first = pair % 4 * P
                    T.matmul(PA[pair // 4][:, first:first + P], selA[:, pair * P:(pair + 1) * P], mTA[:],
                             start=True, stop=False)
                    for b in range(2):
                        last = T.matmul(PA[pair // 4][:, first + b * SEQ:first + (b + 1) * SEQ],
                                        ks[:, pair, b].rearrange("p h t -> p (h t)"), qs[:, pair, b * SEQ:(b + 1) * SEQ],
                                        start=False, stop=(b == 1))
                    if pair % 4 == 3:
                        last.then_inc(eA_ps, 1)

            def attend_a(t):
                pe.wait_ge(probsA_ready, at(t, probsA_ready, 2))
                for pair in range(SP_):
                    first = pair * 2 * (SD + 1)
                    for b in range(2):
                        last = T.matmul(PA[0][b * SEQ:(b + 1) * SEQ, first:first + 2 * (SD + 1)],
                                        probsA[:, pair, b * SEQ:(b + 1) * SEQ],
                                        vA[:, b, pair].rearrange("p h d -> p (h d)"), start=True, stop=True)
                last.then_inc(oA_ps, 1)

            def transpose_xq2(t, older):
                pe.wait_ge(xq2_ready, at(t, xq2_ready, 1))
                if older:
                    pe.wait_ge(hTl_ready, at(older, hTl_ready, NB))
                for k in range(KC):
                    last = T.transpose(TR[:, 0:P].bitcast(BF16)[:, k * P:(k + 1) * P], xq2[:, k * P:(k + 1) * P], identb[:])
                last.then_inc(xq2T_ps, 1)

            def project_out(t):
                pe.wait_ge(xq2T_ready, at(t, xq2T_ready, 1))
                for k in range(KC):
                    last = T.matmul(TR[:, 0:HID], xq2T[:, k], wo_t[:, k], start=(k == 0), stop=(k == KC - 1))
                last.then_inc(wo_ps, 1)

            def stack_context(t):
                pe.wait_ge(c_ready, at(t, c_ready, 1))
                if t.later:
                    pe.wait_ge(probsB_ready, at(t, probsB_ready, 0))
                dst = PB[1][:].bitcast(F16).rearrange("p (c b h t) -> p c b h t", c=2, b=2, h=4)
                for c in range(2):
                    for h in range(4):
                        first = 4 * c * (P + XD) + h * P
                        last = T.transpose(dst[:, c, :, h], c_parts[:, first:first + P], ident16[:])
                last.then_inc(cs_ps, 1)

            def stack_x1(t):
                pe.wait_ge(x1_lo, at(t, x1_lo, 1))
                if t.later:
                    pe.wait_ge(attB_ready, at(t, attB_ready, 0))
                for cg in range(8):
                    last = T.transpose(PB[0][:].bitcast(F16)[:, cg * P:(cg + 1) * P],
                                       x_parts[:, cg].rearrange("p a d -> p (a d)"), ident16[:])
                last.then_inc(xs_ps, 1)

            def scores_b(t, banks):
                if 0 in banks:
                    pe.wait_ge(xs_ready, at(t, xs_ready, 1))
                    pe.wait_ge(cs_ready, at(t, cs_ready, 1))
                for n in banks:
                    if n >= 2:
                        pe.wait_ge(mB_done, at(t, mB_done, n - 1))
                    for cg in (2 * n, 2 * n + 1):
                        first = cg % 2 * 4 * SEQ
                        for b in range(2):
                            last = T.matmul(PB[n % 2][b * SEQ:(b + 1) * SEQ, first:first + 4 * SEQ],
                                            xs[:, cg, b * SEQ:(b + 1) * SEQ], cs[:, cg // 4, b].rearrange("p h t -> p (h t)"),
                                            start=True, stop=True)
                    last.then_inc(sB_ps, 1)

            def transpose_maxima_b(t):
                pe.wait_ge(mpB_ready, at(t, mpB_ready, 1))
                T.transpose(PB[0][:, 0:P // 2].bitcast(BF16), mpB[:], identb[:]).then_inc(mTB_ps, 1)

            def exponents_b(t, banks):
                if 0 in banks:
                    pe.wait_ge(mTB_ready, at(t, mTB_ready, 1))
                for n in banks:
                    if n >= 2:
                        pe.wait_ge(probsB_ready, at(t, probsB_ready, n - 1))
                    for hp in range(4 * n, 4 * n + 4):
                        c, cg, half = hp // 8, hp // 2, hp % 2
                        first = hp % 4 * P
                        T.matmul(PB[n % 2][:, first:first + P], selB[:, hp * P:(hp + 1) * P], mTB[:], start=True, stop=False)
                        for b in range(2):
                            last = T.matmul(PB[n % 2][:, first + b * SEQ:first + (b + 1) * SEQ],
                                            cs[:, c, b, 2 * half:2 * half + 2].rearrange("p h t -> p (h t)"),
                                            xs[:, cg, b * SEQ:(b + 1) * SEQ], start=False, stop=(b == 1))
                    last.then_inc(eB_ps, 1)

            def attend_b(t):
                pe.wait_ge(probsB_ready, at(t, probsB_ready, 4))
                pe.wait_ge(vB_ready, at(t, vB_ready, 1))
                for hp in range(XP):
                    first = hp * 2 * (XD + 1)
                    for b in range(2):
                        last = T.matmul(PB[0][b * SEQ:(b + 1) * SEQ, first:first + 2 * (XD + 1)],
                                        probsB[:, hp, b * SEQ:(b + 1) * SEQ],
                                        vB[:, b, hp // 8 * 2 + hp % 2].rearrange("p h d -> p (h d)"),
                                        start=True, stop=True)
                last.then_inc(oB_ps, 1)

            parts = [(a, w, k) for a, w in ((xTh, 0), (xTl, 0), (xTh, 1)) for k in range(KC)]

            def transpose_x2(t, younger, older):
                pe.wait_ge(x2_ready, at(t, x2_ready, 1))
                if younger:
                    pe.wait_ge(resA_ready, at(younger, resA_ready, 1))
                elif older:
                    pe.wait_ge(hTl_ready, at(older, hTl_ready, NB))
                for k in range(KC):
                    last = T.transpose(TR[:, k * P:(k + 1) * P], x2[:, k * P:(k + 1) * P], ident)
                last.then_inc(xT_ps, 1)

            def up(t, m):
                first, w_ = (4 * (m - 1) * P, 4 * P) if m else (2 * NE * P, 2 * P + NE)
                if m == 0:
                    pe.wait_ge(ffn_lo, 1)
                    pe.wait_ge(xTl_ready, at(t, xTl_ready, 1))
                if t.later or m >= 2:
                    pe.wait_ge(h_ready, at(t, h_ready, max(m - 1, 0)))
                for n, (a, w, k) in enumerate(parts):
                    last = T.matmul(UP[m % 2][:, 0:w_], a[:, k], (w13h, w13l)[w][:, k, first:first + w_],
                                    start=(n == 0), stop=(n == 5))
                last.then_inc(up_ps, 1)

            def transpose_h(t, m):
                pe.wait_ge(h_ready, at(t, h_ready, m + 1))
                if m:
                    pe.wait_ge(hTl_ready, at(t, hTl_ready, m))
                for e in range(width(m) // P):
                    last = T.transpose(TR[:, e * P:(e + 1) * P], hh[:, m % 2, e * P:(e + 1) * P], ident)
                last.then_inc(hT_ps, 1)

            def down(t, m):
                pe.wait_ge(hTl_ready, at(t, hTl_ready, m + 1))
                if m == 0 and t.later:
                    pe.wait_ge(resC_ready, at(t, resC_ready, 0))
                for e in range(width(m) // P):
                    ex = 2 * (m - 1) + e if m else NE
                    for n, (a, w) in enumerate(((hTh, w2h), (hTl, w2h), (hTh, w2l))):
                        last = T.matmul(ACC[:, 0:HID], a[:, m % 2, e * P:(e + 1) * P], w[:, ex],
                                        start=(m == 0 and n == 0), stop=(m == NB - 1 and e == 1 and n == 2))
                last.then_inc(down_ps, 1)

            def turn(t0, t1, t2, t3, t4, t5):
                if t4:
                    transpose_h(t4, 3)
                if t3:
                    attend_b(t3)
                if t4:
                    down(t4, 2)
                    transpose_h(t4, 4)
                if t1:
                    project_v(t1)
                if t4:
                    down(t4, 3)
                if t2:
                    transpose_xq2(t2, t4)
                if t4:
                    down(t4, 4)
                if t2:
                    project_out(t2)
                if t1:
                    stack_a(t1)
                if t3:
                    transpose_x2(t3, t2, t4)
                if t2:
                    stack_context(t2)
                if t3:
                    up(t3, 0)
                if t1:
                    scores_a(t1)
                if t3:
                    up(t3, 1)
                if t1:
                    transpose_maxima_a(t1)
                if t2:
                    stack_x1(t2)
                if t3:
                    transpose_h(t3, 0)
                    up(t3, 2)
                if t2:
                    scores_b(t2, (0, 1))
                if t1:
                    exponents_a(t1)
                if t2:
                    scores_b(t2, (2, 3))
                if t3:
                    down(t3, 0)
                    transpose_h(t3, 1)
                    up(t3, 3)
                if t2:
                    transpose_maxima_b(t2)
                if t1:
                    attend_a(t1)
                if t2:
                    exponents_b(t2, (0, 1))
                if t3:
                    transpose_h(t3, 2)
                    up(t3, 4)
                if t0:
                    transpose_xq(t0)
                if t2:
                    exponents_b(t2, (2, 3))
                if t0:
                    project_qk(t0)
                if t3:
                    down(t3, 1)

            run(pe, turn)


def kernel(x, ctx_512, L0_attn_w_q, L0_attn_w_k, L0_attn_w_v, L0_attn_w_o, L0_ffn_gate_w, L0_ffn_w1, L0_ffn_w2,
           L0_ffn_w3, L0_ffn_ws1, L0_ffn_ws2, L0_ffn_ws3):
    import concourse.bacc as bacc
    from concourse.bass_utils import run_bass_kernel_spmd

    def chunks(w):
        w = np.asarray(w)
        return w.T.reshape(KC, P, w.shape[0]).transpose(1, 0, 2)

    def experts(w):
        w = np.asarray(w)
        return w.transpose(2, 0, 1).reshape(KC, P, -1)

    order = np.arange(HID).reshape(2, 4, 4, XD).transpose(0, 2, 1, 3).reshape(-1)
    arrays = {
        "x": np.asarray(x).reshape(-1, P, HID),
        "x_perm": np.asarray(x).reshape(-1, P, HID)[:, :, order],
        "ctx": np.asarray(ctx_512).reshape(-1, P, SEQ),
        "wq": chunks(L0_attn_w_q), "wk": chunks(L0_attn_w_k), "wv": chunks(L0_attn_w_v), "wo": chunks(np.asarray(L0_attn_w_o)[order]),
        "gate": chunks(np.asarray(L0_ffn_gate_w)[:, order]),
        "w1": experts(np.asarray(L0_ffn_w1)[:, :, order]),
        "w2": np.asarray(L0_ffn_w2)[:, order].transpose(2, 0, 1),
        "w3": experts(np.asarray(L0_ffn_w3)[:, :, order]),
        "ws1": experts(np.asarray(L0_ffn_ws1)[None][:, :, order]),
        "ws2": np.asarray(L0_ffn_ws2)[order].T,
        "ws3": experts(np.asarray(L0_ffn_ws3)[None][:, :, order]),
        "const": constants(),
    }
    arrays = {k: np.ascontiguousarray(v) for k, v in arrays.items()}
    nc = bacc.Bacc("TRN2", target_bir_lowering=False, num_devices=1)
    args = [nc.dram_tensor(k, v.shape, mybir.dt.from_np(v.dtype), kind="ExternalInput").ap() for k, v in arrays.items()]
    shape = arrays["x"].shape
    out = nc.dram_tensor("out", shape, F32, kind="ExternalOutput").ap()
    decoder_layer(nc, *args, out)
    r = run_bass_kernel_spmd(nc, [arrays], core_ids=[0])
    return r.results[0]["out"][:, :, np.argsort(order)].reshape(x.shape)
```

```python
from contextlib import ExitStack

import concourse.bass as bass
import numpy as np
from concourse import mybir

F32 = mybir.dt.float32
F32R = mybir.dt.float32r
F16 = mybir.dt.float16
BF16 = mybir.dt.bfloat16
ALU = mybir.AluOpType
ACT = mybir.ActivationFunctionType
AX = mybir.AxisListType
RMAX = bass.bass_isa.ReduceOp.max
RADD = bass.bass_isa.ReduceOp.add

P = 128
SEQ = 64
HID = 256
KC = HID // P
NE = 8
NB = 5
SH = 16
SD = HID // SH
SP_ = SH // 2
XP = 16
XD = 8
EPS = 1e-5
QB = 127.0
MAGIC = 12582912.0
TINY = 1e-30
STEPS = 3
LAG = 6

C_IDENT = 0
C_SELA = C_IDENT + P
C_SELB = C_SELA + SP_ * P
C_DUP = C_SELB + XP * P
C_COS = C_DUP + P
C_SIN = C_COS + SD
C_MASKA = C_SIN + SD
C_HALF = C_MASKA + 2
C_RANK = C_HALF + 2
C_END = C_RANK + NE


def constants():
    c = np.zeros((P, C_END), np.float32)
    c[:, C_IDENT:C_IDENT + P] = np.eye(P)
    col = np.arange(P)
    for pair in range(SP_):
        for part in range(2):
            c[part * SH + 2 * pair + col // SEQ, C_SELA + pair * P + col] = -1.0
    for pair in range(XP):
        for part in range(2):
            c[part * 2 * XP + 2 * pair + col // SEQ, C_SELB + pair * P + col] = -1.0
    for b in range(2):
        c[b * SEQ + col % SEQ, C_DUP + col] = 1.0
        c[b * SEQ:(b + 1) * SEQ, C_HALF + b] = 1.0
    inv_freq = (1.0 / np.float32(10000.0) ** (np.arange(0, SD, 2, dtype=np.float32) / np.float32(SD))).astype(np.float32)
    angle = np.outer(np.arange(P) % SEQ, inv_freq).astype(np.float32)
    c[:, C_COS:C_COS + SD] = np.cos(np.concatenate([angle, angle], 1))
    c[:, C_SIN:C_SIN + SD] = np.concatenate([-np.sin(angle), np.sin(angle)], 1)
    for h in range(2):
        c[:, C_MASKA + h] = (col % 32) // SD == h
    c[:, C_RANK:C_END] = (NE - np.arange(NE)) / (2.0 * NE)
    return c


class Tile:

    def __init__(self, base, shift=0):
        self.base, self.shift = base, shift
        self.later = not isinstance(base, int) or base > 0


def decoder_layer(nc, x, x_perm, ctx_in, wq, wk, wv, wo, gate, w1, w2, w3, ws1, ws2, ws3, const, out):
    ntiles = x.shape[0]
    with ExitStack() as stack:
        def sb(name, shape, dt=F32):
            return stack.enter_context(nc.sbuf_tensor(name, shape, dt))

        def bank(name):
            return stack.enter_context(nc.psum_tensor(name, [P, 512], F32))

        def sem(name):
            return stack.enter_context(nc.semaphore(name))

        rises = {}

        def sig(name, per=1):
            handle = sem(name)
            rises[name] = per
            return handle

        def at(t, handle, n):
            per = rises[handle.name]
            return t.base * per + (t.shift * per + n)

        cst = sb("cst", [P, C_END])
        ident = cst[:, C_IDENT:C_IDENT + P]
        ident16 = sb("ident16", [P, P], F16)
        identb = sb("identb", [P, P], BF16)
        selA = sb("selA", [P, SP_ * P], BF16)
        selB = sb("selB", [P, XP * P], BF16)
        dup = cst[:, C_DUP:C_DUP + P]
        cos = cst[:, C_COS:C_COS + SD]
        sin = cst[:, C_SIN:C_SIN + SD]
        watt = sb("watt", [P, 4, KC, HID])
        wabs = sb("wabs", [P, 4])
        wsum = sb("wsum", [P, 4])
        wscale = sb("wscale", [P, 4])
        winv = sb("winv", [P, 4])
        wround = sb("wround", [P, KC * HID])
        wqk = sb("wqk", [P, KC, 2 * HID], BF16)
        wqk_rot = sb("wqk_rot", [P, KC, 2 * HID], BF16)
        wv_t = sb("wv_t", [P, KC, HID], BF16)
        wo_t = sb("wo_t", [P, KC, HID], BF16)
        score_c = sb("score_c", [P, 1])
        v_c = sb("v_c", [P, 1])
        o_c = sb("o_c", [P, 1])
        COLS = (2 * NE + 2) * P + NE
        w13 = sb("w13", [P, KC, COLS])
        w13h = sb("w13h", [P, KC, COLS], F32R)
        w13l = sb("w13l", [P, KC, COLS], F32R)
        w2f = sb("w2f", [P, NE + 1, HID])
        w2h = sb("w2h", [P, NE + 1, HID], F32R)
        w2l = sb("w2l", [P, NE + 1, HID], F32R)
        neghalf = sb("neghalf", [P, 1])
        negone = sb("negone", [P, 1])
        xin = sb("xin", [P, HID])
        xres = sb("xres", [P, HID])
        ga = sb("ga", [P, 12])
        gall = sb("gall", [P, 1])
        gv = sb("gv", [P, 2])
        rnd = sb("rnd", [P, HID])
        xq = sb("xq", [P, HID], BF16)
        xqT = sb("xqT", [P, KC, P], BF16)
        rope_c = sb("rope_c", [P, 2 * HID])
        rope_s = sb("rope_s", [P, 2 * HID])
        rope = sb("rope", [P, 2 * HID])
        qk_parts = sb("qk_parts", [P, 2 * SP_, 4, 32], F16)
        gvd = sb("gvd", [P, 2])
        vA = sb("vA", [P, 2, SP_, 2, SD + 1])
        qs = sb("qs", [P, SP_, P], F16)
        ks = sb("ks", [P, SP_, 2, 2, SEQ], F16)
        mA = sb("mA", [P, SH])
        mpA = sb("mpA", [P, P], BF16)
        mTA = sb("mTA", [P, P], BF16)
        probsA = sb("probsA", [P, SP_, P])
        rsA = sb("rsA", [P, SH])
        att = sb("att", [P, HID])
        rnd2 = sb("rnd2", [P, HID])
        xq2 = sb("xq2", [P, HID], BF16)
        xq2T = sb("xq2T", [P, KC, P], BF16)
        resA = sb("resA", [P, HID])
        stA = sb("stA", [P, 12])
        x1 = sb("x1", [P, HID])
        ctxt = sb("ctxt", [P, SEQ])
        ctxd = sb("ctxd", [P, 2, SEQ])
        gb = sb("gb", [P, 8])
        call = sb("call", [P, 1])
        cnorm = sb("cnorm", [P, SEQ])
        c_parts = sb("c_parts", [P, 8 * (P + XD)], F16)
        x_parts = sb("x_parts", [P, 8, 4, 32], F16)
        vB = sb("vB", [P, 2, 4, 2, XD + 1])
        xs = sb("xs", [P, 8, P], F16)
        cs = sb("cs", [P, 2, 2, 4, SEQ], F16)
        mB = sb("mB", [P, 2 * XP])
        mpB = sb("mpB", [P, P], BF16)
        mTB = sb("mTB", [P, P], BF16)
        probsB = sb("probsB", [P, XP, P])
        rsB = sb("rsB", [P, 2 * XP])
        attB = sb("attB", [P, HID])
        resB = sb("resB", [P, HID])
        stB = sb("stB", [P, 12])
        x2 = sb("x2", [P, HID])
        xTh = sb("xTh", [P, KC, P], F32R)
        xTl = sb("xTl", [P, KC, P], F32R)
        tanh_g = sb("tanh_g", [P, NE])
        rt = sb("rt", [P, 8, NE])
        gate_s = sb("gate_s", [P, 3, NE])
        th = sb("th", [P, 2, 2 * P])
        ug = sb("ug", [P, 2, 2 * P])
        hh = sb("hh", [P, 2, 2 * P])
        hTh = sb("hTh", [P, 2, 2 * P], F32R)
        hTl = sb("hTl", [P, 2, 2 * P], F32R)
        resC = sb("resC", [P, HID])
        stC = sb("stC", [P, 12])
        y = sb("y", [P, HID])
        PA = [bank("PA0"), bank("PA1")]
        PB = [bank("PB0"), bank("PB1")]
        UP = [bank("UP0"), bank("UP1")]
        TR = bank("TR")
        ACC = bank("ACC")

        ld_att, ld_ffn, ld_cst = [sem(f"ld_att{k}") for k in range(4)], sem("ld_ffn"), sem("ld_cst")
        set_up = sem("set_up")
        cst16 = sem("cst16")
        wabs_ready, wsum_ready, wchain = sem("wabs_ready"), sem("wsum_ready"), sem("wchain")
        watt_ready, ffn_hi, ffn_lo = sem("watt_ready"), sem("ffn_hi"), sem("ffn_lo")
        w2_lo = sem("w2_lo")
        xin_ld, xres_ld = sig("xin_ld", 16), sig("xres_ld", 16)
        quant, g_ready, gall_ready, xq_ready = sig("quant", 3), sig("g_ready"), sig("gall_ready"), sig("xq_ready")
        ginv = sig("ginv")
        xqT_ps, xqT_ready = sig("xqT_ps"), sig("xqT_ready")
        rnd_ready, rnd2_ready = sig("rnd_ready"), sig("rnd2_ready")
        scales = sig("scales")
        qk_ps, rope_ready, rope_sum = sig("qk_ps", 2), sig("rope_ready", 2), sig("rope_sum")
        qk_hi, q_lo, k_lo = sig("qk_hi", 2), sig("q_lo"), sig("k_lo")
        v_ps, gvd_ready, v_ready = sig("v_ps"), sig("gvd_ready"), sig("v_ready")
        qs_ps, ks_ps, qs_ready = sig("qs_ps"), sig("ks_ps"), sig("qs_ready")
        ks_ready = sig("ks_ready")
        sA_ps, mA_done, mhA_ready, mpA_ready = sig("sA_ps", 2), sig("mA_done", 2), sig("mhA_ready"), sig("mpA_ready")
        mTA_ps, mTA_ready = sig("mTA_ps"), sig("mTA_ready")
        eA_ps, probsA_ready, oA_ps = sig("eA_ps", 2), sig("probsA_ready", 2), sig("oA_ps")
        rsA_ready, att_ready, quant2 = sig("rsA_ready"), sig("att_ready"), sig("quant2", 4)
        xq2_ready, xq2T_ps, xq2T_ready, wo_ps = sig("xq2_ready"), sig("xq2T_ps"), sig("xq2T_ready"), sig("wo_ps")
        resA_ready, bnA, varA_ready = sig("resA_ready"), sig("bnA"), sig("varA_ready")
        epsA, powA, rstdA_ready, x1_ready = sig("epsA"), sig("powA"), sig("rstdA_ready"), sig("x1_ready")
        ctxt_ld, ctxd_ld = sig("ctxt_ld", 16), sig("ctxd_ld", 32)
        cmax_ready, call_ready, cscale, c_ready = sig("cmax_ready"), sig("call_ready"), sig("cscale", 3), sig("c_ready")
        c_high = sig("c_high")
        vB_ready, x1_hi, x1_lo = sig("vB_ready"), sig("x1_hi"), sig("x1_lo")
        xs_ps, cs_ps, xs_ready, cs_ready = sig("xs_ps"), sig("cs_ps"), sig("xs_ready"), sig("cs_ready")
        sB_ps, mB_done, mhB_ready, mpB_ready = sig("sB_ps", 4), sig("mB_done", 4), sig("mhB_ready"), sig("mpB_ready")
        mTB_ps, mTB_ready = sig("mTB_ps"), sig("mTB_ready")
        eB_ps, probsB_ready, oB_ps = sig("eB_ps", 4), sig("probsB_ready", 4), sig("oB_ps")
        rsB_ready, attB_ready, resB_ready = sig("rsB_ready"), sig("attB_ready"), sig("resB_ready")
        bnB, varB_ready, epsB, powB, rstdB_ready, x2_ready = (sig("bnB"), sig("varB_ready"), sig("epsB"), sig("powB"), sig("rstdB_ready"),
                                                        sig("x2_ready"))
        xT_ps, xTh_ready, xTl_ready = sig("xT_ps"), sig("xTh_ready"), sig("xTl_ready")
        gate_th, route, s_ready, sh_ready = sig("gate_th"), sig("route", 5), sig("s_ready"), sig("sh_ready")
        up_ps, th_ready, u_ready = sig("up_ps", NB), sig("th_ready", NB), sig("u_ready", NB)
        h_ready, hT_ps = sig("h_ready", NB), sig("hT_ps", NB)
        hTh_ready, hTl_ready, down_ps = sig("hTh_ready", NB), sig("hTl_ready", NB), sig("down_ps", NB)
        resC_ready, bnC, varC_ready = sig("resC_ready"), sig("bnC"), sig("varC_ready")
        epsC, powC, rstdC_ready, y_ready, y_out = sig("epsC"), sig("powC"), sig("rstdC_ready"), sig("y_ready"), sig("y_out", 16)

        held = {}

        def settle(eng):
            if eng not in held:
                held[eng] = sem(f"held{len(held)}")
            eng.sem_inc(held[eng], 1)

        def chain(eng, t, handle):
            count = [0]

            def link(ins):
                count[0] += 1
                ins.then_inc(handle, 1)
                eng.wait_ge(handle, at(t, handle, count[0]))
            return link

        def twice(ap, n):
            return ap.rearrange("p (n o d) -> p n o d", n=n, o=1).broadcast_to([P, n, 2, 32])

        def each(ap, n, d):
            return ap.rearrange("p (n o) -> p n o", o=1).broadcast_to([P, n, d])

        def heads(ap, d):
            return ap.rearrange("p (h d) -> p h d", d=d)

        LEFT_HI, LEFT_LO = slice(0, 3, 2), slice(1, 4, 2)
        RIGHT_HI, RIGHT_LO = slice(0, 4, 3), slice(1, 3)

        def width(n):
            return P if n == 0 else 2 * P

        def run(eng, turn, after={}):
            def single(i):
                turn(*[Tile(i - k) if 0 <= i - k < ntiles else None for k in range(LAG + 1)])
            begin = LAG + 1 + (ntiles - LAG - 1) % STEPS
            for i in range(begin):
                single(i)
                if i in after:
                    after[i]()
            with eng.Fori(0, (ntiles - begin) // STEPS) as i:
                first = i * STEPS + begin
                for step in range(STEPS):
                    turn(*[Tile(first, step - k) for k in range(LAG + 1)])
            for i in range(ntiles, ntiles + LAG):
                single(i)

        def rows(dram, t):
            if isinstance(t.base, int):
                n = t.base + t.shift
                return dram[n:n + 1].rearrange("a p c -> (a p) c")
            return dram[bass.ds(t.base + t.shift, 1)].rearrange("a p c -> (a p) c")

        block = stack.enter_context(nc.Block())

        @block.sync
        def _(sp):
            for n, w in enumerate((wq, wk, wv, wo)):
                sp.dma_start(watt[:, n], w).then_inc(ld_att[n], 16)
            sp.dma_start(cst[:], const).then_inc(ld_cst, 16)

            def load_x(t):
                if t.later:
                    sp.wait_ge(rnd_ready, at(t, rnd_ready, 0))
                sp.dma_start(xin[:], rows(x, t)).then_inc(xin_ld, 16)

            def load_residual(t):
                if t.later:
                    sp.wait_ge(resA_ready, at(t, resA_ready, 0))
                sp.dma_start(xres[:], rows(x_perm, t)).then_inc(xres_ld, 16)

            def load_context(t):
                if t.later:
                    sp.wait_ge(c_ready, at(t, c_ready, 0))
                sp.dma_start(ctxt[:], rows(ctx_in, t)).then_inc(ctxt_ld, 16)

            def load_context_v(t):
                if t.later:
                    sp.wait_ge(vB_ready, at(t, vB_ready, 0))
                for half in range(2):
                    sp.dma_start(ctxd[half * SEQ:(half + 1) * SEQ],
                                 rows(ctx_in, t).rearrange("(b k) d -> k b d", b=2)).then_inc(ctxd_ld, 16)

            def store(t):
                sp.wait_ge(y_ready, at(t, y_ready, 1))
                sp.dma_start(rows(out, t), y[:]).then_inc(y_out, 16)

            load_x(Tile(0))
            load_residual(Tile(0))
            load_context(Tile(0))
            load_context_v(Tile(0))
            for kc in range(KC):
                view = w13[:, kc, 0:NE * 2 * P].rearrange("p (b m n) -> p b m n", b=NE // 2, m=2)
                for m, w in enumerate((w1, w3)):
                    sp.dma_start(view[:, :, m], w[kc].rearrange("p (b n) -> p b n", b=NE // 2)).then_inc(ld_ffn, 16)
                for m, w in enumerate((ws1, ws3)):
                    first = (2 * NE + m) * P
                    sp.dma_start(w13[:, kc, first:first + P], w[kc]).then_inc(ld_ffn, 16)
            sp.dma_start(w13[:, :, (2 * NE + 2) * P:], gate).then_inc(ld_ffn, 16)
            sp.dma_start(w2f[:, 0:NE], w2).then_inc(ld_ffn, 16)
            sp.dma_start(w2f[:, NE], ws2).then_inc(ld_ffn, 16)
            def turn(t0, t1, t2, t3, t4, t5, t6):
                if t0 and t0.later:
                    load_x(t0)
                if t2 and t2.later:
                    load_context(t2)
                if t6:
                    store(t6)
                if t2 and t2.later:
                    load_residual(t2)
                if t2 and t2.later:
                    load_context_v(t2)

            run(sp, turn)
            sp.wait_ge(y_out, 16 * ntiles)

        FFN_LOADS = 16 * (4 * KC + 3)

        @block.vector
        def _(dve):
            V = nc.vector
            V.memset(neghalf[:], -0.5)
            V.memset(negone[:], -1.0)
            V.memset(mpA[:], 0.0)
            V.memset(mpB[:], 0.0)
            V.memset(vA[:], 0.0)
            V.memset(c_parts[:], 0.0)
            V.memset(vB[:], 0.0).then_inc(set_up, 1)
            dve.wait_ge(set_up, 1)
            V.memset(vA[0:SEQ, :, :, 0, SD:SD + 1], 1.0)
            V.memset(vA[SEQ:P, :, :, 1, SD:SD + 1], 1.0)
            V.memset(vB[0:SEQ, :, :, 0, XD:XD + 1], 1.0)
            V.memset(vB[SEQ:P, :, :, 1, XD:XD + 1], 1.0).then_inc(set_up, 1)
            for k in range(4):
                dve.wait_ge(ld_att[k], 16)
                V.tensor_reduce(wabs[:, k:k + 1], watt[:, k].rearrange("p k n -> p (k n)"), axis=AX.X, op=ALU.add,
                                apply_absolute_value=True).then_inc(wabs_ready, 1)
            dve.wait_ge(wsum_ready, 1)
            links = 0

            def wlink(ins):
                nonlocal links
                links += 1
                ins.then_inc(wchain, 1)
                dve.wait_ge(wchain, links)

            wlink(V.tensor_scalar(wscale[:], wsum[:], 1.0 / (HID * HID), EPS, ALU.mult, ALU.add))
            wlink(V.reciprocal(winv[:], wscale[:]))
            dest = (wqk[:, :, 0:HID], wqk[:, :, HID:2 * HID], wv_t[:], wo_t[:])

            def ternary(k):
                wlink(V.tensor_scalar(wround[:], watt[:, k].rearrange("p k n -> p (k n)"), winv[:, k:k + 1], MAGIC,
                                      ALU.mult, ALU.add))
                wlink(V.tensor_scalar(wround[:], wround[:], MAGIC, 1.0, ALU.subtract, ALU.min))
                wlink(V.tensor_scalar(dest[k], wround[:].rearrange("p (k n) -> p k n", k=KC), -1.0, None, ALU.max))

            ternary(0)
            ternary(1)
            src = wqk[:].rearrange("p k (h two d) -> p (k h) two d", two=2, d=SD // 2)
            rot = wqk_rot[:].rearrange("p k (h two d) -> p (k h) two d", two=2, d=SD // 2)
            V.tensor_copy(rot[:, :, 0], src[:, :, 1])
            V.tensor_copy(rot[:, :, 1], src[:, :, 0])
            wlink(V.tensor_tensor(score_c[:], wscale[:, 0:1], wscale[:, 1:2], ALU.mult))
            wlink(V.tensor_scalar(score_c[:], score_c[:], 1.0 / (QB * QB * SD ** 0.5), None, ALU.mult))
            wlink(V.tensor_scalar(v_c[:], wscale[:, 2:3], 1.0 / QB, None, ALU.mult))
            V.tensor_scalar(o_c[:], wscale[:, 3:4], 1.0 / QB, None, ALU.mult).then_inc(watt_ready, 1)

            def ternary_v_o():
                ternary(2)
                ternary(3)
                dve.sem_inc(watt_ready, 1)

            def low_parts_w13():
                for kc in range(KC):
                    dve.wait_ge(ffn_hi, kc + 1)
                    V.tensor_tensor(w13l[:, kc], w13[:, kc], w13h[:, kc].bitcast(F32), ALU.subtract).then_inc(ffn_lo, 1)

            def sums(t, st, res, res_ready, bn):
                dve.wait_ge(res_ready, at(t, res_ready, 1))
                V.bn_stats(st[:, 0:6], res[:]).then_inc(bn, 1)

            def mean_variance(t, st, bn, var_ready):
                dve.wait_ge(bn, at(t, bn, 1))
                settle(dve)
                V.bn_aggr(st[:, 6:8], st[:, 0:6]).then_inc(var_ready, 1)

            def quantise(t):
                link = chain(dve, t, quant)
                dve.wait_ge(xin_ld, at(t, xin_ld, 16))
                link(V.tensor_reduce(ga[:, 0:1], xin[:], axis=AX.X, op=ALU.max, apply_absolute_value=True))
                if t.later:
                    dve.wait_ge(scales, at(t, scales, 0))
                V.tensor_scalar(ga[:, 1:2], ga[:, 0:1], EPS, None, ALU.add).then_inc(g_ready, 1)
                dve.wait_ge(g_ready, at(t, g_ready, 1))
                link(V.reciprocal(ga[:, 2:3], ga[:, 1:2]))
                link(V.tensor_scalar(ga[:, 2:3], ga[:, 2:3], QB, None, ALU.mult))
                if t.later:
                    dve.wait_ge(xq_ready, at(t, xq_ready, 0))
                V.tensor_scalar(rnd[:], xin[:], ga[:, 2:3], MAGIC, ALU.mult, ALU.add).then_inc(rnd_ready, 1)

            def rope_parts(t):
                dve.wait_ge(scales, at(t, scales, 1))
                if t.later:
                    dve.wait_ge(rope_sum, at(t, rope_sum, 0))
                for k, (dst, table) in enumerate(((rope_c, cos), (rope_s, sin))):
                    dve.wait_ge(qk_ps, at(t, qk_ps, k + 1))
                    V.scalar_tensor_tensor(out=heads(dst[:], SD), in0=heads(PA[k][:], SD), scalar=ga[:, 4:5],
                                           in1=table.rearrange("p (o d) -> p o d", o=1).broadcast_to([P, 2 * SH, SD]),
                                           op0=ALU.mult, op1=ALU.mult).then_inc(rope_ready, 1)

            def mask_k(t):
                dve.wait_ge(ks_ps, at(t, ks_ps, 1))
                if t.later:
                    dve.wait_ge(eA_ps, at(t, eA_ps, 0))
                for h in range(2):
                    last = V.tensor_scalar(ks[:, :, :, h].rearrange("p h b t -> p (h b) t"), heads(PA[1][:].bitcast(F16), SEQ),
                                           cst[:, C_MASKA + h:C_MASKA + h + 1], None, ALU.mult)
                last.then_inc(ks_ready, 1)

            def maxima_a(t):
                for k in range(2):
                    dve.wait_ge(sA_ps, at(t, sA_ps, k + 1))
                    V.tensor_reduce(mA[:, k * 8:k * 8 + 8], heads(PA[k][:], SEQ), axis=AX.X,
                                    op=ALU.max).then_inc(mA_done, 1)

            def high_maxima_a(t):
                dve.wait_ge(mA_done, at(t, mA_done, 2))
                if t.later:
                    dve.wait_ge(mTA_ps, at(t, mTA_ps, 0))
                V.tensor_copy(mpA[:, 0:SH], mA[:]).then_inc(mhA_ready, 1)

            def low_maxima_a(t):
                dve.wait_ge(mhA_ready, at(t, mhA_ready, 1))
                V.tensor_tensor(mpA[:, SH:2 * SH], mA[:], mpA[:, 0:SH], ALU.subtract).then_inc(mpA_ready, 1)

            def normalise_a(t):
                dve.wait_ge(oA_ps, at(t, oA_ps, 1))
                o = heads(PA[0][:, 0:SH * (SD + 1)], SD + 1)
                V.reciprocal(rsA[:].rearrange("p (h o) -> p h o", o=1), o[:, :, SD:SD + 1]).then_inc(rsA_ready, 1)
                dve.wait_ge(rsA_ready, at(t, rsA_ready, 1))
                V.tensor_tensor(heads(att[:], SD), o[:, :, 0:SD], each(rsA[:], SH, SD), ALU.mult).then_inc(att_ready, 1)

            def quantise_att(t):
                dve.wait_ge(att_ready, at(t, att_ready, 1))
                link = chain(dve, t, quant2)
                link(V.tensor_reduce(ga[:, 8:9], att[:], axis=AX.X, op=ALU.max, apply_absolute_value=True))
                link(V.tensor_scalar(ga[:, 9:10], ga[:, 8:9], EPS, None, ALU.add))
                link(V.reciprocal(ga[:, 9:10], ga[:, 9:10]))
                link(V.tensor_scalar(ga[:, 9:10], ga[:, 9:10], QB, None, ALU.mult))
                V.tensor_scalar(ga[:, 10:11], ga[:, 8:9], EPS, o_c[:, 0:1], ALU.add, ALU.mult)
                if t.later:
                    dve.wait_ge(xq2_ready, at(t, xq2_ready, 0))
                V.tensor_scalar(rnd2[:], att[:], ga[:, 9:10], MAGIC, ALU.mult, ALU.add).then_inc(rnd2_ready, 1)

            def residual_a(t):
                dve.wait_ge(wo_ps, at(t, wo_ps, 1))
                dve.wait_ge(xres_ld, at(t, xres_ld, 16))
                if t.later:
                    dve.wait_ge(x1_ready, at(t, x1_ready, 0))
                    dve.wait_ge(x1_hi, at(t, x1_hi, 0))
                V.scalar_tensor_tensor(out=resA[:], in0=TR[:, 0:HID], scalar=ga[:, 10:11], in1=xres[:],
                                       op0=ALU.mult, op1=ALU.add).then_inc(resA_ready, 1)

            def context_max(t):
                dve.wait_ge(ctxt_ld, at(t, ctxt_ld, 16))
                if t.later:
                    dve.wait_ge(call_ready, at(t, call_ready, 0))
                V.tensor_reduce(gb[:, 0:1], ctxt[:], axis=AX.X, op=ALU.max,
                                apply_absolute_value=True).then_inc(cmax_ready, 1)

            def copy_context(t):
                dve.wait_ge(cs_ps, at(t, cs_ps, 1))
                if t.later:
                    dve.wait_ge(eB_ps, at(t, eB_ps, 0))
                V.tensor_copy(cs[:].rearrange("p c b h t -> p (c b h t)"), PB[1][:].bitcast(F16)).then_inc(cs_ready, 1)

            def maxima_b(t, ks_):
                for k in ks_:
                    dve.wait_ge(sB_ps, at(t, sB_ps, k + 1))
                    V.tensor_reduce(mB[:, k * 8:k * 8 + 8], heads(PB[k % 2][:], SEQ), axis=AX.X,
                                    op=ALU.max).then_inc(mB_done, 1)

            def high_maxima_b(t):
                dve.wait_ge(mB_done, at(t, mB_done, 4))
                if t.later:
                    dve.wait_ge(mTB_ps, at(t, mTB_ps, 0))
                V.tensor_copy(mpB[:, 0:2 * XP], mB[:]).then_inc(mhB_ready, 1)

            def low_maxima_b(t):
                dve.wait_ge(mhB_ready, at(t, mhB_ready, 1))
                V.tensor_tensor(mpB[:, 2 * XP:4 * XP], mB[:], mpB[:, 0:2 * XP], ALU.subtract).then_inc(mpB_ready, 1)

            def normalise_b(t):
                dve.wait_ge(oB_ps, at(t, oB_ps, 1))
                o = heads(PB[0][:, 0:2 * XP * (XD + 1)], XD + 1)
                V.reciprocal(rsB[:].rearrange("p (h o) -> p h o", o=1), o[:, :, XD:XD + 1]).then_inc(rsB_ready, 1)
                dve.wait_ge(rsB_ready, at(t, rsB_ready, 1))
                if t.later:
                    dve.wait_ge(resB_ready, at(t, resB_ready, 0))
                V.tensor_tensor(heads(attB[:], XD), o[:, :, 0:XD], each(rsB[:], 2 * XP, XD),
                                ALU.mult).then_inc(attB_ready, 1)

            def x_low(t):
                dve.wait_ge(xTh_ready, at(t, xTh_ready, 1))
                V.tensor_tensor(xTl[:], TR[:, 0:HID].rearrange("p (k t) -> p k t", k=KC), xTh[:].bitcast(F32),
                                ALU.subtract).then_inc(xTl_ready, 1)

            def top2(t):
                link = chain(dve, t, route)
                scores, top, key, ktop = rt[:, 0], rt[:, 1], rt[:, 2], rt[:, 3]
                rank = cst[:, C_RANK:C_RANK + NE]
                dve.wait_ge(gate_th, at(t, gate_th, 1))
                link(V.tensor_scalar(scores, tanh_g[:], 0.5, 0.5, ALU.mult, ALU.add))
                settle(dve)
                link(V.max(top, scores))
                link(V.scalar_tensor_tensor(out=key, in0=scores, scalar=top[:, 1:2], in1=rank,
                                            op0=ALU.is_equal, op1=ALU.mult))
                link(V.scalar_tensor_tensor(out=key, in0=scores, scalar=top[:, 1:2], in1=key,
                                            op0=ALU.is_gt, op1=ALU.add))
                settle(dve)
                link(V.max(ktop, key))
                if t.later:
                    dve.wait_ge(th_ready, at(t, th_ready, 0))
                V.scalar_tensor_tensor(out=gate_s[:, 0], in0=key, scalar=ktop[:, 1:2], in1=scores,
                                       op0=ALU.is_ge, op1=ALU.mult).then_inc(s_ready, 1)
                dve.wait_ge(s_ready, at(t, s_ready, 1))
                V.tensor_scalar(gate_s[:, 1], gate_s[:, 0], 0.5, None, ALU.mult)
                V.tensor_tensor(gate_s[:, 2], gate_s[:, 0], gate_s[:, 0], ALU.mult).then_inc(sh_ready, 1)

            def gated(t, n):
                w, k = width(n), n % 2
                dve.wait_ge(th_ready, at(t, th_ready, n + 1))
                V.scalar_tensor_tensor(out=ug[:, k, 0:w], in0=th[:, k, 0:w], scalar=1.0, in1=UP[k][:, 0:w],
                                       op0=ALU.add, op1=ALU.mult).then_inc(u_ready, 1)

            def times_up(t, n):
                w, k = width(n), n % 2
                dve.wait_ge(u_ready, at(t, u_ready, n + 1))
                if t.later or n >= 2:
                    dve.wait_ge(hT_ps, at(t, hT_ps, max(n - 1, 0)))
                if n == 0:
                    V.tensor_tensor(hh[:, k, 0:w], UP[k][:, w:2 * w], ug[:, k, 0:w], ALU.mult).then_inc(h_ready, 1)
                else:
                    if n == 1:
                        dve.wait_ge(sh_ready, at(t, sh_ready, 1))
                    for e in range(2):
                        ex = 2 * (n - 1) + e
                        last = V.scalar_tensor_tensor(out=hh[:, k, e * P:(e + 1) * P], in0=UP[k][:, w + e * P:w + (e + 1) * P],
                                                      scalar=gate_s[:, 2, ex:ex + 1], in1=ug[:, k, e * P:(e + 1) * P],
                                                      op0=ALU.mult, op1=ALU.mult)
                    last.then_inc(h_ready, 1)

            def h_low(t, n):
                w, k = width(n), n % 2
                dve.wait_ge(hTh_ready, at(t, hTh_ready, n + 1))
                V.tensor_tensor(hTl[:, k, 0:w], TR[:, 0:w], hTh[:, k, 0:w].bitcast(F32),
                                ALU.subtract).then_inc(hTl_ready, 1)

            def residual_c(t):
                dve.wait_ge(down_ps, at(t, down_ps, NB))
                if t.later:
                    dve.wait_ge(y_ready, at(t, y_ready, 0))
                V.scalar_tensor_tensor(out=resC[:], in0=ACC[:, 0:HID], scalar=0.5, in1=x2[:],
                                       op0=ALU.mult, op1=ALU.add).then_inc(resC_ready, 1)

            def turn(t0, t1, t2, t3, t4, t5, t6):
                if t5:
                    h_low(t5, 3)
                    times_up(t5, 4)
                if t4:
                    normalise_b(t4)
                if t5:
                    h_low(t5, 4)
                if t4:
                    sums(t4, stB, resB, resB_ready, bnB)
                    mean_variance(t4, stB, bnB, varB_ready)
                if t3:
                    residual_a(t3)
                if t5:
                    residual_c(t5)
                if t3:
                    sums(t3, stA, resA, resA_ready, bnA)
                    mean_variance(t3, stA, bnA, varA_ready)
                if t2:
                    mask_k(t2)
                if t4:
                    x_low(t4)
                if t3:
                    copy_context(t3)
                if t2:
                    maxima_a(t2)
                    high_maxima_a(t2)
                if t5:
                    sums(t5, stC, resC, resC_ready, bnC)
                if t2:
                    low_maxima_a(t2)
                if t4:
                    gated(t4, 0)
                    times_up(t4, 0)
                    top2(t4)
                    h_low(t4, 0)
                if t2:
                    context_max(t2)
                if t3:
                    maxima_b(t3, (0, 1))
                if t4:
                    gated(t4, 1)
                if t5:
                    mean_variance(t5, stC, bnC, varC_ready)
                if t4:
                    times_up(t4, 1)
                if t3:
                    maxima_b(t3, (2, 3))
                    high_maxima_b(t3)
                    low_maxima_b(t3)
                if t4:
                    h_low(t4, 1)
                    gated(t4, 2)
                    times_up(t4, 2)
                if t2:
                    normalise_a(t2)
                if t4:
                    gated(t4, 3)
                if t1:
                    rope_parts(t1)
                if t4:
                    times_up(t4, 3)
                    h_low(t4, 2)
                if t2:
                    quantise_att(t2)
                if t0:
                    quantise(t0)
                if t4:
                    gated(t4, 4)

            dve.wait_ge(ld_cst, 16)
            run(dve, turn, {0: ternary_v_o, 1: low_parts_w13})

        @block.scalar
        def _(act):
            S = nc.scalar
            act.wait_ge(ld_cst, 16)
            S.copy(ident16[:], ident)
            S.copy(identb[:], ident)
            S.copy(selA[:], cst[:, C_SELA:C_SELB])
            S.copy(selB[:], cst[:, C_SELB:C_DUP]).then_inc(cst16, 1)

            def high_parts():
                act.wait_ge(ld_ffn, FFN_LOADS)
                for kc in range(KC):
                    S.copy(w13h[:, kc], w13[:, kc]).then_inc(ffn_hi, 1)
                S.copy(w2h[:], w2f[:]).then_inc(ffn_hi, 1)

            def normalise(dst, res, st):
                return S.activation(dst, res, ACT.Identity, scale=st[:, 8:9], bias=st[:, 10:11])

            def round_x(t):
                act.wait_ge(rnd_ready, at(t, rnd_ready, 1))
                if t.later:
                    act.wait_ge(xqT_ps, at(t, xqT_ps, 0))
                S.activation(xq[:], rnd[:], ACT.Copy, bias=-MAGIC).then_inc(xq_ready, 1)

            def round_att(t):
                act.wait_ge(rnd2_ready, at(t, rnd2_ready, 1))
                if t.later:
                    act.wait_ge(xq2T_ps, at(t, xq2T_ps, 0))
                S.activation(xq2[:], rnd2[:], ACT.Copy, bias=-MAGIC).then_inc(xq2_ready, 1)

            def copy_xqT(t):
                act.wait_ge(xqT_ps, at(t, xqT_ps, 1))
                if t.later:
                    act.wait_ge(v_ps, at(t, v_ps, 0))
                S.copy(xqT[:], TR[:, 0:P].bitcast(BF16).rearrange("p (k t) -> p k t", k=KC)).then_inc(xqT_ready, 1)

            def qk_high(t):
                act.wait_ge(rope_sum, at(t, rope_sum, 1))
                if t.later:
                    act.wait_ge(ks_ps, at(t, ks_ps, 0))
                S.copy(qk_parts[:, 0:SP_, LEFT_HI], twice(rope[:, 0:HID], SP_)).then_inc(qk_hi, 1)
                S.copy(qk_parts[:, SP_:2 * SP_, RIGHT_HI], twice(rope[:, HID:2 * HID], SP_)).then_inc(qk_hi, 1)

            def v_heads(t):
                act.wait_ge(v_ps, at(t, v_ps, 1))
                S.copy(gvd[:], PA[1][:, 0:2]).then_inc(gvd_ready, 1)
                act.wait_ge(gvd_ready, at(t, gvd_ready, 1))
                if t.later:
                    act.wait_ge(oA_ps, at(t, oA_ps, 0))
                for h in range(2):
                    half = slice(h * SEQ, (h + 1) * SEQ)
                    for b in range(2):
                        last = S.activation(vA[half, b, :, h, 0:SD], heads(PA[0][half, b * P:(b + 1) * P], SD),
                                            ACT.Copy, scale=gvd[half, b:b + 1])
                last.then_inc(v_ready, 1)

            def copy_stacks_a(t):
                act.wait_ge(qs_ps, at(t, qs_ps, 1))
                if t.later:
                    act.wait_ge(eA_ps, at(t, eA_ps, 0))
                S.copy(qs[:], heads(PA[0][:].bitcast(F16), P)).then_inc(qs_ready, 1)

            def copy_maxima_a(t):
                act.wait_ge(mTA_ps, at(t, mTA_ps, 1))
                if t.later:
                    act.wait_ge(eA_ps, at(t, eA_ps, 0))
                S.copy(mTA[:], PA[0][:, 0:P // 2].bitcast(BF16)).then_inc(mTA_ready, 1)

            def exp_a(t):
                if t.later:
                    act.wait_ge(oA_ps, at(t, oA_ps, 0))
                for k in range(2):
                    act.wait_ge(eA_ps, at(t, eA_ps, k + 1))
                    S.activation(probsA[:, 4 * k:4 * k + 4].rearrange("p h t -> p (h t)"), PA[k][:], ACT.Exp,
                                 scale=ga[:, 5:6]).then_inc(probsA_ready, 1)

            def copy_xq2T(t):
                act.wait_ge(xq2T_ps, at(t, xq2T_ps, 1))
                if t.later:
                    act.wait_ge(wo_ps, at(t, wo_ps, 0))
                S.copy(xq2T[:], TR[:, 0:P].bitcast(BF16).rearrange("p (k t) -> p k t", k=KC)).then_inc(xq2T_ready, 1)

            def norm_a(t):
                act.wait_ge(rstdA_ready, at(t, rstdA_ready, 1))
                if t.later:
                    act.wait_ge(x1_lo, at(t, x1_lo, 0))
                    act.wait_ge(resB_ready, at(t, resB_ready, 0))
                    act.wait_ge(xs_ps, at(t, xs_ps, 0))
                normalise(x1[:], resA[:], stA).then_inc(x1_ready, 1)
                normalise(x_parts[:, :, LEFT_HI], twice(resA[:], 8), stA).then_inc(x1_hi, 1)

            def copy_stacks_b(t):
                act.wait_ge(xs_ps, at(t, xs_ps, 1))
                if t.later:
                    act.wait_ge(eB_ps, at(t, eB_ps, 0))
                S.copy(xs[:], heads(PB[0][:].bitcast(F16), P)).then_inc(xs_ready, 1)

            def copy_maxima_b(t):
                act.wait_ge(mTB_ps, at(t, mTB_ps, 1))
                if t.later:
                    act.wait_ge(eB_ps, at(t, eB_ps, 0))
                S.copy(mTB[:], PB[0][:, 0:P // 2].bitcast(BF16)).then_inc(mTB_ready, 1)

            def exp_b(t, banks):
                if t.later and 0 in banks:
                    act.wait_ge(oB_ps, at(t, oB_ps, 0))
                for k in banks:
                    act.wait_ge(eB_ps, at(t, eB_ps, k + 1))
                    S.activation(probsB[:, 4 * k:4 * k + 4].rearrange("p h t -> p (h t)"), PB[k % 2][:], ACT.Exp,
                                 scale=gb[:, 3:4]).then_inc(probsB_ready, 1)

            def x_high(t):
                act.wait_ge(xT_ps, at(t, xT_ps, 1))
                if t.later:
                    act.wait_ge(up_ps, at(t, up_ps, 0))
                S.copy(xTh[:], TR[:, 0:HID].rearrange("p (k t) -> p k t", k=KC)).then_inc(xTh_ready, 1)

            def norm_b(t):
                act.wait_ge(rstdB_ready, at(t, rstdB_ready, 1))
                if t.later:
                    act.wait_ge(xT_ps, at(t, xT_ps, 0))
                    act.wait_ge(resC_ready, at(t, resC_ready, 0))
                normalise(x2[:], resB[:], stB).then_inc(x2_ready, 1)

            def norm_c(t):
                act.wait_ge(rstdC_ready, at(t, rstdC_ready, 1))
                if t.later:
                    act.wait_ge(y_out, at(t, y_out, 0))
                normalise(y[:], resC[:], stC).then_inc(y_ready, 1)

            def gate_tanh(t):
                act.wait_ge(up_ps, at(t, up_ps, 1))
                if t.later:
                    act.wait_ge(s_ready, at(t, s_ready, 0))
                S.activation(tanh_g[:], UP[0][:, 2 * P:2 * P + NE], ACT.Tanh, scale=0.5).then_inc(gate_th, 1)

            def tanh_up(t, n):
                w, k = width(n), n % 2
                act.wait_ge(up_ps, at(t, up_ps, n + 1))
                if n == 1:
                    act.wait_ge(sh_ready, at(t, sh_ready, 1))
                if t.later or n >= 2:
                    act.wait_ge(u_ready, at(t, u_ready, max(n - 1, 0)))
                for e in range(w // P):
                    ex = 2 * (n - 1) + e
                    last = S.activation(th[:, k, e * P:(e + 1) * P], UP[k][:, e * P:(e + 1) * P], ACT.Tanh,
                                        scale=gate_s[:, 1, ex:ex + 1] if n else 0.5)
                last.then_inc(th_ready, 1)

            def h_high(t, n):
                w, k = width(n), n % 2
                act.wait_ge(hT_ps, at(t, hT_ps, n + 1))
                if t.later or n >= 2:
                    act.wait_ge(down_ps, at(t, down_ps, max(n - 1, 0)))
                S.copy(hTh[:, k, 0:w], TR[:, 0:w]).then_inc(hTh_ready, 1)

            def turn(t0, t1, t2, t3, t4, t5, t6):
                if t5:
                    h_high(t5, 3)
                if t1:
                    round_x(t1)
                if t6:
                    norm_c(t6)
                if t3:
                    copy_xq2T(t3)
                if t5:
                    h_high(t5, 4)
                if t2:
                    v_heads(t2)
                if t4:
                    norm_b(t4)
                if t2:
                    copy_stacks_a(t2)
                if t4:
                    x_high(t4)
                if t3:
                    norm_a(t3)
                if t4:
                    gate_tanh(t4)
                    tanh_up(t4, 0)
                if t2:
                    copy_maxima_a(t2)
                if t3:
                    copy_stacks_b(t3)
                if t4:
                    h_high(t4, 0)
                    tanh_up(t4, 1)
                if t2:
                    exp_a(t2)
                if t4:
                    tanh_up(t4, 2)
                    h_high(t4, 1)
                if t3:
                    copy_maxima_b(t3)
                if t4:
                    tanh_up(t4, 3)
                if t1:
                    copy_xqT(t1)
                if t3:
                    exp_b(t3, (0, 1))
                if t4:
                    h_high(t4, 2)
                if t3:
                    exp_b(t3, (2, 3))
                if t1:
                    qk_high(t1)
                if t2:
                    round_att(t2)
                if t4:
                    tanh_up(t4, 4)

            run(act, turn, {1: high_parts})

        @block.gpsimd
        def _(pool):
            G = nc.gpsimd
            pool.wait_ge(wabs_ready, 4)
            G.partition_all_reduce(wsum[:], wabs[:], P, RADD).then_inc(wsum_ready, 1)
            pool.wait_ge(wsum_ready, 1)
            pool.wait_ge(set_up, 2)

            def low_parts_w2(experts):
                pool.wait_ge(ffn_hi, KC + 1)
                G.tensor_tensor(w2l[:, experts], w2f[:, experts], w2h[:, experts].bitcast(F32), ALU.subtract).then_inc(w2_lo, 1)

            def rstd(t, var_ready, st, eps_added, powered, rstd_ready):
                pool.wait_ge(var_ready, at(t, var_ready, 1))
                settle(pool)
                G.tensor_scalar(st[:, 9:10], st[:, 6:7], -1.0, None, ALU.mult)
                G.tensor_scalar(st[:, 7:8], st[:, 7:8], EPS, None, ALU.add).then_inc(eps_added, 1)
                pool.wait_ge(eps_added, at(t, eps_added, 1))
                G.tensor_tensor(st[:, 8:9], st[:, 7:8], neghalf[:], ALU.pow).then_inc(powered, 1)
                pool.wait_ge(powered, at(t, powered, 1))
                G.tensor_tensor(st[:, 10:11], st[:, 9:10], st[:, 8:9], ALU.mult).then_inc(rstd_ready, 1)

            def largest_g(t):
                pool.wait_ge(g_ready, at(t, g_ready, 1))
                if t.later:
                    pool.wait_ge(scales, at(t, scales, 0))
                settle(pool)
                G.partition_all_reduce(gall[:], ga[:, 1:2], P, RMAX).then_inc(gall_ready, 1)
                pool.wait_ge(gall_ready, at(t, gall_ready, 1))

            def token_scales(t):
                pool.wait_ge(gall_ready, at(t, gall_ready, 1))
                if t.later:
                    pool.wait_ge(probsA_ready, at(t, probsA_ready, 0))
                    pool.wait_ge(rope_ready, at(t, rope_ready, 0))
                    pool.wait_ge(v_ps, at(t, v_ps, 0))
                settle(pool)
                G.tensor_scalar(ga[:, 5:6], gall[:], gall[:, 0:1], score_c[:, 0:1], ALU.mult, ALU.mult)
                G.tensor_scalar(gv[:], cst[:, C_HALF:C_HALF + 2], ga[:, 1:2], v_c[:, 0:1], ALU.mult, ALU.mult)
                G.tensor_tensor(ga[:, 3:4], gall[:], negone[:], ALU.pow).then_inc(ginv, 1)
                pool.wait_ge(ginv, at(t, ginv, 1))
                G.tensor_tensor(ga[:, 4:5], ga[:, 1:2], ga[:, 3:4], ALU.mult).then_inc(scales, 1)

            def add_rope(t):
                pool.wait_ge(rope_ready, at(t, rope_ready, 2))
                if t.later:
                    pool.wait_ge(qk_hi, at(t, qk_hi, 0))
                G.tensor_tensor(rope[:], rope_c[:], rope_s[:], ALU.add).then_inc(rope_sum, 1)

            def q_low(t):
                pool.wait_ge(qk_hi, at(t, qk_hi, 1))
                G.tensor_tensor(qk_parts[:, 0:SP_, LEFT_LO], twice(rope[:, 0:HID], SP_), qk_parts[:, 0:SP_, LEFT_HI],
                                ALU.subtract).then_inc(q_lo, 1)

            def k_low(t):
                pool.wait_ge(qk_hi, at(t, qk_hi, 2))
                G.tensor_tensor(qk_parts[:, SP_:2 * SP_, RIGHT_LO], twice(rope[:, HID:2 * HID], SP_),
                                qk_parts[:, SP_:2 * SP_, RIGHT_HI], ALU.subtract).then_inc(k_lo, 1)

            def largest_c(t):
                pool.wait_ge(cmax_ready, at(t, cmax_ready, 1))
                if t.later:
                    pool.wait_ge(c_ready, at(t, c_ready, 0))
                settle(pool)
                G.partition_all_reduce(call[:], gb[:, 0:1], P, RMAX).then_inc(call_ready, 1)
                pool.wait_ge(call_ready, at(t, call_ready, 1))

            def context_parts(t):
                pool.wait_ge(call_ready, at(t, call_ready, 1))
                if t.later:
                    pool.wait_ge(probsB_ready, at(t, probsB_ready, 0))
                    pool.wait_ge(cs_ps, at(t, cs_ps, 0))
                settle(pool)
                G.tensor_scalar(gb[:, 1:2], call[:], TINY, None, ALU.add).then_inc(cscale, 1)
                G.tensor_scalar(gb[:, 3:4], call[:], XD ** -0.5, None, ALU.mult)
                pool.wait_ge(cscale, at(t, cscale, 1))
                G.tensor_tensor(gb[:, 2:3], gb[:, 1:2], negone[:], ALU.pow).then_inc(cscale, 1)
                pool.wait_ge(cscale, at(t, cscale, 2))
                G.tensor_tensor(cnorm[:], ctxt[:], gb[:, 2:3].broadcast_to([P, SEQ]), ALU.mult).then_inc(cscale, 1)
                parts = c_parts[:].rearrange("p (g w) -> p g w", w=P + XD)[:, :, 0:P].rearrange(
                    "p g (a d) -> p g a d", a=4)[:, :, :, 0:XD]
                source = cnorm[:].rearrange("p (g o d) -> p g o d", o=1, d=XD).broadcast_to([P, 8, 2, XD])
                pool.wait_ge(cscale, at(t, cscale, 3))
                settle(pool)
                G.tensor_copy(parts[:, :, RIGHT_HI], source).then_inc(c_high, 1)
                pool.wait_ge(c_high, at(t, c_high, 1))
                G.tensor_tensor(parts[:, :, RIGHT_LO], source, parts[:, :, RIGHT_HI], ALU.subtract).then_inc(c_ready, 1)

            def context_v(t):
                pool.wait_ge(ctxd_ld, at(t, ctxd_ld, 32))
                pool.wait_ge(x1_lo, at(t, x1_lo, 1))
                if t.later:
                    pool.wait_ge(oB_ps, at(t, oB_ps, 0))
                settle(pool)
                for h in range(2):
                    for b in range(2):
                        last = G.tensor_copy(vB[h * SEQ:(h + 1) * SEQ, b, :, h, 0:XD],
                                             ctxd[h * SEQ:(h + 1) * SEQ, b].rearrange(
                                                 "p (q two d) -> p q two d", two=2, d=XD)[:, :, h])
                last.then_inc(vB_ready, 1)
                pool.wait_ge(vB_ready, at(t, vB_ready, 1))

            def x1_low(t):
                pool.wait_ge(x1_hi, at(t, x1_hi, 1))
                G.tensor_tensor(x_parts[:, :, LEFT_LO], twice(x1[:], 8), x_parts[:, :, LEFT_HI],
                                ALU.subtract).then_inc(x1_lo, 1)

            def residual_b(t):
                pool.wait_ge(attB_ready, at(t, attB_ready, 1))
                if t.later:
                    pool.wait_ge(x2_ready, at(t, x2_ready, 0))
                G.tensor_tensor(resB[:], attB[:], x1[:], ALU.add).then_inc(resB_ready, 1)

            def turn(t0, t1, t2, t3, t4, t5, t6):
                if t2:
                    token_scales(t2)
                    add_rope(t2)
                if t3:
                    context_parts(t3)
                if t2:
                    q_low(t2)
                if t4:
                    residual_b(t4)
                if t2:
                    k_low(t2)
                if t4:
                    rstd(t4, varB_ready, stB, epsB, powB, rstdB_ready)
                if t3:
                    rstd(t3, varA_ready, stA, epsA, powA, rstdA_ready)
                    x1_low(t3)
                    context_v(t3)
                if t5:
                    rstd(t5, varC_ready, stC, epsC, powC, rstdC_ready)
                if t2:
                    largest_c(t2)
                if t1:
                    largest_g(t1)

            run(pool, turn, {2: lambda: low_parts_w2(slice(0, NE // 2)), 3: lambda: low_parts_w2(slice(NE // 2, NE + 1))})

        @block.tensor
        def _(pe):
            T = nc.tensor
            pe.wait_ge(cst16, 1)
            pe.wait_ge(set_up, 2)
            pe.wait_ge(watt_ready, 1)

            def reader(*readers):
                return next((r for r in readers if r[1]), None)

            def transpose_xq(t, last_reader):
                pe.wait_ge(xq_ready, at(t, xq_ready, 1))
                if last_reader:
                    handle, tile, n = last_reader
                    pe.wait_ge(handle, at(tile, handle, n))
                for k in range(KC):
                    last = T.transpose(TR[:, 0:P].bitcast(BF16)[:, k * P:(k + 1) * P], xq[:, k * P:(k + 1) * P], identb[:])
                last.then_inc(xqT_ps, 1)

            def project_qk(t):
                pe.wait_ge(xqT_ready, at(t, xqT_ready, 1))
                if t.later:
                    pe.wait_ge(att_ready, at(t, att_ready, 0))
                for n, w in enumerate((wqk, wqk_rot)):
                    for k in range(KC):
                        last = T.matmul(PA[n][:], xqT[:, k], w[:, k], start=(k == 0), stop=(k == KC - 1))
                    last.then_inc(qk_ps, 1)

            def project_v(t):
                pe.wait_ge(rope_ready, at(t, rope_ready, 2))
                for b in range(2):
                    for h in range(2):
                        for k in range(KC):
                            T.matmul(PA[0][h * SEQ:(h + 1) * SEQ, b * P:(b + 1) * P], xqT[:, k, b * SEQ:(b + 1) * SEQ],
                                     wv_t[:, k].rearrange("p (h two d) -> p h two d", two=2, d=SD)[:, :, h],
                                     start=(k == 0), stop=(k == KC - 1))
                pe.wait_ge(scales, at(t, scales, 1))
                T.matmul(PA[1][:, 0:2], dup, gv[:], start=True, stop=True).then_inc(v_ps, 1)

            def stack_a(t):
                pe.wait_ge(q_lo, at(t, q_lo, 1))
                pe.wait_ge(k_lo, at(t, k_lo, 1))
                pe.wait_ge(v_ready, at(t, v_ready, 1))
                for pair in range(SP_):
                    last = T.transpose(PA[1][:].bitcast(F16)[:, pair * P:(pair + 1) * P],
                                       qk_parts[:, SP_ + pair].rearrange("p a d -> p (a d)"), ident16[:])
                last.then_inc(ks_ps, 1)
                for pair in range(SP_):
                    last = T.transpose(PA[0][:].bitcast(F16)[:, pair * P:(pair + 1) * P],
                                       qk_parts[:, pair].rearrange("p a d -> p (a d)"), ident16[:])
                last.then_inc(qs_ps, 1)

            def scores_a(t):
                pe.wait_ge(qs_ready, at(t, qs_ready, 1))
                pe.wait_ge(ks_ready, at(t, ks_ready, 1))
                for pair in range(SP_):
                    for b in range(2):
                        first = pair % 4 * P
                        last = T.matmul(PA[pair // 4][b * SEQ:(b + 1) * SEQ, first:first + P],
                                        qs[:, pair, b * SEQ:(b + 1) * SEQ], ks[:, pair, b].rearrange("p h t -> p (h t)"),
                                        start=True, stop=True)
                    if pair % 4 == 3:
                        last.then_inc(sA_ps, 1)

            def transpose_maxima_a(t):
                pe.wait_ge(mpA_ready, at(t, mpA_ready, 1))
                T.transpose(PA[0][:, 0:P // 2].bitcast(BF16), mpA[:], identb[:]).then_inc(mTA_ps, 1)

            def exponents_a(t):
                pe.wait_ge(mTA_ready, at(t, mTA_ready, 1))
                for pair in range(SP_):
                    first = pair % 4 * P
                    T.matmul(PA[pair // 4][:, first:first + P], selA[:, pair * P:(pair + 1) * P], mTA[:],
                             start=True, stop=False)
                    for b in range(2):
                        last = T.matmul(PA[pair // 4][:, first + b * SEQ:first + (b + 1) * SEQ],
                                        ks[:, pair, b].rearrange("p h t -> p (h t)"), qs[:, pair, b * SEQ:(b + 1) * SEQ],
                                        start=False, stop=(b == 1))
                    if pair % 4 == 3:
                        last.then_inc(eA_ps, 1)

            def attend_a(t):
                pe.wait_ge(probsA_ready, at(t, probsA_ready, 2))
                for pair in range(SP_):
                    first = pair * 2 * (SD + 1)
                    for b in range(2):
                        last = T.matmul(PA[0][b * SEQ:(b + 1) * SEQ, first:first + 2 * (SD + 1)],
                                        probsA[:, pair, b * SEQ:(b + 1) * SEQ],
                                        vA[:, b, pair].rearrange("p h d -> p (h d)"), start=True, stop=True)
                last.then_inc(oA_ps, 1)

            def transpose_xq2(t, last_reader):
                pe.wait_ge(xq2_ready, at(t, xq2_ready, 1))
                if last_reader:
                    handle, tile, n = last_reader
                    pe.wait_ge(handle, at(tile, handle, n))
                for k in range(KC):
                    last = T.transpose(TR[:, 0:P].bitcast(BF16)[:, k * P:(k + 1) * P], xq2[:, k * P:(k + 1) * P], identb[:])
                last.then_inc(xq2T_ps, 1)

            def project_out(t, last_reader):
                pe.wait_ge(xq2T_ready, at(t, xq2T_ready, 1))
                if last_reader:
                    handle, tile, n = last_reader
                    pe.wait_ge(handle, at(tile, handle, n))
                for k in range(KC):
                    last = T.matmul(TR[:, 0:HID], xq2T[:, k], wo_t[:, k], start=(k == 0), stop=(k == KC - 1))
                last.then_inc(wo_ps, 1)

            def stack_context(t):
                pe.wait_ge(c_ready, at(t, c_ready, 1))
                if t.later:
                    pe.wait_ge(probsB_ready, at(t, probsB_ready, 0))
                dst = PB[1][:].bitcast(F16).rearrange("p (c b h t) -> p c b h t", c=2, b=2, h=4)
                for c in range(2):
                    for h in range(4):
                        first = 4 * c * (P + XD) + h * P
                        last = T.transpose(dst[:, c, :, h], c_parts[:, first:first + P], ident16[:])
                last.then_inc(cs_ps, 1)

            def stack_x1(t):
                pe.wait_ge(x1_lo, at(t, x1_lo, 1))
                if t.later:
                    pe.wait_ge(attB_ready, at(t, attB_ready, 0))
                for cg in range(8):
                    last = T.transpose(PB[0][:].bitcast(F16)[:, cg * P:(cg + 1) * P],
                                       x_parts[:, cg].rearrange("p a d -> p (a d)"), ident16[:])
                last.then_inc(xs_ps, 1)

            def scores_b(t, banks):
                if 0 in banks:
                    pe.wait_ge(xs_ready, at(t, xs_ready, 1))
                    pe.wait_ge(cs_ready, at(t, cs_ready, 1))
                for n in banks:
                    if n >= 2:
                        pe.wait_ge(mB_done, at(t, mB_done, n - 1))
                    for cg in (2 * n, 2 * n + 1):
                        first = cg % 2 * 4 * SEQ
                        for b in range(2):
                            last = T.matmul(PB[n % 2][b * SEQ:(b + 1) * SEQ, first:first + 4 * SEQ],
                                            xs[:, cg, b * SEQ:(b + 1) * SEQ], cs[:, cg // 4, b].rearrange("p h t -> p (h t)"),
                                            start=True, stop=True)
                    last.then_inc(sB_ps, 1)

            def transpose_maxima_b(t):
                pe.wait_ge(mpB_ready, at(t, mpB_ready, 1))
                T.transpose(PB[0][:, 0:P // 2].bitcast(BF16), mpB[:], identb[:]).then_inc(mTB_ps, 1)

            def exponents_b(t, banks):
                if 0 in banks:
                    pe.wait_ge(mTB_ready, at(t, mTB_ready, 1))
                for n in banks:
                    if n >= 2:
                        pe.wait_ge(probsB_ready, at(t, probsB_ready, n - 1))
                    for hp in range(4 * n, 4 * n + 4):
                        c, cg, half = hp // 8, hp // 2, hp % 2
                        first = hp % 4 * P
                        T.matmul(PB[n % 2][:, first:first + P], selB[:, hp * P:(hp + 1) * P], mTB[:], start=True, stop=False)
                        for b in range(2):
                            last = T.matmul(PB[n % 2][:, first + b * SEQ:first + (b + 1) * SEQ],
                                            cs[:, c, b, 2 * half:2 * half + 2].rearrange("p h t -> p (h t)"),
                                            xs[:, cg, b * SEQ:(b + 1) * SEQ], start=False, stop=(b == 1))
                    last.then_inc(eB_ps, 1)

            def attend_b(t):
                pe.wait_ge(probsB_ready, at(t, probsB_ready, 4))
                pe.wait_ge(vB_ready, at(t, vB_ready, 1))
                for hp in range(XP):
                    first = hp * 2 * (XD + 1)
                    for b in range(2):
                        last = T.matmul(PB[0][b * SEQ:(b + 1) * SEQ, first:first + 2 * (XD + 1)],
                                        probsB[:, hp, b * SEQ:(b + 1) * SEQ],
                                        vB[:, b, hp // 8 * 2 + hp % 2].rearrange("p h d -> p (h d)"),
                                        start=True, stop=True)
                last.then_inc(oB_ps, 1)

            parts = [(a, w, k) for a, w in ((xTh, 0), (xTl, 0), (xTh, 1)) for k in range(KC)]

            def transpose_x2(t, last_reader):
                pe.wait_ge(x2_ready, at(t, x2_ready, 1))
                if last_reader:
                    handle, tile, n = last_reader
                    pe.wait_ge(handle, at(tile, handle, n))
                for k in range(KC):
                    last = T.transpose(TR[:, k * P:(k + 1) * P], x2[:, k * P:(k + 1) * P], ident)
                last.then_inc(xT_ps, 1)

            def up(t, m):
                first, w_ = (4 * (m - 1) * P, 4 * P) if m else (2 * NE * P, 2 * P + NE)
                if m == 0:
                    pe.wait_ge(ffn_lo, KC)
                    pe.wait_ge(xTl_ready, at(t, xTl_ready, 1))
                if t.later or m >= 2:
                    pe.wait_ge(h_ready, at(t, h_ready, max(m - 1, 0)))
                for n, (a, w, k) in enumerate(parts):
                    last = T.matmul(UP[m % 2][:, 0:w_], a[:, k], (w13h, w13l)[w][:, k, first:first + w_],
                                    start=(n == 0), stop=(n == 5))
                last.then_inc(up_ps, 1)

            def transpose_h(t, m, last_reader):
                pe.wait_ge(h_ready, at(t, h_ready, m + 1))
                if last_reader:
                    handle, tile, n = last_reader
                    pe.wait_ge(handle, at(tile, handle, n))
                for e in range(width(m) // P):
                    last = T.transpose(TR[:, e * P:(e + 1) * P], hh[:, m % 2, e * P:(e + 1) * P], ident)
                last.then_inc(hT_ps, 1)

            def down(t, m):
                pe.wait_ge(hTl_ready, at(t, hTl_ready, m + 1))
                if m == 0:
                    pe.wait_ge(w2_lo, 2)
                if m == 0 and t.later:
                    pe.wait_ge(resC_ready, at(t, resC_ready, 0))
                for e in range(width(m) // P):
                    ex = 2 * (m - 1) + e if m else NE
                    for n, (a, w) in enumerate(((hTh, w2h), (hTl, w2h), (hTh, w2l))):
                        last = T.matmul(ACC[:, 0:HID], a[:, m % 2, e * P:(e + 1) * P], w[:, ex],
                                        start=(m == 0 and n == 0), stop=(m == NB - 1 and e == 1 and n == 2))
                last.then_inc(down_ps, 1)

            def turn(t0, t1, t2, t3, t4, t5, t6):
                if t5:
                    transpose_h(t5, 3, reader((hTl_ready, t5, 3)))
                if t4:
                    attend_b(t4)
                if t3:
                    transpose_xq2(t3, reader((hTl_ready, t5, 4), (xqT_ready, t2, 1), (resA_ready, t4, 1),
                                             (hTl_ready, t6, 5)))
                if t5:
                    down(t5, 2)
                    transpose_h(t5, 4, reader((xq2T_ready, t3, 1), (hTl_ready, t5, 4)))
                if t2:
                    project_v(t2)
                if t5:
                    down(t5, 3)
                if t3:
                    project_out(t3, reader((hTl_ready, t5, 5), (xq2T_ready, t3, 1)))
                if t5:
                    down(t5, 4)
                if t2:
                    stack_a(t2)
                if t4:
                    transpose_x2(t4, reader((resA_ready, t3, 1), (hTl_ready, t5, 5), (xqT_ready, t2, 1)))
                if t3:
                    stack_context(t3)
                if t2:
                    scores_a(t2)
                if t4:
                    up(t4, 0)
                    up(t4, 1)
                if t2:
                    transpose_maxima_a(t2)
                if t3:
                    stack_x1(t3)
                if t4:
                    transpose_h(t4, 0, reader((xTl_ready, t4, 1)))
                if t2:
                    exponents_a(t2)
                if t3:
                    scores_b(t3, (0, 1))
                if t4:
                    up(t4, 2)
                if t3:
                    scores_b(t3, (2, 3))
                if t2:
                    attend_a(t2)
                if t4:
                    transpose_h(t4, 1, reader((hTl_ready, t4, 1)))
                    up(t4, 3)
                if t3:
                    transpose_maxima_b(t3)
                if t1:
                    transpose_xq(t1, reader((hTl_ready, t4, 2), (resA_ready, t3, 1), (hTl_ready, t5, 5),
                                            (xqT_ready, t2, 1)))
                if t4:
                    down(t4, 0)
                if t3:
                    exponents_b(t3, (0, 1))
                if t1:
                    project_qk(t1)
                if t4:
                    down(t4, 1)
                    transpose_h(t4, 2, reader((xqT_ready, t1, 1), (hTl_ready, t4, 2)))
                if t3:
                    exponents_b(t3, (2, 3))
                if t4:
                    up(t4, 4)

            def weights_v_o():
                pe.wait_ge(watt_ready, 2)

            run(pe, turn, {0: weights_v_o})


def kernel(x, ctx_512, L0_attn_w_q, L0_attn_w_k, L0_attn_w_v, L0_attn_w_o, L0_ffn_gate_w, L0_ffn_w1, L0_ffn_w2,
           L0_ffn_w3, L0_ffn_ws1, L0_ffn_ws2, L0_ffn_ws3):
    import concourse.bacc as bacc
    from concourse.bass_utils import run_bass_kernel_spmd

    def chunks(w):
        w = np.asarray(w)
        return w.T.reshape(KC, P, w.shape[0]).transpose(1, 0, 2)

    def experts(w):
        w = np.asarray(w)
        return w.transpose(2, 0, 1).reshape(KC, P, -1)

    order = np.arange(HID).reshape(2, 4, 4, XD).transpose(0, 2, 1, 3).reshape(-1)
    arrays = {
        "x": np.asarray(x).reshape(-1, P, HID),
        "x_perm": np.asarray(x).reshape(-1, P, HID)[:, :, order],
        "ctx": np.asarray(ctx_512).reshape(-1, P, SEQ),
        "wq": chunks(L0_attn_w_q), "wk": chunks(L0_attn_w_k), "wv": chunks(L0_attn_w_v), "wo": chunks(np.asarray(L0_attn_w_o)[order]),
        "gate": chunks(np.asarray(L0_ffn_gate_w)[:, order]),
        "w1": experts(np.asarray(L0_ffn_w1)[:, :, order]),
        "w2": np.asarray(L0_ffn_w2)[:, order].transpose(2, 0, 1),
        "w3": experts(np.asarray(L0_ffn_w3)[:, :, order]),
        "ws1": experts(np.asarray(L0_ffn_ws1)[None][:, :, order]),
        "ws2": np.asarray(L0_ffn_ws2)[order].T,
        "ws3": experts(np.asarray(L0_ffn_ws3)[None][:, :, order]),
        "const": constants(),
    }
    arrays = {k: np.ascontiguousarray(v) for k, v in arrays.items()}
    nc = bacc.Bacc("TRN2", target_bir_lowering=False, num_devices=1)
    args = [nc.dram_tensor(k, v.shape, mybir.dt.from_np(v.dtype), kind="ExternalInput").ap() for k, v in arrays.items()]
    shape = arrays["x"].shape
    out = nc.dram_tensor("out", shape, F32, kind="ExternalOutput").ap()
    decoder_layer(nc, *args, out)
    r = run_bass_kernel_spmd(nc, [arrays], core_ids=[0])
    return r.results[0]["out"][:, :, np.argsort(order)].reshape(x.shape)
```
